# Optimizing a Trainium2 kernel written in Bass

```python
import numpy as np
import jax
import jax.numpy as jnp

def _softmax(x, axis=-1):
    return jax.nn.softmax(x, axis=axis)

def _gelu(x):
    return jax.nn.gelu(x, approximate=True)

def _silu(x):
    return jax.nn.silu(x)

def _sigmoid(x):
    return jax.nn.sigmoid(x)

def _layernorm(x, axis=-1, eps=1e-05):
    m = jnp.mean(x, axis=axis, keepdims=True)
    v = jnp.var(x, axis=axis, keepdims=True)
    return (x - m) / jnp.sqrt(v + eps)

def _scatter_add(tgt, idx, src, axis=0):
    return tgt.at[idx].add(src)

def _segment_sum(src, seg, n):
    return jax.ops.segment_sum(src, seg, n)
kernel_name = 'mk_gnn_resnorm_d4_gnn_r8_968a6b'

def setup_inputs(seed: int=0):
    np.random.seed(seed)
    _w = jnp.asarray

    def _rec_inputs():
        import jax
        import jax.numpy as jnp
        _gk = jax.random.key(seed)
        x = -0.0003713 + 1 * jax.random.normal(jax.random.fold_in(_gk, 1), (6250, 64), jnp.float32)
        src = jax.random.randint(jax.random.fold_in(_gk, 2), (200000,), 0, 6250, jnp.int32)
        dst = jax.random.randint(jax.random.fold_in(_gk, 3), (200000,), 0, 6250, jnp.int32)
        _o = jnp.argsort(dst, stable=True)
        src = src[_o]
        dst = dst[_o]
        edge_attr_16 = 0.000216709 + 1.00012 * jax.random.normal(jax.random.fold_in(_gk, 12), (200000, 16), jnp.float32)
        edge_type_16 = jax.random.randint(jax.random.fold_in(_gk, 14), (200000,), 0, 16, jnp.int32)
        edge_weight = jax.random.uniform(jax.random.fold_in(_gk, 15), (200000,), jnp.float32, 0.0, 0.999999)
        return (x, src, dst, edge_attr_16, edge_type_16, edge_weight)
    x, src, dst, edge_attr_16, edge_type_16, edge_weight = _rec_inputs()

    def _L0_gnn_setup():
        import jax, jax.numpy as jnp
        import numpy as np
        N_NODES = 25000
        N_EDGES = 250000
        NUM_RELS = 16
        F_IN = 64
        F_OUT = 64
        key = jax.random.key(seed)
        k0, k1, k2, k3, k4 = jax.random.split(key, 5)
        feat = jax.random.normal(k0, (N_NODES, F_IN), dtype=jnp.float32)
        W = jax.random.normal(k1, (NUM_RELS, F_OUT, F_IN), dtype=jnp.float32) * 0.05
        src = jax.random.randint(k2, (N_EDGES,), 0, N_NODES, dtype=jnp.int32)
        dst = jax.random.randint(k3, (N_EDGES,), 0, N_NODES, dtype=jnp.int32)
        etype = jax.random.randint(k4, (N_EDGES,), 0, NUM_RELS, dtype=jnp.int32)
        return {'feat': feat, 'W': W, 'src': src, 'dst': dst, 'etype': etype}
    _L0_gnn_all = _L0_gnn_setup()
    _L0_gnn_in = {k: v for k, v in _L0_gnn_all.items() if k in ('W',)}
    del _L0_gnn_all

    def _L1_gnn_setup():
        import jax, jax.numpy as jnp
        import numpy as np
        N_NODES = 12500
        key = jax.random.key(seed)
        k1, k2 = jax.random.split(key)
        node_features = jax.random.normal(k1, (N_NODES, 64), dtype=jnp.float32)
        edge_index = jax.random.randint(k2, (2, 200000), 0, N_NODES, dtype=jnp.int64)
        return {'node_features': node_features, 'edge_index': edge_index}
    _L1_gnn_all = _L1_gnn_setup()
    _L1_gnn_in = {k: v for k, v in _L1_gnn_all.items() if k in ()}
    del _L1_gnn_all

    def _L2_gnn_setup():
        import jax, jax.numpy as jnp
        import numpy as np
        N_NODES = 12500

        def gcn_conv(x, edge_index, W, b, num_nodes):
            src = jnp.concatenate([edge_index[0], jnp.arange(num_nodes, dtype=edge_index.dtype)])
            dst = jnp.concatenate([edge_index[1], jnp.arange(num_nodes, dtype=edge_index.dtype)])
            deg = jax.ops.segment_sum(jnp.ones_like(dst, dtype=x.dtype), dst, num_segments=num_nodes)
            dinv = jnp.where(deg > 0, jax.lax.rsqrt(deg), 0.0)
            norm = dinv[src] * dinv[dst]
            h = x @ W
            msg = h[src] * norm[:, None]
            out = jax.ops.segment_sum(msg, dst, num_segments=num_nodes)
            return out + b
        key = jax.random.key(seed)
        k1, k2, k3, k4, k5, k6 = jax.random.split(key, 6)
        d_in, d_hid, d_out = (64, 64, 64)
        x = jax.random.normal(k1, (N_NODES, d_in), dtype=jnp.float32)
        edge_index = jax.random.randint(k2, (2, 125000), 0, N_NODES, dtype=jnp.int64)
        W1 = jax.random.normal(k3, (d_in, d_hid), dtype=jnp.float32) / np.sqrt(d_in)
        b1 = jnp.zeros((d_hid,), dtype=jnp.float32)
        W2 = jax.random.normal(k4, (d_hid, d_out), dtype=jnp.float32) / np.sqrt(d_hid)
        b2 = jnp.zeros((d_out,), dtype=jnp.float32)
        return {'x': x, 'edge_index': edge_index, 'W1': W1, 'b1': b1, 'W2': W2, 'b2': b2}
    _L2_gnn_all = _L2_gnn_setup()
    _L2_gnn_in = {k: v for k, v in _L2_gnn_all.items() if k in ('W1', 'b1', 'W2', 'b2')}
    del _L2_gnn_all

    def _L3_gnn_setup():
        import jax, jax.numpy as jnp
        import numpy as np
        N = 12500
        E = 200000
        F_IN = 64
        F_HID = 128
        F_EDGE = 16
        CUTOFF = 5.0
        IN_DIM = 2 * F_IN + F_EDGE + 1
        key = jax.random.key(seed)
        ks = jax.random.split(key, 12)

        def lin(k, fan_in, fan_out):
            bound = 1.0 / np.sqrt(fan_in)
            kw, kb = jax.random.split(k)
            W = jax.random.uniform(kw, (fan_in, fan_out), jnp.float32, -bound, bound)
            b = jax.random.uniform(kb, (fan_out,), jnp.float32, -bound, bound)
            return (W, b)
        x = jax.random.normal(ks[0], (N, F_IN), jnp.float32)
        edge_index = jax.random.randint(ks[1], (2, E), 0, N, jnp.int32)
        edge_weight = jax.random.uniform(ks[2], (E,), jnp.float32)
        edge_attr = jax.random.normal(ks[3], (E, F_EDGE), jnp.float32)
        ew1, eb1 = lin(ks[4], IN_DIM, F_HID)
        ew2, eb2 = lin(ks[5], F_HID, F_HID)
        nw1, nb1 = lin(ks[6], F_IN + F_HID, F_HID)
        nw2, nb2 = lin(ks[7], F_HID, F_IN)
        return {'x': x, 'edge_index': edge_index, 'edge_weight': edge_weight, 'edge_attr': edge_attr, 'ew1': ew1, 'eb1': eb1, 'ew2': ew2, 'eb2': eb2, 'nw1': nw1, 'nb1': nb1, 'nw2': nw2, 'nb2': nb2}
    _L3_gnn_all = _L3_gnn_setup()
    _L3_gnn_in = {k: v for k, v in _L3_gnn_all.items() if k in ('ew1', 'eb1', 'ew2', 'eb2', 'nw1', 'nb1', 'nw2', 'nb2')}
    del _L3_gnn_all
    return {'x': x, 'src': src, 'dst': dst, 'edge_attr_16': edge_attr_16, 'edge_type_16': edge_type_16, 'edge_weight': edge_weight, 'L0_gnn_W': _L0_gnn_in['W'], 'L2_gnn_W1': _L2_gnn_in['W1'], 'L2_gnn_b1': _L2_gnn_in['b1'], 'L2_gnn_W2': _L2_gnn_in['W2'], 'L2_gnn_b2': _L2_gnn_in['b2'], 'L3_gnn_ew1': _L3_gnn_in['ew1'], 'L3_gnn_eb1': _L3_gnn_in['eb1'], 'L3_gnn_ew2': _L3_gnn_in['ew2'], 'L3_gnn_eb2': _L3_gnn_in['eb2'], 'L3_gnn_nw1': _L3_gnn_in['nw1'], 'L3_gnn_nb1': _L3_gnn_in['nb1'], 'L3_gnn_nw2': _L3_gnn_in['nw2'], 'L3_gnn_nb2': _L3_gnn_in['nb2']}

def reference(x, src, dst, edge_attr_16, edge_type_16, edge_weight, L0_gnn_W, L2_gnn_W1, L2_gnn_b1, L2_gnn_W2, L2_gnn_b2, L3_gnn_ew1, L3_gnn_eb1, L3_gnn_ew2, L3_gnn_eb2, L3_gnn_nw1, L3_gnn_nb1, L3_gnn_nw2, L3_gnn_nb2):
    import jax
    import jax.numpy as jnp

    def _L0_gnn_ref(feat, W, src, dst, etype):
        import jax, jax.numpy as jnp
        import numpy as np
        N_NODES = 25000
        N_EDGES = 250000
        NUM_RELS = 16
        F_IN = 64
        F_OUT = 64
        n_dst = feat.shape[0]
        xw = jnp.einsum('rof,nf->rno', W, feat)
        msg = xw[etype, src]
        return jax.ops.segment_sum(msg, dst, num_segments=n_dst)

    def _L1_gnn_ref(node_features, edge_index):
        import jax, jax.numpy as jnp
        import numpy as np
        N_NODES = 12500
        src = node_features[edge_index[0]]
        dest = node_features[edge_index[1]]
        messages = src + dest
        num_nodes = node_features.shape[0]
        target = edge_index[1]
        aggregated = jax.ops.segment_sum(messages, target, num_segments=num_nodes)
        ones = jnp.ones((messages.shape[0],), dtype=messages.dtype)
        counts = jax.ops.segment_sum(ones, target, num_segments=num_nodes)
        aggregated = aggregated / jnp.clip(counts, 1.0)[:, None]
        return node_features + aggregated

    def _L2_gnn_ref(x, edge_index, W1, b1, W2, b2):
        import jax, jax.numpy as jnp
        import numpy as np
        N_NODES = 12500

        def gcn_conv(x, edge_index, W, b, num_nodes):
            src = jnp.concatenate([edge_index[0], jnp.arange(num_nodes, dtype=edge_index.dtype)])
            dst = jnp.concatenate([edge_index[1], jnp.arange(num_nodes, dtype=edge_index.dtype)])
            deg = jax.ops.segment_sum(jnp.ones_like(dst, dtype=x.dtype), dst, num_segments=num_nodes)
            dinv = jnp.where(deg > 0, jax.lax.rsqrt(deg), 0.0)
            norm = dinv[src] * dinv[dst]
            h = x @ W
            msg = h[src] * norm[:, None]
            out = jax.ops.segment_sum(msg, dst, num_segments=num_nodes)
            return out + b
        n = x.shape[0]
        h = jax.nn.relu(gcn_conv(x, edge_index, W1, b1, n))
        out = jax.nn.relu(gcn_conv(h, edge_index, W2, b2, n))
        return out

    def _L3_gnn_ref(x, edge_index, edge_weight, edge_attr, ew1, eb1, ew2, eb2, nw1, nb1, nw2, nb2):
        import jax, jax.numpy as jnp
        import numpy as np
        N = 12500
        E = 200000
        F_IN = 64
        F_HID = 128
        F_EDGE = 16
        CUTOFF = 5.0
        IN_DIM = 2 * F_IN + F_EDGE + 1
        row, col = (edge_index[0], edge_index[1])
        d_raw = (edge_weight / CUTOFF)[:, None]
        edge_input = jnp.concatenate([x[row], x[col], edge_attr, d_raw], axis=-1)
        h = jax.nn.silu(edge_input @ ew1 + eb1)
        m_ij = jax.nn.silu(h @ ew2 + eb2)
        agg = jax.ops.segment_sum(m_ij, row, num_segments=x.shape[0])
        node_in = jnp.concatenate([x, agg], axis=-1)
        upd = jax.nn.silu(node_in @ nw1 + nb1) @ nw2 + nb2
        return x + upd
    edge_index = jnp.stack([src, dst])
    x = _layernorm(x + _L0_gnn_ref(x, L0_gnn_W, src, dst, edge_type_16), axis=-1)
    x = _layernorm(x + _L1_gnn_ref(x, edge_index), axis=-1)
    x = _layernorm(x + _L2_gnn_ref(x, edge_index, L2_gnn_W1, L2_gnn_b1, L2_gnn_W2, L2_gnn_b2), axis=-1)
    x = _layernorm(x + _L3_gnn_ref(x, edge_index, edge_weight, edge_attr_16, L3_gnn_ew1, L3_gnn_eb1, L3_gnn_ew2, L3_gnn_eb2, L3_gnn_nw1, L3_gnn_nb1, L3_gnn_nw2, L3_gnn_nb2), axis=-1)
    return x

_drawn_inputs = setup_inputs


def setup_inputs(seed=0):
    import zlib

    import numpy as np

    out = dict(_drawn_inputs(seed))
    spreads = {'L2_gnn_b1': (0.0, 0.1), 'L2_gnn_b2': (0.0, 0.1)}
    factors = {'edge_attr_16': 3.878,
     'edge_weight': 200.0,
     'L2_gnn_W1': 3.303,
     'L3_gnn_eb1': 2.757,
     'L3_gnn_nb1': 7.807}
    for name, (base, spread) in spreads.items():
        noise = np.random.default_rng([zlib.crc32(name.encode()), seed]).standard_normal(out[name].shape)
        drawn = base * np.exp(spread * noise) if base else spread * noise
        out[name] = jnp.asarray(drawn.astype(out[name].dtype))
    for name, factor in factors.items():
        out[name] = (out[name] * factor).astype(out[name].dtype)
    return out
```

```python
from contextlib import ExitStack

import concourse.bass as bass
from concourse import mybir

N, E, F, H, A, RELS = 6250, 200000, 64, 128, 16, 16
P = 128
NT = -(-N // P)
NP = NT * P
CH = 56
NCH = -(-E // (P * CH))
KT = NCH * CH
EP = KT * P
GR = 4
CE = 28
NCE = KT // CE
NG = CE // GR
HB = 8
NH = CH // HB
ND = CH // GR
EPS = 1e-5
CUTOFF = 5.0
assert NCH % 2 == 0 and NCE % 2 == 0 and NG % 2 == 1 and NH % 2 == 1 and ND % 2 == 0
TILE_GROUPS = [list(range(t, min(t + GR, NT))) for t in range(0, NT, GR)]


def gnn_kernel(nc, x, src, dst, etype, src_t, attr_t, rel_w, gcn_w, bias_rows, ew1, we, ew2, hid_b,
               eb2_rows, nw1x, nw1a, nw2, out):
    f32, bf16, i32 = mybir.dt.float32, mybir.dt.bfloat16, mybir.dt.int32
    ALU, ACT, AX = mybir.AluOpType, mybir.ActivationFunctionType, mybir.AxisListType
    ds = bass.ds
    ctx = ExitStack()
    with ctx, nc.allow_non_contiguous_dma(reason="columns of the edge lists"):
        def sb(name, shape, dt=f32):
            return ctx.enter_context(nc.sbuf_tensor(name, shape, dt))

        def sem(name):
            return ctx.enter_context(nc.semaphore(name))

        def rows(col):
            return bass.IndirectOffsetOnAxis(ap=col, axis=0)

        rel_table = nc.dram_tensor("rel_table", [NP * RELS, F], f32).ap()
        node_table = [nc.dram_tensor(f"node_table{i}", [NP, F], f32).ap() for i in range(3)]
        sums = [nc.dram_tensor(f"sums{i}", [P, KT, F], f32).ap() for i in range(4)]
        p_table = nc.dram_tensor("p_table", [NP, H], f32).ap()
        q_table = nc.dram_tensor("q_table", [NP, H], f32).ap()
        q_starts = nc.dram_tensor("q_starts", [EP + P, H], f32).ap()
        agg_table = [nc.dram_tensor(f"agg_table{j}", [NP + P, H], f32).ap() for j in range(GR)]
        src_split = nc.dram_tensor("src_split", [2, EP], bf16).ap()

        src_i = sb("src_i", [P, KT], i32)
        row_idx = sb("row_idx", [P, KT], i32)
        same = sb("same", [P, KT])
        dst_hl = sb("dst_hl", [P, 2, KT], bf16)
        cross = sb("cross", [P, NP])
        xt = sb("xt", [P, NP])
        X = sb("X", [P, NT, F])
        node = sb("node", [P, 3 * NT * F])
        S1, S2, S3 = (node[:, i * NT * F:(i + 1) * NT * F].rearrange("p (t f) -> p t f", f=F) for i in range(3))
        gbuf = [sb(f"gbuf{u}", [P, CH * F]) for u in range(2)]
        rbuf = [sb(f"rbuf{u}", [P, CH * F]) for u in range(2)]
        G, R = ([b[:, :].rearrange("p (k f) -> p k f", f=F) for b in bufs] for bufs in (gbuf, rbuf))
        GE, QE = ([b[:, :].rearrange("p (k h) -> p k h", h=H) for b in bufs] for bufs in (gbuf, rbuf))
        get_rows = sb("get_rows", [P, 2, CH], i32)
        put_rows = sb("put_rows", [P, 2, CE], i32)
        ident = sb("ident", [P, P])
        before = sb("before", [P, P], bf16)
        upto = sb("upto", [P, P])
        ones = sb("ones", [P, P])
        ones_bf = sb("ones_bf", [2, P], bf16)
        count_i = sb("count_i", [P, P], i32)
        count_bf = sb("count_bf", [P, P], bf16)
        zeros = sb("zeros", [P, 512])
        zero_bf = sb("zero_bf", [P, P], bf16)
        dump_i = sb("dump_i", [P, 2], i32)
        dump = sb("dump", [P, 2])
        comes_in = sb("comes_in", [P, 1])
        goes_out = sb("goes_out", [P, 1])
        last_dst = sb("last_dst", [P, 1])
        near_dst = sb("near_dst", [P, 2], i32)
        first_dst = sb("first_dst", [P, 1], i32)
        deg, has, inv, dinv, tmp, tot, mean, var = (sb(n, [P, NT]) for n in ("deg", "has", "inv", "dinv", "tmp", "tot", "mean", "var"))
        end_row = sb("end_row", [P, NT], i32)
        start_row = sb("start_row", [P, NT], i32)
        q_in = sb("q_in", [P, H])
        gcn_s = sb("gcn_s", [F, 2, F])
        bias_s = sb("bias_s", [P, 3, F])
        eb2_s = sb("eb2_s", [P, H])
        ew1_s = sb("ew1_s", [F, 2 * H])
        we_s = sb("we_s", [1 + A, H])
        ew2_s = sb("ew2_s", [H, H])
        hid_s = sb("hid_s", [H, 2])
        nw1x_s = sb("nw1x_s", [F, H])
        nw1a_s = sb("nw1a_s", [H, H])
        nw2_s = sb("nw2_s", [H, F])
        PS = [ctx.enter_context(nc.psum_tensor(f"PS{i}", [P, 512], f32)) for i in range(8)]

        def over_f(col):
            return col[:, :].rearrange("p (t o) -> p t o", o=1).to_broadcast([P, NT, F])

        begun = sem("begun")

        def wait_counts(eng, *waits):
            counts = [n if isinstance(n, int) else eng.to_reg(n) for _, n in waits]
            eng.wait_ge(begun, 1)
            for (signal, _), n in zip(waits, counts):
                eng.wait_ge(signal, n)

        def by_pairs(eng, n, body):
            for u in range(2):
                body(0, u, u, True)
            with eng.Fori(1, n // 2) as i:
                for u in range(2):
                    body(i, u, i * 2 + u, False)

        class Chain:

            def __init__(self, name):
                self.sem, self.n = sem(name), 0

            def link(self, ins):
                self.n += 1
                ins.then_inc(self.sem, 1)
                nc.vector.wait_ge(self.sem, self.n)

        def prepare():
            loaded, weights, preset, near, wide_done, split, made = (
                sem(n) for n in ("loaded", "weights", "preset", "near", "wide_done", "split", "made"))
            ch = Chain("prep_chain")
            dst_i = rbuf[0][:, 0:KT].bitcast(i32)
            typ_i = rbuf[0][:, KT:2 * KT].bitcast(i32)
            part_i = rbuf[1][:, 0:KT].bitcast(i32)
            srt_i = xt[:, 0:KT].bitcast(i32)
            srt_bf = xt[:, KT:2 * KT].bitcast(bf16).rearrange("p (a k) -> p a k", a=2)
            block = nc.Block()
            with block:
                @block.sync
                def _(sp):
                    for a, b in ((dst_i, dst), (src_i[:, :], src), (typ_i, etype), (srt_i, src_t),
                                 (first_dst[:, :], dst[:, 0:1]),
                                 (X[:, :, :], x.rearrange("(t p) f -> p t f", p=P))):
                        sp.dma_start(a, b).then_inc(loaded, 16)
                    sp.wait_ge(preset, 1)
                    sp.dma_start(near_dst[1:P, 0:1], dst[0:P - 1, KT - 1:KT]).then_inc(near, 16)
                    sp.dma_start(near_dst[0:P - 1, 1:2], dst[1:P, 0:1]).then_inc(near, 16)
                    sp.wait_ge(split, 1)
                    sp.dma_start(src_split.rearrange("a (p k) -> p a k", p=P), srt_bf).then_inc(wide_done, 16)
                    sp.wait_ge(wide_done, 16)

                @block.scalar
                def _(act):
                    for a, b in ((cross[0:F, 0:RELS * F], rel_w), (gcn_s[:, :, :], gcn_w), (bias_s[:, :, :], bias_rows),
                                 (eb2_s[:, :], eb2_rows), (ew1_s[:, :], ew1), (we_s[:, :], we), (ew2_s[:, :], ew2),
                                 (hid_s[:, :], hid_b), (nw1x_s[:, :], nw1x), (nw1a_s[:, :], nw1a), (nw2_s[:, :], nw2)):
                        act.dma_start(a, b).then_inc(weights, 16)
                    act.wait_ge(weights, 16 * 11)

                @block.gpsimd
                def _(pool):
                    nc.gpsimd.memset(near_dst[:, :], -1).then_inc(preset, 1)
                    nc.gpsimd.memset(zeros[:, :], 0.0).then_inc(begun, 1)
                    nc.gpsimd.memset(zero_bf[:, :], 0.0)
                    nc.gpsimd.memset(ones[:, :], 1.0).then_inc(made, 1)
                    nc.gpsimd.memset(ones_bf[:, :], 1.0)
                    nc.gpsimd.iota(dump_i[:, 0:1], pattern=[[0, 1]], base=NP, channel_multiplier=1)
                    nc.gpsimd.iota(dump_i[:, 1:2], pattern=[[0, 1]], base=0, channel_multiplier=1)
                    nc.gpsimd.iota(count_i[:, :], pattern=[[1, P]], base=0, channel_multiplier=0).then_inc(made, 1)
                    pool.wait_ge(made, 2)
                    nc.gpsimd.affine_select(out=ident[:, :], in_=ones[:, :], compare_op=ALU.is_equal, fill=0.0,
                                            base=0, pattern=[[-1, P]], channel_multiplier=1)
                    nc.gpsimd.affine_select(out=before[:, :], in_=ones[:, :], compare_op=ALU.is_gt, fill=0.0,
                                            base=0, pattern=[[-1, P]], channel_multiplier=1)
                    nc.gpsimd.affine_select(out=upto[:, :], in_=ones[:, :], compare_op=ALU.is_ge, fill=0.0,
                                            base=0, pattern=[[1, P]], channel_multiplier=-1)

                @block.vector
                def _(dve):
                    dve.wait_ge(loaded, 16 * 6)
                    for a, mask in enumerate((~127, 127)):
                        ch.link(nc.vector.tensor_scalar(part_i, srt_i, mask, None, ALU.bitwise_and))
                        ins = nc.vector.tensor_copy(srt_bf[:, a, :], part_i)
                        ch.link(ins)
                    nc.vector.tensor_scalar(row_idx[:, :], src_i[:, :], float(RELS), None, ALU.mult).then_inc(split, 1)
                    dve.wait_ge(split, 1)
                    nc.vector.tensor_tensor(same[:, 1:KT], dst_i[:, 1:KT], dst_i[:, 0:KT - 1], ALU.is_equal)
                    nc.vector.tensor_tensor(row_idx[:, :], row_idx[:, :], typ_i, ALU.add)
                    nc.vector.memset(same[:, 0:1], 0.0)
                    ch.link(nc.vector.tensor_scalar(part_i, dst_i, 7, None, ALU.logical_shift_right))
                    ch.link(nc.vector.tensor_copy(dst_hl[:, 0, :], part_i))
                    ch.link(nc.vector.tensor_scalar(part_i, dst_i, P - 1, None, ALU.bitwise_and))
                    ch.link(nc.vector.tensor_copy(dst_hl[:, 1, :], part_i))
                    nc.vector.tensor_copy(last_dst[:, :], dst_i[:, KT - 1:KT])
                    dve.wait_ge(made, 2)
                    nc.vector.tensor_copy(count_bf[:, :], count_i[:, :])
                    nc.vector.tensor_copy(dump[:, :], dump_i[:, :])
                    dve.wait_ge(near, 32)
                    nc.vector.tensor_tensor(comes_in[:, :], near_dst[:, 0:1], dst_i[:, 0:1], ALU.is_equal)
                    nc.vector.tensor_tensor(goes_out[:, :], near_dst[:, 1:2], dst_i[:, KT - 1:KT], ALU.is_equal)
                    dve.wait_ge(weights, 16 * 11)
                    nc.vector.tensor_scalar(we_s[0:1, :], we_s[0:1, :], 1.0 / CUTOFF, None, ALU.mult)


        def pe_transpose(pe, rows3, banks, ps_sem, sb_sem):
            for g, tiles in enumerate(TILE_GROUPS):
                if g >= 2:
                    pe.wait_ge(sb_sem, g - 1)
                for j, t in enumerate(tiles):
                    ins = nc.tensor.transpose(banks[g % 2][0:F, j * P:(j + 1) * P], rows3[:, t, :], ident[:, :])
                ins.then_inc(ps_sem, 1)

        def act_untranspose(act, banks, ps_sem, sb_sem):
            for g, tiles in enumerate(TILE_GROUPS):
                act.wait_ge(ps_sem, g + 1)
                n = len(tiles) * P
                nc.scalar.copy(xt[0:F, g * GR * P:g * GR * P + n], banks[g % 2][0:F, 0:n]).then_inc(sb_sem, 1)

        def relation_table():
            tr_ps, tr_sb, mm, half_v, half_s = (sem(n) for n in ("rel_tr_ps", "rel_tr_sb", "rel_mm", "rel_v", "rel_s"))
            put = [sem(f"rel_put{u}") for u in range(2)]
            block = nc.Block()
            with block:
                @block.tensor
                def _(pe):
                    pe_transpose(pe, X, PS[0:2], tr_ps, tr_sb)
                    for t in range(NT):
                        pe.wait_ge(tr_sb, t // GR + 1)
                        if t >= 2:
                            pe.wait_ge(half_v, t - 1)
                            pe.wait_ge(half_s, t - 1)
                        for h in range(2):
                            ins = nc.tensor.matmul(PS[2 + 2 * (t % 2) + h][:, :], xt[0:F, t * P:(t + 1) * P],
                                                   cross[0:F, h * 512:(h + 1) * 512], start=True, stop=True)
                        ins.then_inc(mm, 1)

                @block.scalar
                def _(act):
                    act_untranspose(act, PS[0:2], tr_ps, tr_sb)
                    for t in range(NT):
                        act.wait_ge(mm, t + 1)
                        if t >= 2:
                            act.wait_ge(put[t % 2], 16 * (t // 2))
                        nc.scalar.copy(gbuf[t % 2][:, 512:1024], PS[3 + 2 * (t % 2)][:, :]).then_inc(half_s, 1)

                @block.vector
                def _(dve):
                    for t in range(NT):
                        dve.wait_ge(mm, t + 1)
                        if t >= 2:
                            dve.wait_ge(put[t % 2], 16 * (t // 2))
                        nc.vector.tensor_copy(gbuf[t % 2][:, 0:512], PS[2 + 2 * (t % 2)][:, :]).then_inc(half_v, 1)

                @block.sync
                def _(sp):
                    for t in range(NT):
                        sp.wait_ge(half_v, t + 1)
                        sp.wait_ge(half_s, t + 1)
                        sp.dma_start(rel_table[t * P * RELS:(t + 1) * P * RELS, :].rearrange("(p r) f -> p (r f)", r=RELS),
                                     gbuf[t % 2][:, 0:RELS * F]).then_inc(put[t % 2], 16)
                    for u in range(2):
                        sp.wait_ge(put[u], 16 * ((NT + 1 - u) // 2))

        def gather_pass(l, table, index):
            idx_ready, gathered, scanned, stored = (
                [sem(f"{n}{l}{u}") for u in range(2)] for n in ("idx_ready", "gathered", "scanned", "stored"))
            if l == 0:
                hot_ready, hot_used, zeroed = sem("hot_ready"), sem("hot_used"), sem("zeroed")
            if l == 1:
                hot_in = [sem(f"rows_in{u}") for u in range(2)]
                eq_ps, eq_used, chained = sem("eq_ps"), sem("eq_used"), sem("chained")
            hot = [xt[:, u * 1024:(u + 1) * 1024].bitcast(bf16) for u in range(2)]
            src_rows = [node[0:2, u * CH * P // 2:(u + 1) * CH * P // 2].bitcast(bf16) for u in range(2)]
            equal, earlier = (xt[:, a * 256:(a + 1) * 256].bitcast(bf16).rearrange("p (j e) -> p j e", e=P) for a in range(2))
            n_before, gap = xt[:, 512:512 + CH], xt[:, 576:576 + CH]
            LINKS = 2 * ND + 2
            block = nc.Block()
            with block:
                @block.gpsimd
                def _(pool):
                    def chunk(i, u, c, first):
                        if not first:
                            pool.wait_ge(gathered[u], i * (16 * CH))
                            pool.wait_ge(scanned[u], i)
                        nc.gpsimd.tensor_copy(get_rows[:, u, :], index[:, ds(c * CH, CH)]).then_inc(idx_ready[u], 1)
                        wait_counts(pool, (idx_ready[u], i + 1))
                        for k in range(CH):
                            nc.gpsimd.indirect_dma_start(G[u][:, k, :], None, table, rows(get_rows[:, u, k:k + 1]))\
                                .then_inc(gathered[u], 16)
                    by_pairs(pool, NCH, chunk)

                @block.vector
                def _(dve):
                    def histogram_rows(c, u, first):
                        for s in range(NH):
                            b = (u + s) % 2
                            if not first or u * NH + s >= 2:
                                dve.wait_ge(hot_used, c * NH + (s - 1))
                            at = dst_hl[:, :, ds(c * CH + s * HB, HB)]
                            nc.vector.tensor_tensor(
                                hot[b][:, 0:HB * P].rearrange("p (k e) -> p k e", e=P),
                                at[:, 1, :].rearrange("p (k o) -> p k o", o=1).to_broadcast([P, HB, P]),
                                count_bf[:, :].rearrange("p (o e) -> p o e", o=1).to_broadcast([P, HB, P]), ALU.is_equal)
                            nc.vector.tensor_tensor(
                                hot[b][:, HB * P:HB * (P + NT)].rearrange("p (k e) -> p k e", e=NT),
                                at[:, 0, :].rearrange("p (k o) -> p k o", o=1).to_broadcast([P, HB, NT]),
                                count_bf[:, 0:NT].rearrange("p (o e) -> p o e", o=1).to_broadcast([P, HB, NT]), ALU.is_equal)\
                                .then_inc(hot_ready, 1)

                    def scatter_rows(c, u, first):
                        for g in range(ND):
                            dve.wait_ge(eq_ps, c * ND + (g + 1))
                            nc.vector.tensor_tensor(
                                equal, PS[g % 2][:, :].rearrange("p (j e) -> p j e", e=P),
                                src_i[:, ds(c * CH + g * GR, GR)].rearrange("p (j o) -> p j o", o=1).to_broadcast([P, GR, P]),
                                ALU.is_equal).then_inc(eq_used, 1)
                            dve.wait_ge(eq_used, c * ND + (g + 1))
                            nc.vector.tensor_tensor(
                                earlier, equal, before[:, :].rearrange("p (o e) -> p o e", o=1).to_broadcast([P, GR, P]),
                                ALU.mult).then_inc(chained, 1)
                            dve.wait_ge(chained, c * LINKS + (2 * g + 1))
                            nc.vector.tensor_reduce(n_before[:, g * GR:(g + 1) * GR], earlier, AX.X, ALU.add).then_inc(chained, 1)
                            dve.wait_ge(chained, c * LINKS + (2 * g + 2))
                        at = src_i[:, ds(c * CH, CH)]
                        nc.vector.tensor_scalar(gap, at, -1.0, dump[:, 0:1], ALU.mult, ALU.add).then_inc(chained, 1)
                        dve.wait_ge(chained, c * LINKS + (2 * ND + 1))
                        nc.vector.scalar_tensor_tensor(out=gap, in0=n_before, scalar=0.0, in1=gap, op0=ALU.is_gt,
                                                       op1=ALU.mult).then_inc(chained, 1)
                        dve.wait_ge(chained, c * LINKS + (2 * ND + 2))
                        nc.vector.tensor_tensor(row_idx[:, ds(c * CH, CH)], gap, at, ALU.add)

                    def chunk(i, u, c, first):
                        if l == 0:
                            histogram_rows(c, u, first)
                        if l == 1:
                            scatter_rows(c, u, first)
                        dve.wait_ge(gathered[u], (i + 1) * (16 * CH))
                        if not first:
                            dve.wait_ge(stored[u], i * 16)
                        if u == 1:
                            dve.wait_ge(scanned[0], i + 1)
                        elif not first:
                            dve.wait_ge(scanned[1], i)
                        for f in range(F):
                            start = 0.0 if first and u == 0 else R[1 - u][:, CH - 1, f:f + 1]
                            ins = nc.vector.tensor_tensor_scan(R[u][:, :, f], same[:, ds(c * CH, CH)], G[u][:, :, f],
                                                               start, ALU.mult, ALU.add)
                        ins.then_inc(scanned[u], 1)
                    by_pairs(dve, NCH, chunk)

                @block.sync
                def _(sp):
                    def chunk(i, u, c, first):
                        if l == 1:
                            if not first:
                                wait_counts(sp, (eq_ps, (c - 1) * ND))
                            sp.dma_start(src_rows[u], src_split[:, ds(c * (CH * P), CH * P)]).then_inc(hot_in[u], 16)
                        wait_counts(sp, (scanned[u], i + 1))
                        sp.dma_start(sums[l][:, ds(c * CH, CH), :], R[u]).then_inc(stored[u], 16)
                    by_pairs(sp, NCH, chunk)
                    for u in range(2):
                        sp.wait_ge(stored[u], 16 * (NCH // 2))

                if l == 0:
                    @block.scalar
                    def _(act):
                        wide = zeros[:, :].rearrange("p (o n) -> p o n", o=1)
                        per = EP // P // NCH * H // 512

                        def chunk(i, u, c, first):
                            act.dma_start(
                                q_starts[ds(c * (CH * P), CH * P), :].rearrange("(p a b) h -> p a (b h)", p=P, b=4),
                                wide.to_broadcast([P, per, 512])).then_inc(zeroed, 16)
                            act.wait_ge(gathered[u], (i + 1) * (16 * CH))
                        by_pairs(act, NCH, chunk)
                        act.dma_start(q_starts[EP:EP + P, :], zeros[:, 0:H]).then_inc(zeroed, 16)
                        for j in range(GR):
                            act.dma_start(agg_table[j].rearrange("(p a) h -> p a h", p=P),
                                          zeros[:, 0:H].rearrange("p (o n) -> p o n", o=1).to_broadcast([P, (NP + P) // P, H]))\
                                .then_inc(zeroed, 16)
                        act.wait_ge(zeroed, 16 * (NCH + 1 + GR))

                    @block.tensor
                    def _(pe):
                        nc.tensor.matmul(PS[7][:, 0:NT], zero_bf[:, :], zero_bf[:, 0:NT], start=True, stop=False)

                        def chunk(i, u, c, first):
                            for s in range(NH):
                                b = (u + s) % 2
                                pe.wait_ge(hot_ready, c * NH + (s + 1))
                                for k in range(HB):
                                    ins = nc.tensor.matmul(PS[7][:, 0:NT], hot[b][:, k * P:(k + 1) * P],
                                                           hot[b][:, HB * P + k * NT:HB * P + (k + 1) * NT],
                                                           start=False, stop=False)
                                ins.then_inc(hot_used, 1)
                        by_pairs(pe, NCH, chunk)
                        nc.tensor.matmul(PS[7][:, 0:NT], zero_bf[:, :], zero_bf[:, 0:NT], start=False, stop=True)

                if l == 1:
                    @block.tensor
                    def _(pe):
                        def chunk(i, u, c, first):
                            pe.wait_ge(hot_in[u], (i + 1) * 16)
                            for g in range(ND):
                                if not first or u * ND + g >= 2:
                                    pe.wait_ge(eq_used, c * ND + (g - 1))
                                nc.tensor.matmul(PS[g % 2][:, :], ones_bf[:, :], src_rows[u][:, g * GR * P:(g + 1) * GR * P],
                                                 start=True, stop=True).then_inc(eq_ps, 1)
                        by_pairs(pe, NCH, chunk)

        def degrees():
            ch = Chain("deg_chain")
            deg_sb, prefix, root, rooted, counted = (sem(n) for n in ("deg_sb", "prefix", "root", "rooted", "counted"))
            block = nc.Block()
            with block:
                @block.gpsimd
                def _(pool):
                    nc.gpsimd.iota(cross[:, :], pattern=[[1, NP]], base=0, channel_multiplier=0,
                                   allow_small_or_imprecise_dtypes=True).then_inc(counted, 1)

                @block.tensor
                def _(pe):
                    pe.wait_ge(deg_sb, 1)
                    nc.tensor.matmul(PS[0][:, 0:NT], upto[:, :], deg[:, :], start=True, stop=True)
                    nc.tensor.matmul(PS[1][:, 0:NT], ones[:, :], deg[:, :], start=True, stop=True).then_inc(prefix, 1)

                @block.scalar
                def _(act):
                    act.wait_ge(root, 1)
                    nc.scalar.activation(tmp[:, :], tmp[:, :], ACT.Sqrt).then_inc(rooted, 1)

                @block.vector
                def _(dve):
                    nc.vector.tensor_copy(deg[:, :], PS[7][:, 0:NT]).then_inc(deg_sb, 1)
                    dve.wait_ge(deg_sb, 1)
                    nc.vector.tensor_scalar(has[:, :], deg[:, :], 1.0, None, ALU.min)
                    ch.link(nc.vector.tensor_scalar(inv[:, :], deg[:, :], 1.0, None, ALU.max))
                    ch.link(nc.vector.reciprocal(inv[:, :], inv[:, :]))
                    nc.vector.tensor_scalar(tmp[:, :], deg[:, :], 1.0, None, ALU.add).then_inc(root, 1)
                    dve.wait_ge(rooted, 1)
                    ch.link(nc.vector.reciprocal(dinv[:, :], tmp[:, :]))
                    dve.wait_ge(prefix, 1)
                    ch.link(nc.vector.tensor_copy(tot[:, :], PS[1][:, 0:NT]))
                    ch.link(nc.vector.tensor_tensor_scan(tmp[:, :], ones[:, 0:NT], tot[:, :], 0.0, ALU.mult, ALU.add))
                    ch.link(nc.vector.tensor_tensor(tmp[:, :], tmp[:, :], tot[:, :], ALU.subtract))
                    ch.link(nc.vector.tensor_tensor(tmp[:, :], tmp[:, :], PS[0][:, 0:NT], ALU.add))
                    nc.vector.tensor_scalar(end_row[:, :], tmp[:, :], -1.0, 0.0, ALU.add, ALU.max)
                    ch.link(nc.vector.tensor_tensor(tmp[:, :], tmp[:, :], deg[:, :], ALU.subtract))
                    ch.link(nc.vector.tensor_scalar(tot[:, :], tmp[:, :], -1.0, float(EP), ALU.mult, ALU.add))
                    ch.link(nc.vector.tensor_scalar(tot[:, :], tot[:, :], dump[:, 1:2], None, ALU.add))
                    ch.link(nc.vector.tensor_scalar(mean[:, :], has[:, :], -1.0, 1.0, ALU.mult, ALU.add))
                    ch.link(nc.vector.tensor_tensor(tot[:, :], tot[:, :], mean[:, :], ALU.mult))
                    nc.vector.tensor_tensor(start_row[:, :], tmp[:, :], tot[:, :], ALU.add)
                    dve.wait_ge(counted, 1)
                    nc.vector.tensor_scalar(cross[:, :], cross[:, :], last_dst[:, 0:1], goes_out[:, 0:1],
                                            ALU.is_equal, ALU.mult)

        def layer_norm(dve, ch, Y, scratch, var_made, root_made, n):
            ch.link(nc.vector.tensor_reduce(mean[:, :], Y, AX.X, ALU.add))
            ch.link(nc.vector.tensor_scalar(mean[:, :], mean[:, :], 1.0 / F, None, ALU.mult))
            ch.link(nc.vector.tensor_tensor(Y, Y, over_f(mean), ALU.subtract))
            ch.link(nc.vector.tensor_tensor(scratch, Y, Y, ALU.mult))
            ch.link(nc.vector.tensor_reduce(var[:, :], scratch, AX.X, ALU.add))
            nc.vector.tensor_scalar(var[:, :], var[:, :], 1.0 / F, EPS, ALU.mult, ALU.add).then_inc(var_made, 1)
            dve.wait_ge(root_made, n)
            ch.link(nc.vector.reciprocal(var[:, :], var[:, :]))
            ch.link(nc.vector.tensor_tensor(Y, Y, over_f(var), ALU.mult))

        def node_stage(l):
            ch = Chain(f"node_chain{l}")
            fetched, carried, var_made, root_made, ready, tabled = (
                sem(f"{n}{l}") for n in ("fetched", "carried", "var_made", "root_made", "ready", "tabled"))
            if l >= 2:
                tr_ps, tr_sb, mixed, u_made = (sem(f"{n}{l}") for n in ("tr_ps", "tr_sb", "mixed", "u_made"))
            banks = [list(range(t, min(t + 8, NT))) for t in range(0, NT, 8)]
            block = nc.Block()

            def bank3(b, n):
                return PS[b][:, 0:n * F].rearrange("p (t f) -> p t f", f=F)

            with block:
                @block.gpsimd
                def _(pool):
                    by_edge = sums[l].rearrange("p k f -> (p k) f")
                    for t in range(NT):
                        nc.gpsimd.indirect_dma_start(S1[:, t, :], None, by_edge, rows(end_row[:, t:t + 1])).then_inc(fetched, 16)

                @block.tensor
                def _(pe):
                    for b, tiles in enumerate(banks):
                        for j, t in enumerate(tiles):
                            ins = nc.tensor.matmul(PS[b][:, j * F:(j + 1) * F], cross[:, t * P:(t + 1) * P],
                                                   R[1][:, CH - 1, :], start=True, stop=True)
                    ins.then_inc(carried, 1)
                    if l >= 2:
                        pe.wait_ge(u_made, 1)
                        for g, tiles in enumerate(TILE_GROUPS):
                            if g >= 1:
                                pe.wait_ge(tr_sb, g)
                            for j, t in enumerate(tiles):
                                ins = nc.tensor.transpose(PS[7][0:F, j * P:(j + 1) * P], S1[:, t, :], ident[:, :])
                            ins.then_inc(tr_ps, 1)
                        pe.wait_ge(tr_sb, len(TILE_GROUPS))
                        for b, tiles in enumerate(banks):
                            for j, t in enumerate(tiles):
                                ins = nc.tensor.matmul(PS[b][:, j * F:(j + 1) * F], xt[0:F, t * P:(t + 1) * P],
                                                       gcn_s[:, l - 2, :], start=True, stop=True)
                        ins.then_inc(mixed, 1)

                @block.scalar
                def _(act):
                    if l >= 2:
                        act_untranspose(act, [PS[7], PS[7]], tr_ps, tr_sb)
                    if l != 2:
                        act.wait_ge(var_made, 1)
                        nc.scalar.activation(var[:, :], var[:, :], ACT.Sqrt).then_inc(root_made, 1)

                @block.vector
                def _(dve):
                    dve.wait_ge(fetched, 16 * NT)
                    ch.link(nc.vector.tensor_tensor(S1, S1, over_f(has), ALU.mult))
                    dve.wait_ge(carried, 1)
                    for b, tiles in enumerate(banks):
                        part = S1[:, tiles[0]:tiles[-1] + 1, :]
                        ins = nc.vector.tensor_tensor(part, part, bank3(b, len(tiles)), ALU.add)
                    ch.link(ins)
                    if l == 0:
                        ch.link(nc.vector.tensor_tensor(X[:, :, :], X[:, :, :], S1, ALU.add))
                    elif l == 1:
                        ch.link(nc.vector.tensor_tensor(S2, X[:, :, :], over_f(deg), ALU.mult))
                        ch.link(nc.vector.tensor_tensor(S1, S1, S2, ALU.add))
                        ch.link(nc.vector.tensor_tensor(S1, S1, over_f(inv), ALU.mult))
                        ch.link(nc.vector.tensor_tensor(S1, S1, X[:, :, :], ALU.add))
                        ch.link(nc.vector.tensor_tensor(X[:, :, :], S1, X[:, :, :], ALU.add))
                    else:
                        ch.link(nc.vector.tensor_tensor(S1, S1, S2, ALU.add))
                        nc.vector.tensor_tensor(S1, S1, over_f(dinv), ALU.mult).then_inc(u_made, 1)
                        dve.wait_ge(mixed, 1)
                        for b, tiles in enumerate(banks):
                            bias = bias_s[:, l - 2:l - 1, :].to_broadcast([P, len(tiles), F])
                            ins = nc.vector.tensor_tensor(S3[:, tiles[0]:tiles[-1] + 1, :], bank3(b, len(tiles)), bias, ALU.add)
                        ch.link(ins)
                        ch.link(nc.vector.tensor_scalar(S3, S3, 0.0, None, ALU.max))
                        if l == 3:
                            ch.link(nc.vector.tensor_tensor(X[:, :, :], X[:, :, :], S3, ALU.add))
                    if l != 2:
                        layer_norm(dve, ch, X[:, :, :], S1, var_made, root_made, 1)
                    if l in (1, 2):
                        ch.link(nc.vector.tensor_tensor(S2, X[:, :, :] if l == 1 else S3, over_f(dinv), ALU.mult))
                    nc.vector.tensor_copy(tot[:, 0:1], mean[:, 0:1]).then_inc(ready, 1)

                if l < 3:
                    @block.sync
                    def _(sp):
                        sp.wait_ge(ready, 1)
                        sp.dma_start(node_table[l].rearrange("(t p) f -> p t f", p=P), X[:, :, :] if l == 0 else S2)\
                            .then_inc(tabled, 16)
                        sp.wait_ge(tabled, 16)

        def edge_tables():
            tr_ps, tr_sb, mm, got_p, got_q, stored, put, first = (
                sem(n) for n in ("et_tr_ps", "et_tr_sb", "et_mm", "et_p", "et_q", "et_stored", "et_put", "et_first"))
            Pn = node[:, 0:NT * H].rearrange("p (t h) -> p t h", h=H)
            Qn = cross[:, :].rearrange("p (t h) -> p t h", h=H)
            block = nc.Block()
            with block:
                @block.tensor
                def _(pe):
                    pe_transpose(pe, X, PS[0:2], tr_ps, tr_sb)
                    for g, tiles in enumerate(TILE_GROUPS):
                        pe.wait_ge(tr_sb, g + 1)
                        if g >= 2:
                            pe.wait_ge(got_p, g - 1)
                            pe.wait_ge(got_q, g - 1)
                        for a in range(2):
                            for j, t in enumerate(tiles):
                                ins = nc.tensor.matmul(PS[2 + 2 * a + g % 2][:, j * H:(j + 1) * H], xt[0:F, t * P:(t + 1) * P],
                                                       ew1_s[:, a * H:(a + 1) * H], start=True, stop=True)
                        ins.then_inc(mm, 1)

                def bank(a, g, tiles):
                    return PS[2 + 2 * a + g % 2][:, 0:len(tiles) * H].rearrange("p (t h) -> p t h", h=H)

                @block.scalar
                def _(act):
                    act_untranspose(act, PS[0:2], tr_ps, tr_sb)
                    for g, tiles in enumerate(TILE_GROUPS):
                        act.wait_ge(mm, g + 1)
                        nc.scalar.copy(Qn[:, tiles[0]:tiles[-1] + 1, :], bank(1, g, tiles)).then_inc(got_q, 1)

                @block.vector
                def _(dve):
                    for g, tiles in enumerate(TILE_GROUPS):
                        dve.wait_ge(mm, g + 1)
                        nc.vector.tensor_copy(Pn[:, tiles[0]:tiles[-1] + 1, :], bank(0, g, tiles)).then_inc(got_p, 1)
                    nc.vector.tensor_copy(same[:, 0:1], comes_in[:, :])

                @block.sync
                def _(sp):
                    sp.wait_ge(got_p, len(TILE_GROUPS))
                    sp.wait_ge(got_q, len(TILE_GROUPS))
                    sp.dma_start(p_table.rearrange("(t p) h -> p t h", p=P), Pn).then_inc(stored, 16)
                    sp.dma_start(q_table.rearrange("(t p) h -> p t h", p=P), Qn).then_inc(stored, 16)
                    sp.wait_ge(stored, 32)

                @block.gpsimd
                def _(pool):
                    pool.wait_ge(got_q, len(TILE_GROUPS))
                    for t in range(NT):
                        nc.gpsimd.indirect_dma_start(q_starts, rows(start_row[:, t:t + 1]), Qn[:, t, :], None).then_inc(put, 16)
                    pool.wait_ge(stored, 32)
                    nc.gpsimd.indirect_dma_start(q_in[:, :], None, q_table, rows(first_dst[:, 0:1])).then_inc(first, 16)
                    pool.wait_ge(put, 16 * NT)
                    pool.wait_ge(first, 16)

        def edge_mlp():
            got, attr_in, rows_in, q_landed, idx_ready, put_ready = (
                [sem(f"{n}{u}") for u in range(2)] for n in ("e_got", "e_attr", "e_rows", "e_q", "e_idx", "e_pidx"))
            q_done, added, z1_ps, eq_ps, h1_sb, eq_sb, z2_ps, z2_sb, m_sb, s_ps, s_sb = (
                sem(f"e_{n}") for n in ("q_done", "added", "z1_ps", "eq_ps", "h1_sb", "eq_sb", "z2_ps", "z2_sb", "m_sb",
                                        "s_ps", "s_sb"))
            put = [sem(f"e_put{j}") for j in range(GR)]
            attr_s = [cross[0:1 + A, 0:CE * P], node[0:1 + A, 0:CE * P]]
            src_rows = [node[0:2, CE * P + u * CE * P // 2:CE * P + (u + 1) * CE * P // 2].bitcast(bf16) for u in range(2)]
            h1, z2b, msg, equal, total = ([xt[:, 1024 * a + 512 * b:1024 * a + 512 * (b + 1)] for b in range(2)] for a in range(5))
            q_rows = q_starts[0:EP, :].rearrange("(p k) h -> p k h", p=P)

            def groups(c, u, first, lag, do):
                for s in range(NG + lag[-1]):
                    for d, f in zip(lag, do):
                        g = s - d
                        if 0 <= g < NG:
                            f(g, (u + g) % 2, first and u * NG + g < 2)

            block = nc.Block()
            with block:
                @block.sync
                def _(sp):
                    def chunk(i, u, c, first):
                        if not first:
                            wait_counts(sp, (z1_ps, (c - 1) * NG), (eq_ps, (c - 1) * NG), (added, (c - 1) * NG), (q_done, c))
                        sp.dma_start(attr_s[u], attr_t[:, ds(c * (CE * P), CE * P)]).then_inc(attr_in[u], 16)
                        sp.dma_start(src_rows[u], src_split[:, ds(c * (CE * P), CE * P)]).then_inc(rows_in[u], 16)
                        sp.dma_start(QE[u], q_rows[:, ds(c * CE, CE), :]).then_inc(q_landed[u], 16)
                    by_pairs(sp, NCE, chunk)

                @block.gpsimd
                def _(pool):
                    def both(i, u, c, first, puts):
                        if c is not None:
                            if not first:
                                pool.wait_ge(got[u], i * (16 * CE))
                                pool.wait_ge(z1_ps, (c - 1) * NG)
                            nc.gpsimd.tensor_copy(get_rows[:, u, 0:CE], src_i[:, ds(c * CE, CE)]).then_inc(idx_ready[u], 1)
                            wait_counts(pool, (idx_ready[u], i + 1))
                        if puts:
                            pi, pu, pc, pfirst = puts
                            nc.gpsimd.tensor_copy(put_rows[:, pu, :], row_idx[:, ds(pc * CE, CE)]).then_inc(put_ready[pu], 1)
                            wait_counts(pool, (put_ready[pu], pi + 1))
                        for g in range(NG):
                            if c is not None:
                                for k in range(g * GR, (g + 1) * GR):
                                    nc.gpsimd.indirect_dma_start(GE[u][:, k, :], None, p_table, rows(get_rows[:, u, k:k + 1]))\
                                        .then_inc(got[u], 16)
                            if puts:
                                b = (pu + g) % 2
                                wait_counts(pool, (s_sb, pc * NG + (g + 1)))
                                for j in range(GR):
                                    if not (pfirst and pu * NG + g == 0):
                                        wait_counts(pool, (put[j], pc * (16 * NG) + 16 * g))
                                    nc.gpsimd.indirect_dma_start(
                                        agg_table[j], rows(put_rows[:, pu, g * GR + j:g * GR + j + 1]),
                                        total[b][:, j * H:(j + 1) * H], None, compute_op=ALU.add).then_inc(put[j], 16)

                    both(0, 0, 0, True, None)
                    both(0, 1, 1, True, (0, 0, 0, True))
                    with pool.Fori(1, NCE // 2) as i:
                        both(i, 0, i * 2, False, (i - 1, 1, i * 2 - 1, False))
                        both(i, 1, i * 2 + 1, False, (i, 0, i * 2, False))
                    both(None, None, None, None, (NCE // 2 - 1, 1, NCE - 1, False))
                    for j in range(GR):
                        pool.wait_ge(put[j], 16 * NG * NCE)

                @block.vector
                def _(dve):
                    def chunk(i, u, c, first):
                        dve.wait_ge(q_landed[u], (i + 1) * 16)
                        if not (first and u == 0):
                            dve.wait_ge(q_done, c)
                        for h in range(H):
                            start = q_in[:, h:h + 1] if first and u == 0 else QE[1 - u][:, CE - 1, h:h + 1]
                            ins = nc.vector.tensor_tensor_scan(QE[u][:, :, h], same[:, ds(c * CE, CE)], QE[u][:, :, h],
                                                               start, ALU.mult, ALU.add)
                        ins.then_inc(q_done, 1)
                        dve.wait_ge(q_done, c + 1)
                        dve.wait_ge(got[u], (i + 1) * (16 * CE))

                        def add(g, b, fresh):
                            part = GE[u][:, g * GR:(g + 1) * GR, :]
                            nc.vector.tensor_tensor(part, part, QE[u][:, g * GR:(g + 1) * GR, :], ALU.add).then_inc(added, 1)

                        def compare(g, b, fresh):
                            dve.wait_ge(eq_ps, c * NG + (g + 1))
                            if not fresh:
                                dve.wait_ge(s_ps, c * NG + (g - 1))
                            nc.vector.tensor_tensor(
                                equal[b].rearrange("p (j e) -> p j e", e=P), PS[2 + b][:, :].rearrange("p (j e) -> p j e", e=P),
                                src_i[:, ds(c * CE + g * GR, GR)].rearrange("p (j o) -> p j o", o=1).to_broadcast([P, GR, P]),
                                ALU.is_equal).then_inc(eq_sb, 1)

                        def bias(g, b, fresh):
                            dve.wait_ge(z2_ps, c * NG + (g + 1))
                            if not fresh:
                                dve.wait_ge(m_sb, c * NG + (g - 1))
                            nc.vector.tensor_tensor(
                                z2b[b].rearrange("p (j h) -> p j h", h=H), PS[4 + b][:, :].rearrange("p (j h) -> p j h", h=H),
                                eb2_s[:, :].rearrange("p (o h) -> p o h", o=1).to_broadcast([P, GR, H]), ALU.add)\
                                .then_inc(z2_sb, 1)
                        groups(c, u, first, (0, 0, 1), (add, compare, bias))
                    by_pairs(dve, NCE, chunk)

                @block.tensor
                def _(pe):
                    def chunk(i, u, c, first):
                        pe.wait_ge(attr_in[u], (i + 1) * 16)
                        pe.wait_ge(rows_in[u], (i + 1) * 16)

                        def layer1(g, b, fresh):
                            if not fresh:
                                pe.wait_ge(h1_sb, c * NG + (g - 1))
                            nc.tensor.matmul(PS[b][:, :], we_s[:, :], attr_s[u][:, g * GR * P:(g + 1) * GR * P],
                                             start=True, stop=False)
                            pe.wait_ge(added, c * NG + (g + 1))
                            for j in range(GR):
                                ins = nc.tensor.matmul(PS[b][:, j * P:(j + 1) * P], GE[u][:, g * GR + j, :], ident[:, :],
                                                       start=False, stop=j == GR - 1)
                            ins.then_inc(z1_ps, 1)

                        def sources(g, b, fresh):
                            if not fresh:
                                pe.wait_ge(eq_sb, c * NG + (g - 1))
                            nc.tensor.matmul(PS[2 + b][:, :], ones_bf[:, :], src_rows[u][:, g * GR * P:(g + 1) * GR * P],
                                             start=True, stop=True).then_inc(eq_ps, 1)

                        def layer2(g, b, fresh):
                            pe.wait_ge(h1_sb, c * NG + (g + 1))
                            if not fresh:
                                pe.wait_ge(z2_sb, c * NG + (g - 1))
                            for j in range(GR):
                                ins = nc.tensor.matmul(PS[4 + b][:, j * H:(j + 1) * H], h1[b][:, j * P:(j + 1) * P], ew2_s[:, :],
                                                       start=True, stop=True)
                            ins.then_inc(z2_ps, 1)

                        def combine(g, b, fresh):
                            pe.wait_ge(m_sb, c * NG + (g + 1))
                            pe.wait_ge(eq_sb, c * NG + (g + 1))
                            if not fresh:
                                pe.wait_ge(s_sb, c * NG + (g - 1))
                            for j in range(GR):
                                ins = nc.tensor.matmul(PS[6 + b][:, j * H:(j + 1) * H], equal[b][:, j * P:(j + 1) * P],
                                                       msg[b][:, j * H:(j + 1) * H], start=True, stop=True)
                            ins.then_inc(s_ps, 1)
                        groups(c, u, first, (0, 0, 1, 2), (layer1, sources, layer2, combine))
                    by_pairs(pe, NCE, chunk)

                @block.scalar
                def _(act):
                    def chunk(i, u, c, first):
                        def silu1(g, b, fresh):
                            act.wait_ge(z1_ps, c * NG + (g + 1))
                            if not fresh:
                                act.wait_ge(z2_ps, c * NG + (g - 1))
                            nc.scalar.activation(h1[b], PS[b][:, :], ACT.Silu, bias=hid_s[:, 0:1]).then_inc(h1_sb, 1)

                        def silu2(g, b, fresh):
                            act.wait_ge(z2_sb, c * NG + (g + 1))
                            if not fresh:
                                act.wait_ge(s_ps, c * NG + (g - 1))
                            nc.scalar.activation(msg[b], z2b[b], ACT.Silu).then_inc(m_sb, 1)

                        def take(g, b, fresh):
                            act.wait_ge(s_ps, c * NG + (g + 1))
                            if not fresh:
                                for j in range(GR):
                                    act.wait_ge(put[j], c * (16 * NG) + 16 * (g - 1))
                            nc.scalar.copy(total[b], PS[6 + b][:, :]).then_inc(s_sb, 1)
                        groups(c, u, first, (0, 1, 2), (silu1, silu2, take))
                    by_pairs(act, NCE, chunk)

        def finish():
            ch = Chain("fin_chain")
            tab, summed, a_ps, x_ps, a_sb, x_sb, h_ps, h_sb, u_ps, u_sb, var_made, root_made, normed, written = (
                sem(f"f_{n}") for n in ("tab", "summed", "a_ps", "x_ps", "a_sb", "x_sb", "h_ps", "h_sb", "u_ps", "u_sb",
                                        "var", "root", "normed", "written"))
            part = [cross[:, :], node[:, 0:NP], xt[:, :]]
            agg = cross[:, :].rearrange("p (t h) -> p t h", h=H)
            aT, xT, hT = ([b[:, w:w + 512] for b in gbuf] for w in (0, 512, 1024))
            block = nc.Block()
            with block:
                @block.sync
                def _(sp):
                    for j in range(GR):
                        if j == 3:
                            sp.wait_ge(summed, 1)
                        sp.dma_start(part[j if j < 3 else 1].rearrange("p (t h) -> p t h", h=H),
                                     agg_table[j][0:NP, :].rearrange("(t p) h -> p t h", p=P)).then_inc(tab, 16)
                    sp.wait_ge(normed, 1)
                    whole = N // P
                    sp.dma_start(out[0:whole * P, :].rearrange("(t p) f -> p t f", p=P), X[:, 0:whole, :]).then_inc(written, 16)
                    sp.dma_start(out[whole * P:N, :], X[0:N - whole * P, whole, :]).then_inc(written, 16)
                    sp.wait_ge(written, 32)

                @block.tensor
                def _(pe):
                    pe.wait_ge(summed, 3)
                    for g, tiles in enumerate(TILE_GROUPS):
                        b, n = g % 2, len(tiles)
                        if g >= 2:
                            pe.wait_ge(a_sb, g - 1)
                            pe.wait_ge(x_sb, g - 1)
                        for j, t in enumerate(tiles):
                            ins = nc.tensor.transpose(PS[b][:, j * P:(j + 1) * P], agg[:, t, :], ident[:, :])
                        ins.then_inc(a_ps, 1)
                        for j, t in enumerate(tiles):
                            ins = nc.tensor.transpose(PS[2 + b][0:F, j * P:(j + 1) * P], X[:, t, :], ident[:, :])
                        ins.then_inc(x_ps, 1)
                        pe.wait_ge(a_sb, g + 1)
                        pe.wait_ge(x_sb, g + 1)
                        if g >= 2:
                            pe.wait_ge(h_sb, g - 1)
                        nc.tensor.matmul(PS[4 + b][:, 0:n * P], nw1x_s[:, :], xT[b][0:F, 0:n * P], start=True, stop=False)
                        nc.tensor.matmul(PS[4 + b][:, 0:n * P], nw1a_s[:, :], aT[b][:, 0:n * P], start=False, stop=True)\
                            .then_inc(h_ps, 1)
                        pe.wait_ge(h_sb, g + 1)
                        if g >= 2:
                            pe.wait_ge(u_sb, g - 1)
                        for j in range(n):
                            ins = nc.tensor.matmul(PS[6 + b][:, j * F:(j + 1) * F], hT[b][:, j * P:(j + 1) * P], nw2_s[:, :],
                                                   start=True, stop=True)
                        ins.then_inc(u_ps, 1)

                @block.scalar
                def _(act):
                    for g, tiles in enumerate(TILE_GROUPS):
                        b, n = g % 2, len(tiles)
                        act.wait_ge(a_ps, g + 1)
                        if g >= 2:
                            act.wait_ge(h_ps, g - 1)
                        nc.scalar.copy(aT[b][:, 0:n * P], PS[b][:, 0:n * P]).then_inc(a_sb, 1)
                        act.wait_ge(h_ps, g + 1)
                        if g >= 2:
                            act.wait_ge(u_ps, g - 1)
                        nc.scalar.activation(hT[b][:, 0:n * P], PS[4 + b][:, 0:n * P], ACT.Silu, bias=hid_s[:, 1:2]).then_inc(h_sb, 1)
                    act.wait_ge(var_made, 1)
                    nc.scalar.activation(var[:, :], var[:, :], ACT.Sqrt).then_inc(root_made, 1)

                @block.vector
                def _(dve):
                    for j in range(1, GR):
                        dve.wait_ge(tab, 16 * (3 if j < 3 else 4))
                        nc.vector.tensor_tensor(part[0], part[0], part[j if j < 3 else 1], ALU.add).then_inc(summed, 1)
                        dve.wait_ge(summed, j)
                    for g, tiles in enumerate(TILE_GROUPS):
                        b, n = g % 2, len(tiles)
                        dve.wait_ge(x_ps, g + 1)
                        if g >= 2:
                            dve.wait_ge(h_ps, g - 1)
                        nc.vector.tensor_copy(xT[b][0:F, 0:n * P], PS[2 + b][0:F, 0:n * P]).then_inc(x_sb, 1)
                        dve.wait_ge(u_ps, g + 1)
                        nc.vector.tensor_tensor(S1[:, tiles[0]:tiles[-1] + 1, :],
                                                PS[6 + b][:, 0:n * F].rearrange("p (t f) -> p t f", f=F),
                                                bias_s[:, 2:3, :].to_broadcast([P, n, F]), ALU.add).then_inc(u_sb, 1)
                    dve.wait_ge(u_sb, len(TILE_GROUPS))
                    ch.link(nc.vector.tensor_tensor(S1, S1, X[:, :, :], ALU.add))
                    ch.link(nc.vector.tensor_tensor(X[:, :, :], S1, X[:, :, :], ALU.add))
                    layer_norm(dve, ch, X[:, :, :], S1, var_made, root_made, 1)
                    nc.vector.tensor_copy(tot[:, 0:1], mean[:, 0:1]).then_inc(normed, 1)

        prepare()
        relation_table()
        gather_pass(0, rel_table, row_idx)
        degrees()
        node_stage(0)
        for l in (1, 2, 3):
            gather_pass(l, node_table[l - 1], src_i)
            node_stage(l)
        edge_tables()
        edge_mlp()
        finish()


def kernel(**inputs):
    import numpy as np
    import concourse.bacc as bacc
    from concourse.bass_utils import run_bass_kernel_spmd

    a = {k: np.asarray(v) for k, v in inputs.items()}

    def edges(v, fill):
        full = np.full((EP,) + v.shape[1:], fill, v.dtype)
        full[:E] = v
        return full.reshape((P, KT) + v.shape[1:])

    src, dst = edges(a["src"], NP - 1), edges(a["dst"], N)
    ew1 = a["L3_gnn_ew1"]
    bias_rows = np.stack([a["L2_gnn_b1"], a["L2_gnn_b2"], a["L3_gnn_nb2"]])
    weighted = np.concatenate([a["edge_weight"][:, None], a["edge_attr_16"]], 1)
    arrays = {
        "x": np.concatenate([a["x"], np.zeros((NP - N, F), a["x"].dtype)]),
        "src": src,
        "dst": dst,
        "etype": edges(a["edge_type_16"], 0),
        "src_t": src.T.reshape(P, KT),
        "attr_t": edges(weighted, 0).transpose(2, 1, 0).reshape(1 + A, EP),
        "rel_w": a["L0_gnn_W"].transpose(2, 0, 1).reshape(F, RELS * F),
        "gcn_w": np.stack([a["L2_gnn_W1"], a["L2_gnn_W2"]], 1),
        "bias_rows": np.broadcast_to(bias_rows, (P, 3, F)),
        "ew1": np.concatenate([ew1[:F], ew1[F:2 * F]], 1),
        "we": np.concatenate([ew1[2 * F + A:], ew1[2 * F:2 * F + A]]),
        "ew2": a["L3_gnn_ew2"],
        "hid_b": np.stack([a["L3_gnn_eb1"], a["L3_gnn_nb1"]], 1),
        "eb2_rows": np.broadcast_to(a["L3_gnn_eb2"], (P, H)),
        "nw1x": a["L3_gnn_nw1"][:F],
        "nw1a": a["L3_gnn_nw1"][F:],
        "nw2": a["L3_gnn_nw2"],
    }
    arrays = {k: np.ascontiguousarray(v) for k, v in arrays.items()}
    nc = bacc.Bacc("TRN2", target_bir_lowering=False, num_devices=1)
    args = {k: nc.dram_tensor(f"in_{k}", v.shape, mybir.dt.from_np(v.dtype), kind="ExternalInput").ap() for k, v in arrays.items()}
    out = nc.dram_tensor("out", (N, F), mybir.dt.float32, kind="ExternalOutput").ap()
    gnn_kernel(nc, out=out, **args)
    r = run_bass_kernel_spmd(nc, [{f"in_{k}": v for k, v in arrays.items()}], core_ids=[0])
    return r.results[0]["out"]
```

```python
from contextlib import ExitStack

import concourse.bass as bass
from concourse import mybir

N, E, F, H, A, RELS = 6250, 200000, 64, 128, 16, 16
P = 128
NT = -(-N // P)
NP = NT * P
CH = 56
NCH = -(-E // (P * CH))
KT = NCH * CH
EP = KT * P
GR = 4
CE = 28
NCE = KT // CE
NG = CE // GR
HB = 8
NH = CH // HB
WN = 8
WJ = 3
WE = WJ * P
WC = WN * NT
WT = P // WN
BT = 4 * (NCH // 2 - 1)
WA, WB = BT * WT // 32, 32
WR = (BT + 4) * WT
WH = 16
EXACT = 256
PARTS = 3
EPS = 1e-5
CUTOFF = 5.0
assert BT >= NT and WA * WB == BT * WT and NT % 4 == 1 and KT % (2 * WH) == 0
assert NCH % 2 == 0 and NCE % 2 == 0 and NG % 2 == 1 and NH % 2 == 1
TILE_GROUPS = [list(range(t, min(t + GR, NT))) for t in range(0, NT, GR)]


def gnn_kernel(nc, x, src, dst, etype, src_t, dst_t, attr_t, attr_rows, rel_w, gcn_w, bias_rows, ew1, we, ew2, hid_b,
               eb2_rows, nw1x, nw1a, nw2, out):
    f32, bf16, i32 = mybir.dt.float32, mybir.dt.bfloat16, mybir.dt.int32
    ALU, ACT, AX = mybir.AluOpType, mybir.ActivationFunctionType, mybir.AxisListType
    ds = bass.ds
    ctx = ExitStack()
    with ctx, nc.allow_non_contiguous_dma(reason="columns of the edge lists"):
        def sb(name, shape, dt=f32):
            return ctx.enter_context(nc.sbuf_tensor(name, shape, dt))

        def sem(name):
            return ctx.enter_context(nc.semaphore(name))

        def rows(col):
            return bass.IndirectOffsetOnAxis(ap=col, axis=0)

        rel_table = nc.dram_tensor("rel_table", [NP * RELS, F], f32).ap()
        node_table = [nc.dram_tensor(f"node_table{i}", [NP, F], f32).ap() for i in range(3)]
        sums = [nc.dram_tensor(f"sums{i}", [P, KT, F], f32).ap() for i in range(4)]
        p_table = nc.dram_tensor("p_table", [NP, H], f32).ap()
        q_table = nc.dram_tensor("q_table", [NP, H], f32).ap()
        q_starts = nc.dram_tensor("q_starts", [EP + NP, H], f32).ap()
        agg_table = [nc.dram_tensor(f"agg_table{j}", [NP + P, H], f32).ap() for j in range(GR)]
        src_split = nc.dram_tensor("src_split", [2, EP], bf16).ap()

        by_dst = {n: nc.dram_tensor(f"by_dst_{n}", [EP, 1], i32).ap() for n in ("dst", "src", "type")}
        by_dst_src_t = nc.dram_tensor("by_dst_src_t", [P, KT], i32).ap()
        by_dst_rows = nc.dram_tensor("by_dst_rows", [EP, 1 + A], f32).ap()
        edge_attr = nc.dram_tensor("edge_attr", [1 + A, EP], f32).ap()
        cursor = nc.dram_tensor("cursor", [NP + P, 1], f32).ap()
        starts = nc.dram_tensor("starts", [NP, 1], f32).ap()

        keys = nc.dram_tensor("keys", [EP + 4 * P, 2], f32).ap()
        win_first = nc.dram_tensor("win_first", [WA * WB, 1], i32).ap()
        counts = nc.dram_tensor("counts", [BT, P, NT * P], bf16).ap()

        src_i = sb("src_i", [P, KT], i32)
        row_idx = sb("row_idx", [P, KT], i32)
        same = sb("same", [P, KT])
        dst_tile = sb("dst_tile", [P, KT], bf16)
        cross = sb("cross", [P, NP])
        xt = sb("xt", [P, NP])
        X = sb("X", [P, NT, F])
        node = sb("node", [P, 3 * NT * F])
        S1, S2, S3 = (node[:, i * NT * F:(i + 1) * NT * F].rearrange("p (t f) -> p t f", f=F) for i in range(3))
        gbuf = [sb(f"gbuf{u}", [P, CH * F]) for u in range(2)]
        rbuf = [sb(f"rbuf{u}", [P, CH * F]) for u in range(2)]
        G, R = ([b[:, :].rearrange("p (k f) -> p k f", f=F) for b in bufs] for bufs in (gbuf, rbuf))
        GE, QE = ([b[:, :].rearrange("p (k h) -> p k h", h=H) for b in bufs] for bufs in (gbuf, rbuf))
        get_rows = sb("get_rows", [P, 2, CH], i32)
        put_rows = sb("put_rows", [P, 2, CE], i32)
        ident = sb("ident", [P, P])
        before = sb("before", [P, P], bf16)
        upto = sb("upto", [P, P])
        ones = sb("ones", [P, P])
        ones_bf = sb("ones_bf", [2, P], bf16)
        count_i = sb("count_i", [P, P], i32)
        count_bf = sb("count_bf", [P, P], bf16)
        zeros = sb("zeros", [P, 512])
        zero_bf = sb("zero_bf", [P, P], bf16)
        dump_i = sb("dump_i", [P, 1 + NT], i32)
        dump = sb("dump", [P, 1 + NT])
        comes_in = sb("comes_in", [P, 1])
        goes_out = sb("goes_out", [P, 1])
        last_dst = sb("last_dst", [P, 1])
        near_dst = sb("near_dst", [P, 2], i32)
        first_dst = sb("first_dst", [P, 1], i32)
        deg, has, inv, dinv, tmp, tot, mean, var = (sb(n, [P, NT]) for n in ("deg", "has", "inv", "dinv", "tmp", "tot", "mean", "var"))
        end_row = sb("end_row", [P, NT], i32)
        start_row = sb("start_row", [P, NT], i32)
        q_in = sb("q_in", [P, H])
        gcn_s = sb("gcn_s", [F, 2, F])
        bias_s = sb("bias_s", [P, 3, F])
        eb2_s = sb("eb2_s", [P, H])
        ew1_s = sb("ew1_s", [F, 2 * H])
        we_s = sb("we_s", [1 + A, H])
        ew2_s = sb("ew2_s", [H, H])
        hid_s = sb("hid_s", [H, 2])
        nw1x_s = sb("nw1x_s", [F, H])
        nw1a_s = sb("nw1a_s", [H, H])
        nw2_s = sb("nw2_s", [H, F])
        win_hl = node[:, NP:NP + KT].bitcast(bf16).rearrange("p (a k) -> p a k", a=2)
        place_off = node[:, NP + KT:NP + 2 * KT]
        minus = sb("minus", [P, 8])
        lane = sb("lane", [P, WC], mybir.dt.float16)
        win_base = sb("win_base", [P, WT])
        win_most = sb("win_most", [P, 1])
        key_slot = sb("key_slot", [P, 4, WT, 2 * WJ])
        key_rel = sb("key_rel", [P, WT, WJ])
        irregular = sb("irregular", [P, 1], i32)
        shuffled = sb("shuffled", [P, 1], i32)
        attr_there = sem("attr_there")
        dst_i = rbuf[0][:, 0:KT].bitcast(i32)
        typ_i = rbuf[0][:, KT:2 * KT].bitcast(i32)
        srt_i = xt[:, 0:KT].bitcast(i32)
        PS = [ctx.enter_context(nc.psum_tensor(f"PS{i}", [P, 512], f32)) for i in range(8)]

        def over_f(col):
            return col[:, :].rearrange("p (t o) -> p t o", o=1).to_broadcast([P, NT, F])

        begun = sem("begun")

        def wait_counts(eng, *waits):
            counts = [n if isinstance(n, int) else eng.to_reg(n) for _, n in waits]
            eng.wait_ge(begun, 1)
            for (signal, _), n in zip(waits, counts):
                eng.wait_ge(signal, n)

        def by_pairs(eng, n, body):
            for u in range(2):
                body(0, u, u, True)
            with eng.Fori(1, n // 2) as i:
                for u in range(2):
                    body(i, u, i * 2 + u, False)

        class Chain:

            def __init__(self):
                self.sem, self.n = sem("dve_chain"), 0

            def link(self, ins):
                self.n += 1
                ins.then_inc(self.sem, 1)
                nc.vector.wait_ge(self.sem, self.n)

        ch = Chain()
        fetched, carried, ready, tabled, var_made, root_made, nd_tr_ps, nd_tr_sb, mixed, u_made = (
            sem(n) for n in ("fetched", "carried", "ready", "tabled", "var_made", "root_made", "nd_tr_ps", "nd_tr_sb",
                             "mixed", "u_made"))

        def check_order():
            loaded, weights, preset, near, made, summed, flagged = (
                sem(n) for n in ("loaded", "weights", "preset", "near", "made", "viol_sum", "flagged"))
            falls = rbuf[1][:, 0:KT]
            block = nc.Block()
            with block:
                @block.sync
                def _(sp):
                    sp.dma_start(dst_i, dst).then_inc(loaded, 16)
                    sp.dma_start(src_i[:, :], src).then_inc(loaded, 16)
                    sp.dma_start(typ_i, etype).then_inc(loaded, 16)
                    sp.dma_start(X[:, :, :], x.rearrange("(t p) f -> p t f", p=P)).then_inc(loaded, 16)
                    sp.wait_ge(preset, 1)
                    sp.dma_start(near_dst[1:P, 0:1], dst[0:P - 1, KT - 1:KT]).then_inc(near, 16)
                    sp.wait_ge(loaded, 16 * 4)

                @block.scalar
                def _(act):
                    for a, b in ((cross[0:F, 0:RELS * F], rel_w), (gcn_s[:, :, :], gcn_w), (bias_s[:, :, :], bias_rows),
                                 (eb2_s[:, :], eb2_rows), (ew1_s[:, :], ew1), (we_s[:, :], we), (ew2_s[:, :], ew2),
                                 (hid_s[:, :], hid_b), (nw1x_s[:, :], nw1x), (nw1a_s[:, :], nw1a), (nw2_s[:, :], nw2)):
                        act.dma_start(a, b).then_inc(weights, 16)
                    act.wait_ge(weights, 16 * 11)

                @block.gpsimd
                def _(pool):
                    nc.gpsimd.memset(near_dst[:, :], -1).then_inc(preset, 1)
                    nc.gpsimd.memset(zeros[:, :], 0.0).then_inc(begun, 1)
                    nc.gpsimd.memset(zero_bf[:, :], 0.0)
                    nc.gpsimd.memset(ones[:, :], 1.0).then_inc(made, 1)
                    nc.gpsimd.memset(ones_bf[:, :], 1.0)
                    nc.gpsimd.memset(minus[:, :], -1.0)
                    nc.gpsimd.memset(win_most[:, :], 0.0)
                    nc.gpsimd.iota(lane[:, :], pattern=[[1, WC]], base=0, channel_multiplier=0,
                                   allow_small_or_imprecise_dtypes=True)
                    nc.gpsimd.iota(win_base[:, :], pattern=[[WC, WT]], base=0, channel_multiplier=0,
                                   allow_small_or_imprecise_dtypes=True)
                    nc.gpsimd.iota(dump_i[:, 0:1], pattern=[[0, 1]], base=NP, channel_multiplier=1)
                    nc.gpsimd.iota(dump_i[:, 1:1 + NT], pattern=[[P, NT]], base=EP, channel_multiplier=1)
                    nc.gpsimd.iota(count_i[:, :], pattern=[[1, P]], base=0, channel_multiplier=0).then_inc(made, 1)
                    pool.wait_ge(made, 2)
                    nc.gpsimd.affine_select(out=ident[:, :], in_=ones[:, :], compare_op=ALU.is_equal, fill=0.0,
                                            base=0, pattern=[[-1, P]], channel_multiplier=1)
                    nc.gpsimd.affine_select(out=before[:, :], in_=ones[:, :], compare_op=ALU.is_gt, fill=0.0,
                                            base=0, pattern=[[-1, P]], channel_multiplier=1)
                    nc.gpsimd.affine_select(out=upto[:, :], in_=ones[:, :], compare_op=ALU.is_ge, fill=0.0,
                                            base=0, pattern=[[1, P]], channel_multiplier=-1)

                @block.vector
                def _(dve):
                    dve.wait_ge(made, 2)
                    nc.vector.tensor_copy(count_bf[:, :], count_i[:, :])
                    nc.vector.tensor_copy(dump[:, :], dump_i[:, :])
                    dve.wait_ge(weights, 16 * 11)
                    nc.vector.tensor_scalar(we_s[0:1, :], we_s[0:1, :], 1.0 / CUTOFF, None, ALU.mult)
                    dve.wait_ge(loaded, 16 * 4)
                    nc.vector.tensor_tensor(falls[:, 1:KT], dst_i[:, 1:KT], dst_i[:, 0:KT - 1], ALU.is_lt)
                    dve.wait_ge(near, 16)
                    ch.link(nc.vector.tensor_tensor(falls[:, 0:1], dst_i[:, 0:1], near_dst[:, 0:1], ALU.is_lt))
                    nc.vector.tensor_reduce(tmp[:, 0:1], falls, AX.X, ALU.max).then_inc(flagged, 1)
                    dve.wait_ge(summed, 1)
                    nc.vector.tensor_scalar(shuffled[:, :], PS[0][:, 0:1], 1.0, None, ALU.min)

                @block.tensor
                def _(pe):
                    pe.wait_ge(made, 2)
                    pe.wait_ge(flagged, 1)
                    nc.tensor.matmul(PS[0][:, 0:1], ones[:, :], tmp[:, 0:1], start=True, stop=True).then_inc(summed, 1)

        def order_edges():
            srt_in, init, row_in, row_used, idx, cur_in, made, put, totals, table_in, pre, start_out = (
                sem(f"o_{n}") for n in ("srt", "init", "row", "row_used", "idx", "cur", "made", "put", "totals",
                                        "table_in", "pre", "start_out"))
            rec_in, relaid, chain, idx2, cur2, made2 = (
                sem(f"o_{n}") for n in ("rec_in", "relaid", "chain", "idx2", "cur2", "made2"))
            moved = [sem(f"o_moved{a}") for a in range(4)]
            rank = rbuf[1][:, 0:KT]
            row = node[:, 0:P].bitcast(i32)
            same_t, prior = node[:, P:2 * P], node[:, 2 * P:3 * P]
            col = [node[:, 3 * P + 8 * j:3 * P + 8 * j + 1] for j in range(12)]
            col_i = [c.bitcast(i32) for c in col]
            at, target, place, v_dst, v_src, v_typ = col_i[0:6]
            met, n_prior, n_same, count, gap, begin = col[6:12]
            rec = node[:, 512:512 + 1 + A]
            LINKS = 7
            block = nc.Block()

            def steps(eng, body):
                body(0, True)
                with eng.Fori(1, KT) as k:
                    body(k, False)

            with block:
                @block.sync
                def _(sp):
                    flag = sp.value_load(shuffled[0:1, 0:1], min_val=0, max_val=1)
                    with sp.If(flag != 0):
                        sp.dma_start(cursor.rearrange("(p a) o -> p (a o)", p=P), zeros[:, 0:(NP + P) // P]).then_inc(init, 16)

                        def targets(k, first):
                            if not first:
                                wait_counts(sp, (row_used, k * 1))
                            sp.dma_start(row, dst_t[0:1, ds(k * P, P)].to_broadcast([P, P])).then_inc(row_in, 16)
                        steps(sp, targets)
                        sp.wait_ge(put, 16 * KT)
                        sp.dma_start(deg[:, :], cursor[0:NP, :].rearrange("(t p) o -> p (t o)", p=P)).then_inc(table_in, 16)
                        sp.wait_ge(pre, 2)
                        sp.dma_start(starts.rearrange("(t p) o -> p (t o)", p=P), tmp[:, :]).then_inc(start_out, 16)

                        def records(k, first):
                            if not first:
                                wait_counts(sp, (moved[3], k * 16))
                            sp.dma_start(rec, attr_rows[:, ds(k, 1), :].rearrange("p o a -> p (o a)")).then_inc(rec_in, 16)
                        steps(sp, records)
                        for a in range(4):
                            sp.wait_ge(moved[a], 16 * KT)
                        sp.dma_start(by_dst_src_t.rearrange("p k -> (p k)").rearrange("(k p) -> k p", p=P),
                                     by_dst["src"].rearrange("(p k) o -> k (p o)", p=P)).then_inc(relaid, 16)
                        for a in range(1 + A):
                            sp.dma_start(edge_attr[a, :].rearrange("(k p) -> k p", p=P),
                                         by_dst_rows[:, a:a + 1].rearrange("(p k) o -> k (p o)", p=P)).then_inc(relaid, 16)
                        for to, n in ((dst_i, "dst"), (src_i[:, :], "src"), (typ_i, "type")):
                            sp.dma_start(to, by_dst[n].rearrange("(p k) o -> p (k o)", p=P)).then_inc(relaid, 16)
                        sp.wait_ge(relaid, 16 * (2 + A + 3))
                        sp.dma_start(srt_i, by_dst_src_t).then_inc(srt_in, 16)
                        sp.sem_inc(attr_there, 16)
                    with sp.Else():
                        sp.dma_start(edge_attr, attr_t).then_inc(attr_there, 16)
                        sp.dma_start(srt_i, src_t).then_inc(srt_in, 16)
                    sp.wait_ge(srt_in, 16)

                @block.gpsimd
                def _(pool):
                    flag = pool.value_load(shuffled[0:1, 0:1], min_val=0, max_val=1)
                    with pool.If(flag != 0):
                        pool.wait_ge(init, 16)

                        def count_step(k, first):
                            nc.gpsimd.tensor_copy(at, dst_i[:, ds(k, 1)]).then_inc(idx, 1)
                            waits = [(idx, k + 1)]
                            if not first:
                                waits.append((put, k * 16))
                            wait_counts(pool, *waits)
                            nc.gpsimd.indirect_dma_start(met, None, cursor, rows(at)).then_inc(cur_in, 16)
                            wait_counts(pool, (made, k + 1))
                            nc.gpsimd.indirect_dma_start(cursor, rows(target), count, None).then_inc(put, 16)
                        steps(pool, count_step)
                        pool.wait_ge(start_out, 16)

                        def move_step(k, first):
                            if not first:
                                for a in range(4):
                                    pool.wait_ge(moved[a], k * 16)
                            for to, of in ((at, dst_i), (v_dst, dst_i), (v_src, src_i), (v_typ, typ_i)):
                                ins = nc.gpsimd.tensor_copy(to, of[:, ds(k, 1)])
                            ins.then_inc(idx2, 1)
                            wait_counts(pool, (idx2, k + 1))
                            nc.gpsimd.indirect_dma_start(begin, None, starts, rows(at)).then_inc(cur2, 16)
                            wait_counts(pool, (made2, k + 1), (rec_in, k * 16 + 16))
                            for a, (to, of) in enumerate(((by_dst["dst"], v_dst), (by_dst["src"], v_src),
                                                          (by_dst["type"], v_typ), (by_dst_rows, rec))):
                                nc.gpsimd.indirect_dma_start(to, rows(place), of, None).then_inc(moved[a], 16)
                        steps(pool, move_step)
                        for a in range(4):
                            pool.wait_ge(moved[a], 16 * KT)
                    with pool.Else():
                        nc.gpsimd.memset(put_rows[:, :, :], 0)

                @block.vector
                def _(dve):
                    flag = dve.value_load(shuffled[0:1, 0:1], min_val=0, max_val=1)
                    with dve.If(flag != 0):
                        def count_step(k, first):
                            done = [0]

                            def link(ins):
                                done[0] += 1
                                ins.then_inc(chain, 1)
                                dve.wait_ge(chain, k * LINKS + done[0])
                            here = dst_i[:, ds(k, 1)]
                            dve.wait_ge(row_in, k * 16 + 16)
                            nc.vector.tensor_tensor(same_t, row, here.to_broadcast([P, P]), ALU.is_equal).then_inc(row_used, 1)
                            dve.wait_ge(row_used, k + 1)
                            link(nc.vector.tensor_tensor(prior, same_t, before[:, :], ALU.mult))
                            link(nc.vector.tensor_reduce(n_prior, prior, AX.X, ALU.add))
                            link(nc.vector.tensor_reduce(n_same, same_t, AX.X, ALU.add))
                            link(nc.vector.tensor_scalar(gap, here, -1.0, dump[:, 0:1], ALU.mult, ALU.add))
                            link(nc.vector.scalar_tensor_tensor(out=gap, in0=n_prior, scalar=0.0, in1=gap, op0=ALU.is_gt,
                                                                op1=ALU.mult))
                            dve.wait_ge(cur_in, k * 16 + 16)
                            nc.vector.tensor_tensor(target, gap, here, ALU.add)
                            link(nc.vector.tensor_tensor(rank[:, ds(k, 1)], met, n_prior, ALU.add))
                            link(nc.vector.tensor_tensor(count, met, n_same, ALU.add))
                            nc.vector.tensor_copy(n_same, count).then_inc(made, 1)
                        steps(dve, count_step)
                        dve.wait_ge(totals, 1)
                        nc.vector.tensor_copy(tot[:, :], PS[1][:, 0:NT]).then_inc(row_used, 1)
                        dve.wait_ge(row_used, KT + 1)
                        nc.vector.tensor_tensor_scan(tmp[:, :], ones[:, 0:NT], tot[:, :], 0.0, ALU.mult, ALU.add).then_inc(row_used, 1)
                        dve.wait_ge(row_used, KT + 2)
                        nc.vector.tensor_tensor(tmp[:, :], tmp[:, :], tot[:, :], ALU.subtract).then_inc(row_used, 1)
                        dve.wait_ge(row_used, KT + 3)
                        nc.vector.tensor_tensor(tmp[:, :], tmp[:, :], PS[0][:, 0:NT], ALU.add).then_inc(pre, 1)
                        dve.wait_ge(pre, 1)
                        nc.vector.tensor_tensor(tmp[:, :], tmp[:, :], deg[:, :], ALU.subtract).then_inc(pre, 1)

                        def place_step(k, first):
                            dve.wait_ge(cur2, k * 16 + 16)
                            if not first:
                                for a in range(4):
                                    dve.wait_ge(moved[a], k * 16)
                            nc.vector.tensor_tensor(place, begin, rank[:, ds(k, 1)], ALU.add).then_inc(made2, 1)
                        steps(dve, place_step)
                    with dve.Else():
                        nc.vector.memset(tot[:, :], 0.0)

                @block.tensor
                def _(pe):
                    flag = pe.value_load(shuffled[0:1, 0:1], min_val=0, max_val=1)
                    with pe.If(flag != 0):
                        pe.wait_ge(table_in, 16)
                        nc.tensor.matmul(PS[0][:, 0:NT], upto[:, :], deg[:, :], start=True, stop=True)
                        nc.tensor.matmul(PS[1][:, 0:NT], ones[:, :], deg[:, :], start=True, stop=True).then_inc(totals, 1)
                    with pe.Else():
                        nc.tensor.matmul(PS[0][:, 0:1], ones[:, :], ones[:, 0:1], start=True, stop=True)

        def edge_lists():
            preset, near, wide_done, split, first_in = (sem(f"l_{n}") for n in ("preset", "near", "wide", "split", "first"))
            part_i = rbuf[1][:, 0:KT].bitcast(i32)
            srt_bf = xt[:, KT:2 * KT].bitcast(bf16).rearrange("p (a k) -> p a k", a=2)
            block = nc.Block()
            with block:
                @block.gpsimd
                def _(pool):
                    nc.gpsimd.memset(near_dst[:, :], -1).then_inc(preset, 1)

                @block.sync
                def _(sp):
                    sp.wait_ge(preset, 1)
                    sp.dma_start(near_dst[1:P, 0:1], dst_i[0:P - 1, KT - 1:KT]).then_inc(near, 16)
                    sp.dma_start(near_dst[0:P - 1, 1:2], dst_i[1:P, 0:1]).then_inc(near, 16)
                    sp.wait_ge(split, 2)
                    sp.dma_start(src_split.rearrange("a (p k) -> p a k", p=P), srt_bf).then_inc(wide_done, 16)
                    sp.dma_start(keys[EP:EP + 4 * P, :].rearrange("(p a) b -> p (a b)", p=P), minus[:, :]).then_inc(wide_done, 16)
                    sp.wait_ge(split, 3)
                    sp.dma_start(keys[0:EP, :].rearrange("(p k) b -> p (k b)", p=P), gbuf[0][:, 0:2 * KT]).then_inc(wide_done, 16)
                    sp.wait_ge(wide_done, 48)

                @block.vector
                def _(dve):
                    for a, mask in enumerate((~127, 127)):
                        ch.link(nc.vector.tensor_scalar(part_i, srt_i, mask, None, ALU.bitwise_and))
                        ch.link(nc.vector.tensor_copy(srt_bf[:, a, :], part_i))
                    nc.vector.tensor_scalar(row_idx[:, :], src_i[:, :], float(RELS), None, ALU.mult).then_inc(split, 2)
                    dve.wait_ge(split, 2)
                    nc.vector.tensor_tensor(same[:, 1:KT], dst_i[:, 1:KT], dst_i[:, 0:KT - 1], ALU.is_equal)
                    nc.vector.tensor_tensor(row_idx[:, :], row_idx[:, :], typ_i, ALU.add)
                    nc.vector.memset(same[:, 0:1], 0.0)
                    ch.link(nc.vector.tensor_scalar(part_i, dst_i, 7, None, ALU.logical_shift_right))
                    ch.link(nc.vector.tensor_copy(dst_tile[:, :], part_i))
                    ch.link(nc.vector.tensor_scalar(part_i, dst_i, P - 1, None, ALU.bitwise_and))
                    ch.link(nc.vector.tensor_scalar(place_off, part_i, -1.0, 0.5, ALU.mult, ALU.add))
                    for a, (shift, mask) in enumerate(((8, 31), (3, 31))):
                        ch.link(nc.vector.tensor_scalar(part_i, dst_i, shift, mask, ALU.logical_shift_right, ALU.bitwise_and))
                        ch.link(nc.vector.tensor_copy(win_hl[:, a, :], part_i))
                    pair = gbuf[0][:, 0:2 * KT].rearrange("p (k b) -> p k b", b=2)
                    ch.link(nc.vector.tensor_scalar(part_i, src_i[:, :], 7, None, ALU.logical_shift_right))
                    ch.link(nc.vector.scalar_tensor_tensor(out=pair[:, :, 0], in0=dst_i, scalar=float(NT), in1=part_i,
                                                           op0=ALU.mult, op1=ALU.add))
                    ch.link(nc.vector.tensor_scalar(part_i, src_i[:, :], P - 1, None, ALU.bitwise_and))
                    nc.vector.tensor_copy(pair[:, :, 1], part_i).then_inc(split, 1)
                    dve.wait_ge(split, 3)
                    nc.vector.tensor_copy(last_dst[:, :], dst_i[:, KT - 1:KT])
                    nc.vector.tensor_copy(first_dst[:, :], dst_i[:, 0:1])
                    dve.wait_ge(near, 32)
                    nc.vector.tensor_tensor(comes_in[:, :], near_dst[:, 0:1], dst_i[:, 0:1], ALU.is_equal)
                    nc.vector.tensor_tensor(goes_out[:, :], near_dst[:, 1:2], dst_i[:, KT - 1:KT], ALU.is_equal)

        def pe_transpose(pe, rows3, banks, ps_sem, sb_sem):
            for g, tiles in enumerate(TILE_GROUPS):
                if g >= 2:
                    pe.wait_ge(sb_sem, g - 1)
                for j, t in enumerate(tiles):
                    ins = nc.tensor.transpose(banks[g % 2][0:F, j * P:(j + 1) * P], rows3[:, t, :], ident[:, :])
                ins.then_inc(ps_sem, 1)

        def act_untranspose(act, banks, ps_sem, sb_sem, done=0):
            for g, tiles in enumerate(TILE_GROUPS):
                act.wait_ge(ps_sem, done + g + 1)
                n = len(tiles) * P
                nc.scalar.copy(xt[0:F, g * GR * P:g * GR * P + n], banks[g % 2][0:F, 0:n]).then_inc(sb_sem, 1)

        def relation_table():
            tr_ps, tr_sb, mm, half_v, half_s = (sem(n) for n in ("rel_tr_ps", "rel_tr_sb", "rel_mm", "rel_v", "rel_s"))
            put = [sem(f"rel_put{u}") for u in range(2)]
            block = nc.Block()
            with block:
                @block.tensor
                def _(pe):
                    pe_transpose(pe, X, PS[0:2], tr_ps, tr_sb)
                    for t in range(NT):
                        pe.wait_ge(tr_sb, t // GR + 1)
                        if t >= 2:
                            pe.wait_ge(half_v, t - 1)
                            pe.wait_ge(half_s, t - 1)
                        for h in range(2):
                            ins = nc.tensor.matmul(PS[2 + 2 * (t % 2) + h][:, :], xt[0:F, t * P:(t + 1) * P],
                                                   cross[0:F, h * 512:(h + 1) * 512], start=True, stop=True)
                        ins.then_inc(mm, 1)

                @block.scalar
                def _(act):
                    act_untranspose(act, PS[0:2], tr_ps, tr_sb)
                    for t in range(NT):
                        act.wait_ge(mm, t + 1)
                        if t >= 2:
                            act.wait_ge(put[t % 2], 16 * (t // 2))
                        nc.scalar.copy(gbuf[t % 2][:, 512:1024], PS[3 + 2 * (t % 2)][:, :]).then_inc(half_s, 1)

                @block.vector
                def _(dve):
                    for t in range(NT):
                        dve.wait_ge(mm, t + 1)
                        if t >= 2:
                            dve.wait_ge(put[t % 2], 16 * (t // 2))
                        nc.vector.tensor_copy(gbuf[t % 2][:, 0:512], PS[2 + 2 * (t % 2)][:, :]).then_inc(half_v, 1)

                @block.sync
                def _(sp):
                    for t in range(NT):
                        sp.wait_ge(half_v, t + 1)
                        sp.wait_ge(half_s, t + 1)
                        sp.dma_start(rel_table[t * P * RELS:(t + 1) * P * RELS, :].rearrange("(p r) f -> p (r f)", r=RELS),
                                     gbuf[t % 2][:, 0:RELS * F]).then_inc(put[t % 2], 16)
                    for u in range(2):
                        sp.wait_ge(put[u], 16 * ((NT + 1 - u) // 2))

        def only_if(eng, flag, body):
            if flag is None:
                body()
                return
            value = eng.value_load(flag[0:1, 0:1], min_val=0, max_val=1)
            with eng.If(value != 0):
                body()
            with eng.Else():
                eng.wait_ge(begun, 1)

        idx_ready, gathered, scanned, stored = (
            [sem(f"{n}{u}") for u in range(2)] for n in ("idx_ready", "gathered", "scanned", "stored"))

        def gather_pass(l, table, index, flag=None):
            past = l * (NCH // 2)
            block = nc.Block()
            with block:
                @block.gpsimd
                def _(pool):
                    def chunk(i, u, c, first):
                        if not first:
                            pool.wait_ge(gathered[u], (i + past) * (16 * CH))
                            pool.wait_ge(scanned[u], i + past)
                        nc.gpsimd.tensor_copy(get_rows[:, u, :], index[:, ds(c * CH, CH)]).then_inc(idx_ready[u], 1)
                        wait_counts(pool, (idx_ready[u], i + (past + 1)))
                        for k in range(CH):
                            nc.gpsimd.indirect_dma_start(G[u][:, k, :], None, table, rows(get_rows[:, u, k:k + 1]))\
                                .then_inc(gathered[u], 16)
                    only_if(pool, flag, lambda: by_pairs(pool, NCH, chunk))
                    if l == 0:
                        nc.gpsimd.iota(cross[:, :], pattern=[[1, NP]], base=0, channel_multiplier=0,
                                       allow_small_or_imprecise_dtypes=True).then_inc(counted, 1)

                @block.vector
                def _(dve):
                    def chunk(i, u, c, first):
                        if l == 0:
                            dve_counts(dve, i, u, c, first)
                        dve.wait_ge(gathered[u], (i + (past + 1)) * (16 * CH))
                        if not first:
                            dve.wait_ge(stored[u], (i + past) * 16)
                        if u == 1:
                            dve.wait_ge(scanned[0], i + (past + 1))
                        elif not first:
                            dve.wait_ge(scanned[1], i + past)
                        for f in range(F):
                            start = 0.0 if first and u == 0 else R[1 - u][:, CH - 1, f:f + 1]
                            ins = nc.vector.tensor_tensor_scan(R[u][:, :, f], same[:, ds(c * CH, CH)], G[u][:, :, f],
                                                               start, ALU.mult, ALU.add)
                        ins.then_inc(scanned[u], 1)
                    if l == 0:
                        dve_windows(dve)
                    only_if(dve, flag, lambda: by_pairs(dve, NCH, chunk))

                @block.sync
                def _(sp):
                    def chunk(i, u, c, first):
                        if l == 0:
                            sp_keys(sp, i, u, c, first)
                        wait_counts(sp, (scanned[u], i + (past + 1)))
                        sp.dma_start(sums[l][:, ds(c * CH, CH), :], R[u]).then_inc(stored[u], 16)

                    def body():
                        by_pairs(sp, NCH, chunk)
                        for u in range(2):
                            sp.wait_ge(stored[u], 16 * (past + NCH // 2))
                    if l == 0:
                        sp_windows(sp)
                    only_if(sp, flag, body)

                if l == 0:
                    @block.scalar
                    def _(act):
                        wide = zeros[:, :].rearrange("p (o n) -> p o n", o=1)
                        per = EP // P // NCH * H // 512
                        for u in range(2):
                            act.sem_inc(counts_out[u], 16)
                        for _ in range(4):
                            act.sem_inc(win_taken, 1)

                        def chunk(i, u, c, first):
                            act.dma_start(
                                q_starts[ds(c * (CH * P), CH * P), :].rearrange("(p a b) h -> p a (b h)", p=P, b=4),
                                wide.to_broadcast([P, per, 512])).then_inc(zeroed, 16)
                            if first:
                                for s in range(NH):
                                    act_degrees(act, c, u, s, True)
                                act.wait_ge(gathered[u], 16 * CH)
                            else:
                                act_counts(act, i, u, c)
                        for j in range(GR):
                            act.dma_start(agg_table[j].rearrange("(p a) h -> p a h", p=P),
                                          zeros[:, 0:H].rearrange("p (o n) -> p o n", o=1).to_broadcast([P, (NP + P) // P, H]))\
                                .then_inc(zeroed, 16)
                        act.wait_ge(win_sum, 1)
                        by_pairs(act, NCH, chunk)
                        act.wait_ge(zeroed, 16 * (NCH + GR))
                        for u in range(2):
                            act.wait_ge(counts_out[u], 16 * (BT // 2 + 1))

                    @block.tensor
                    def _(pe):
                        for _ in range(4):
                            pe.sem_inc(win_used, 1)
                        pe_windows(pe)
                        nc.tensor.matmul(PS[7][:, 0:NT], zero_bf[:, :], zero_bf[:, 0:NT], start=True, stop=False)

                        def chunk(i, u, c, first):
                            if first:
                                for s in range(NH):
                                    pe_degrees(pe, c, u, s)
                            else:
                                pe_counts(pe, i, u, c)
                        by_pairs(pe, NCH, chunk)
                        nc.tensor.matmul(PS[7][:, 0:NT], zero_bf[:, :], zero_bf[:, 0:NT], start=False, stop=True)

        counted = sem("counted")
        hot_ready, sign_ready, hot_used, zeroed = (sem(n) for n in ("hot_ready", "sign_ready", "hot_used", "zeroed"))
        wh_ready, wh_used, win_sum, win_sb, win_pre, win_made, win_there = (
            sem(n) for n in ("wh_ready", "wh_used", "win_sum", "win_sb", "win_pre", "win_made", "win_there"))
        keys_in = [sem(f"keys_in{q}") for q in range(4)]
        keys_used, win_ready, win_used, win_taken, rel_made = (
            sem(n) for n in ("keys_used", "win_ready", "win_used", "win_taken", "rel_made"))
        counts_out = [sem(f"counts_out{u}") for u in range(2)]
        hot = [xt[:, u * 1024:(u + 1) * 1024].bitcast(bf16) for u in range(2)]
        W0 = 2048
        key_hot = [xt[:, W0 + b * (WJ * WC // 2):W0 + (b + 1) * (WJ * WC // 2)].bitcast(bf16).rearrange("p (j n) -> p j n", j=WJ)
                   for b in range(4)]
        W1 = W0 + 4 * (WJ * WC // 2)
        place_hot = [xt[:, W1 + b * (WJ * P // 2):W1 + (b + 1) * (WJ * P // 2)].bitcast(bf16).rearrange("p (j n) -> p j n", j=WJ)
                     for b in range(4)]
        W2 = W1 + 4 * (WJ * P // 2)
        assert W2 + WR <= NP
        win_row = xt[0:1, W2:W2 + WR].bitcast(i32)
        tile_counts = [node[:, u * NP // 2:(u + 1) * NP // 2].bitcast(bf16) for u in range(2)]

        def batch_at(h, w):
            s, rest = divmod(h * WT + w, 4)
            return s if rest == 0 and s < NH else None

        def win_hot(b, a, n):
            at = 0 if a else WH * WB
            return hot[b][:, at:at + WH * n].rearrange("p (k e) -> p k e", e=n)

        def dve_windows(dve):
            def batch(i, u, c, first):
                if not first:
                    dve.wait_ge(wh_used, c - 1)
                for a, n in ((0, WA), (1, WB)):
                    ins = nc.vector.tensor_tensor(
                        win_hot(u, a, n),
                        win_hl[:, a, ds(c * WH, WH)].rearrange("p (k o) -> p k o", o=1).to_broadcast([P, WH, n]),
                        count_bf[:, 0:n].rearrange("p (o e) -> p o e", o=1).to_broadcast([P, WH, n]), ALU.is_equal)
                ins.then_inc(wh_ready, 1)
            by_pairs(dve, KT // WH, batch)
            size, base, both = deg[0:WB, 0:WA], tot[0:WB, 0:WA], tmp[0:WB, 0:WA]
            dve.wait_ge(win_sum, 1)
            nc.vector.tensor_copy(size, PS[6][0:WB, 0:WA]).then_inc(win_sb, 1)
            dve.wait_ge(win_sb, 1)
            nc.vector.tensor_reduce(win_most[0:WB, :], size, AX.X, ALU.max)
            dve.wait_ge(win_pre, 1)
            ch.link(nc.vector.tensor_copy(both, PS[5][0:WB, 0:WA]))
            ch.link(nc.vector.tensor_tensor_scan(base, ones[0:WB, 0:WA], both, 0.0, ALU.mult, ALU.add))
            ch.link(nc.vector.tensor_tensor(base, base, both, ALU.subtract))
            ch.link(nc.vector.tensor_tensor(base, base, PS[4][0:WB, 0:WA], ALU.add))
            nc.vector.tensor_tensor(end_row[0:WB, 0:WA], base, size, ALU.subtract).then_inc(win_made, 1)
            for _ in range(4):
                dve.sem_inc(keys_used, 1)

        def pe_windows(pe):
            nc.tensor.matmul(PS[6][0:WB, 0:WA], zero_bf[:, 0:WB], zero_bf[:, 0:WA], start=True, stop=False)

            def batch(i, u, c, first):
                pe.wait_ge(wh_ready, c + 1)
                for k in range(WH):
                    ins = nc.tensor.matmul(PS[6][0:WB, 0:WA], win_hot(u, 1, WB)[:, k, :], win_hot(u, 0, WA)[:, k, :],
                                           start=False, stop=False)
                ins.then_inc(wh_used, 1)
            by_pairs(pe, KT // WH, batch)
            nc.tensor.matmul(PS[6][0:WB, 0:WA], zero_bf[:, 0:WB], zero_bf[:, 0:WA], start=False, stop=True).then_inc(win_sum, 1)
            pe.wait_ge(win_sb, 1)
            nc.tensor.matmul(PS[4][0:WB, 0:WA], upto[0:WB, 0:WB], deg[0:WB, 0:WA], start=True, stop=True)
            nc.tensor.matmul(PS[5][0:WB, 0:WA], ones[0:WB, 0:WB], deg[0:WB, 0:WA], start=True, stop=True).then_inc(win_pre, 1)

        def sp_windows(sp):
            sp.wait_ge(win_made, 1)
            sp.dma_start(win_first.rearrange("(a b) o -> b (a o)", b=WB), end_row[0:WB, 0:WA]).then_inc(win_there, 16)
            sp.wait_ge(win_there, 16)
            sp.dma_start(win_row[:, 0:WA * WB], win_first.rearrange("n o -> o n")).then_inc(win_there, 16)
            sp.dma_start(win_row[:, WA * WB:WR], win_first[0:WR - WA * WB, :].rearrange("n o -> o n")).then_inc(win_there, 16)
            sp.wait_ge(win_there, 48)

        def sp_keys(sp, i, u, c, first):
            if first and u == 0:
                return
            for h in range(2):
                q = h if first else (2 * u + 2 + h) % 4
                t = h if first else i * 4 + (2 * u + h - 2)
                if not first:
                    wait_counts(sp, (keys_used, t + 1))
                for w0 in range(0, WT, 4):
                    regs = [sp.value_load(win_row[0:1, ds(t * WT + w, 1)], min_val=0, max_val=EP) for w in range(w0, w0 + 4)]
                    for w, at in zip(range(w0, w0 + 4), regs):
                        sp.dma_start(key_slot[:, q, w, :], keys[ds(at, WE), :].rearrange("(p j) b -> p (j b)", p=P))\
                            .then_inc(keys_in[q], 16)

        def dve_counts(dve, i, u, c, first):
            def batch(s):
                b = (u + s) % 2
                if not first or u * NH + s >= 2:
                    dve.wait_ge(hot_used, c * NH + (s - 1))
                nc.vector.tensor_tensor(
                    hot[b][:, HB * P:HB * (P + NT)].rearrange("p (k e) -> p k e", e=NT),
                    dst_tile[:, ds(c * CH + s * HB, HB)].rearrange("p (k o) -> p k o", o=1).to_broadcast([P, HB, NT]),
                    count_bf[:, 0:NT].rearrange("p (o e) -> p o e", o=1).to_broadcast([P, HB, NT]), ALU.is_equal)\
                    .then_inc(hot_ready, 1)
            if first:
                for s in range(NH):
                    batch(s)
                return
            for h in range(2):
                q = 2 * u + h
                t = i * 4 + (q - 4)
                dve.wait_ge(keys_in[q], i * (16 * WT))
                slot = key_slot[:, q, :, :].rearrange("p w (j b) -> p w j b", b=2)
                nc.vector.tensor_tensor(key_rel[:, :, :], slot[:, :, :, 0],
                                        win_base[:, :].rearrange("p (w o) -> p w o", o=1).to_broadcast([P, WT, WJ]),
                                        ALU.subtract).then_inc(rel_made, 1)
                dve.wait_ge(rel_made, t * 2 + 1)
                nc.vector.tensor_scalar(win_base[:, :], win_base[:, :], float(WT * WC), None, ALU.add).then_inc(rel_made, 1)
                for w in range(WT):
                    if batch_at(h, w) is not None:
                        batch(batch_at(h, w))
                    b = w % 4
                    dve.wait_ge(win_used, t * WT + (w + 1))
                    for j in range(WJ):
                        ins = nc.vector.tensor_scalar(place_hot[b][:, j, :], count_bf[:, :], key_slot[:, q, w, 2 * j + 1:2 * j + 2],
                                                      None, ALU.is_equal)
                        if w == WT - 1 and j == WJ - 1:
                            ins.then_inc(keys_used, 1)
                        ins = nc.vector.tensor_scalar(key_hot[b][:, j, :], lane[:, :], key_rel[:, w, j:j + 1], None, ALU.is_equal)
                    ins.then_inc(win_ready, 1)
                dve.wait_ge(win_ready, t * WT + WT)
                dve.wait_ge(rel_made, t * 2 + 2)

        def pe_degrees(pe, c, u, s):
            b = (u + s) % 2
            pe.wait_ge(hot_ready, c * NH + (s + 1))
            pe.wait_ge(sign_ready, c * NH + (s + 1))
            for k in range(HB):
                ins = nc.tensor.matmul(PS[7][:, 0:NT], hot[b][:, k * P:(k + 1) * P],
                                       hot[b][:, HB * P + k * NT:HB * P + (k + 1) * NT], start=False, stop=False)
            ins.then_inc(hot_used, 1)

        def pe_counts(pe, i, u, c):
            for h in range(2):
                t = i * 4 + (2 * u + h - 4)
                for w in range(WT):
                    if batch_at(h, w - 3) is not None:
                        pe_degrees(pe, c, u, batch_at(h, w - 3))
                    b = w % 4
                    pe.wait_ge(win_ready, t * WT + (w + 1))
                    pe.wait_ge(win_taken, t * WT + (w + 1))
                    for j in range(WJ):
                        ins = nc.tensor.matmul(PS[b][:, 0:WC], place_hot[b][:, j, :], key_hot[b][:, j, :],
                                               start=j == 0, stop=j == WJ - 1)
                    ins.then_inc(win_used, 1)

        def act_degrees(act, c, u, s, first):
            b = (u + s) % 2
            if not first or u * NH + s >= 2:
                act.wait_ge(hot_used, c * NH + (s - 1))
            for k in range(HB):
                ins = nc.scalar.activation(hot[b][:, k * P:(k + 1) * P], count_bf[:, :], ACT.Sign,
                                           bias=place_off[:, ds(c * CH + (s * HB + k), 1)])
            ins.then_inc(sign_ready, 1)

        def act_counts(act, i, u, c):
            for h in range(2):
                q = 2 * u + h
                t = i * 4 + (q - 4)
                act.wait_ge(counts_out[h], i * 32 + (16 * (u + 1) - 32))
                for w in range(WT):
                    if batch_at(h, w) is not None:
                        act_degrees(act, c, u, batch_at(h, w), False)
                    act.wait_ge(win_used, t * WT + (w + 5))
                    nc.scalar.copy(
                        tile_counts[h].rearrange("p (s d) -> p d s", d=P)[:, w * WN:(w + 1) * WN, :],
                        PS[w % 4][:, 0:WC].rearrange("p (d s) -> p d s", s=NT)).then_inc(win_taken, 1)
                wait_counts(act, (win_taken, t * WT + (WT + 4)))
                act.dma_start(counts[ds(t, 1), :, :].rearrange("o p n -> (o p) n"), tile_counts[h]).then_inc(counts_out[h], 16)

        def collect(l, flag=None):
            banks = [list(range(t, min(t + 8, NT))) for t in range(0, NT, 8)]
            block = nc.Block()
            with block:
                @block.gpsimd
                def _(pool):
                    by_edge = sums[l].rearrange("p k f -> (p k) f")

                    def body():
                        for t in range(NT):
                            nc.gpsimd.indirect_dma_start(S1[:, t, :], None, by_edge, rows(end_row[:, t:t + 1])).then_inc(fetched, 16)
                    only_if(pool, flag, body)

                @block.tensor
                def _(pe):
                    def body():
                        for b, tiles in enumerate(banks):
                            for j, t in enumerate(tiles):
                                ins = nc.tensor.matmul(PS[b][:, j * F:(j + 1) * F], cross[:, t * P:(t + 1) * P],
                                                       R[1][:, CH - 1, :], start=True, stop=True)
                        ins.then_inc(carried, 1)
                    only_if(pe, flag, body)

                @block.vector
                def _(dve):
                    def body():
                        dve.wait_ge(fetched, 16 * NT * (l + 1))
                        nc.vector.tensor_tensor(S1, S1, over_f(has), ALU.mult).then_inc(masked, 1)
                        dve.wait_ge(masked, l + 1)
                        dve.wait_ge(carried, l + 1)
                        for b, tiles in enumerate(banks):
                            part = S1[:, tiles[0]:tiles[-1] + 1, :]
                            nc.vector.tensor_tensor(part, part, PS[b][:, 0:len(tiles) * F].rearrange("p (t f) -> p t f", f=F),
                                                    ALU.add)
                    only_if(dve, flag, body)

        masked, parted, product_ps, product_sb = (sem(n) for n in ("masked", "parted", "product_ps", "product_sb"))
        tile_in = [sem(f"tile_in{s}") for s in range(4)]

        def product(l, values):
            turn = l - 1
            before_t = turn * NT
            parts = xt[:, 0:NT * PARTS * F // 2].bitcast(bf16).rearrange("p (t a f) -> p t a f", a=PARTS, f=F)
            rest = node[:, 2 * NT * F:3 * NT * F].rearrange("p (t f) -> p t f", f=F)
            bufs = [b[:, 0:NP // 2].bitcast(bf16) for b in gbuf + rbuf]

            def in_fours(eng, body):
                for s in range(4):
                    body(0, s, s, True)
                with eng.Fori(1, NT // 4) as i:
                    for s in range(4):
                        body(i, s, i * 4 + s, False)
                body(NT // 4, 0, NT - 1, False)

            def unless(eng, body):
                value = eng.value_load(irregular[0:1, 0:1], min_val=0, max_val=1)
                with eng.If(value == 0):
                    body()
                with eng.Else():
                    eng.wait_ge(begun, 1)

            block = nc.Block()
            with block:
                @block.sync
                def _(sp):
                    def tile(i, s, t, first):
                        if not first:
                            wait_counts(sp, (product_ps, t + (before_t - 3)))
                        sp.dma_start(bufs[s], counts[ds(t, 1), :, :].rearrange("o p n -> (o p) n")).then_inc(tile_in[s], 16)
                    unless(sp, lambda: in_fours(sp, tile))

                @block.tensor
                def _(pe):
                    def tile(i, s, t, first):
                        past = turn * (NT // 4 + (s == 0))
                        pe.wait_ge(tile_in[s], i * 16 + 16 * (past + 1))
                        if not first:
                            pe.wait_ge(product_sb, t + (before_t - 3))
                        for k in range(NT):
                            ins = nc.tensor.matmul(PS[s][:, 0:PARTS * F], bufs[s][:, k * P:(k + 1) * P],
                                                   parts[:, k, :, :].rearrange("p a f -> p (a f)"),
                                                   start=k == 0, stop=k == NT - 1)
                        ins.then_inc(product_ps, 1)

                    def body():
                        pe.wait_ge(parted, 5 * (turn + 1))
                        in_fours(pe, tile)
                    unless(pe, body)

                @block.vector
                def _(dve):
                    def tile(i, s, t, first):
                        dve.wait_ge(product_ps, t + (before_t + 1))
                        nc.vector.tensor_reduce(S1[:, ds(t, 1), :].rearrange("p o f -> p (o f)"),
                                                PS[s][:, 0:PARTS * F].rearrange("p (a f) -> p f a", f=F),
                                                AX.X, ALU.add).then_inc(product_sb, 1)

                    def body():
                        steps = ((parts[:, :, 0, :], values, None), (rest, values, parts[:, :, 0, :]),
                                 (parts[:, :, 1, :], rest, None), (rest, rest, parts[:, :, 1, :]), (parts[:, :, 2, :], rest, None))
                        for n, (to, of, less) in enumerate(steps):
                            if less is None:
                                ins = nc.vector.tensor_copy(to, of)
                            else:
                                ins = nc.vector.tensor_tensor(to, of, less, ALU.subtract)
                            ins.then_inc(parted, 1)
                            dve.wait_ge(parted, 5 * turn + n + 1)
                        in_fours(dve, tile)
                    unless(dve, body)

        def degrees():
            cum_sb, doubled, deg_sb, prefix, root, rooted, over, overs = (
                sem(n) for n in ("cum_sb", "doubled", "deg_sb", "prefix", "root", "rooted", "over", "overs"))
            steps = gbuf[0][:, 0:P]
            block = nc.Block()
            with block:
                @block.tensor
                def _(pe):
                    pe.wait_ge(cum_sb, 2)
                    nc.tensor.matmul(PS[3][:, 0:NT], steps, tot[:, :], start=True, stop=True).then_inc(doubled, 1)
                    pe.wait_ge(deg_sb, 1)
                    nc.tensor.matmul(PS[0][:, 0:NT], upto[:, :], deg[:, :], start=True, stop=True)
                    nc.tensor.matmul(PS[1][:, 0:NT], ones[:, :], deg[:, :], start=True, stop=True).then_inc(prefix, 1)
                    pe.wait_ge(over, 1)
                    nc.tensor.matmul(PS[2][:, 0:1], ones[:, :], mean[:, 0:1], start=True, stop=True).then_inc(overs, 1)

                @block.scalar
                def _(act):
                    act.wait_ge(root, 1)
                    nc.scalar.activation(tmp[:, :], tmp[:, :], ACT.Sqrt).then_inc(rooted, 1)

                @block.vector
                def _(dve):
                    nc.vector.tensor_tensor(steps[:, 1:P], ident[:, 1:P], ident[:, 0:P - 1], ALU.subtract)
                    nc.vector.tensor_tensor(steps[:, 0:1], ident[:, 0:1], ident[:, P - 1:P], ALU.add).then_inc(cum_sb, 1)
                    nc.vector.tensor_scalar(tot[:, :], PS[7][:, 0:NT], 0.5, None, ALU.mult).then_inc(cum_sb, 1)
                    dve.wait_ge(doubled, 1)
                    nc.vector.tensor_copy(deg[:, :], PS[3][:, 0:NT]).then_inc(deg_sb, 1)
                    dve.wait_ge(deg_sb, 1)
                    nc.vector.tensor_scalar(has[:, :], deg[:, :], 1.0, None, ALU.min)
                    ch.link(nc.vector.tensor_scalar(inv[:, :], deg[:, :], 1.0, None, ALU.max))
                    ch.link(nc.vector.reciprocal(inv[:, :], inv[:, :]))
                    nc.vector.tensor_scalar(tmp[:, :], deg[:, :], 1.0, None, ALU.add).then_inc(root, 1)
                    dve.wait_ge(rooted, 1)
                    ch.link(nc.vector.reciprocal(dinv[:, :], tmp[:, :]))
                    ch.link(nc.vector.tensor_reduce(var[:, 0:1], deg[:, :], AX.X, ALU.max))
                    ch.link(nc.vector.tensor_scalar(var[:, 0:1], var[:, 0:1], float(EXACT), None, ALU.is_gt))
                    nc.vector.scalar_tensor_tensor(out=mean[:, 0:1], in0=win_most[:, :], scalar=float(WE), in1=var[:, 0:1],
                                                   op0=ALU.is_gt, op1=ALU.max).then_inc(over, 1)
                    dve.wait_ge(overs, 1)
                    ch.link(nc.vector.tensor_scalar(irregular[:, :], PS[2][:, 0:1], 1.0, None, ALU.min))
                    dve.wait_ge(prefix, 1)
                    ch.link(nc.vector.tensor_copy(tot[:, :], PS[1][:, 0:NT]))
                    ch.link(nc.vector.tensor_tensor_scan(tmp[:, :], ones[:, 0:NT], tot[:, :], 0.0, ALU.mult, ALU.add))
                    ch.link(nc.vector.tensor_tensor(tmp[:, :], tmp[:, :], tot[:, :], ALU.subtract))
                    ch.link(nc.vector.tensor_tensor(tmp[:, :], tmp[:, :], PS[0][:, 0:NT], ALU.add))
                    nc.vector.tensor_scalar(end_row[:, :], tmp[:, :], -1.0, 0.0, ALU.add, ALU.max)
                    ch.link(nc.vector.tensor_tensor(tmp[:, :], tmp[:, :], deg[:, :], ALU.subtract))
                    ch.link(nc.vector.tensor_tensor(tot[:, :], dump[:, 1:1 + NT], tmp[:, :], ALU.subtract))
                    ch.link(nc.vector.tensor_scalar(mean[:, :], has[:, :], -1.0, 1.0, ALU.mult, ALU.add))
                    ch.link(nc.vector.tensor_tensor(tot[:, :], tot[:, :], mean[:, :], ALU.mult))
                    nc.vector.tensor_tensor(start_row[:, :], tmp[:, :], tot[:, :], ALU.add)
                    dve.wait_ge(counted, 1)
                    nc.vector.tensor_scalar(cross[:, :], cross[:, :], last_dst[:, 0:1], goes_out[:, 0:1],
                                            ALU.is_equal, ALU.mult)

        def layer_norm(dve, Y, scratch, n):
            ch.link(nc.vector.tensor_reduce(mean[:, :], Y, AX.X, ALU.add))
            ch.link(nc.vector.tensor_scalar(mean[:, :], mean[:, :], 1.0 / F, None, ALU.mult))
            ch.link(nc.vector.tensor_tensor(Y, Y, over_f(mean), ALU.subtract))
            ch.link(nc.vector.tensor_tensor(scratch, Y, Y, ALU.mult))
            ch.link(nc.vector.tensor_reduce(var[:, :], scratch, AX.X, ALU.add))
            nc.vector.tensor_scalar(var[:, :], var[:, :], 1.0 / F, EPS, ALU.mult, ALU.add).then_inc(var_made, 1)
            dve.wait_ge(root_made, n)
            ch.link(nc.vector.reciprocal(var[:, :], var[:, :]))
            ch.link(nc.vector.tensor_tensor(Y, Y, over_f(var), ALU.mult))

        def node_stage(l):
            turn = l - 2
            done = max(turn, 0) * len(TILE_GROUPS)
            norm = min(l, 2) + 1
            banks = [list(range(t, min(t + 8, NT))) for t in range(0, NT, 8)]
            block = nc.Block()

            def bank3(b, n):
                return PS[b][:, 0:n * F].rearrange("p (t f) -> p t f", f=F)

            with block:
                @block.tensor
                def _(pe):
                    if l >= 2:
                        pe.wait_ge(u_made, turn + 1)
                        for g, tiles in enumerate(TILE_GROUPS):
                            if g >= 1:
                                pe.wait_ge(nd_tr_sb, done + g)
                            for j, t in enumerate(tiles):
                                ins = nc.tensor.transpose(PS[7][0:F, j * P:(j + 1) * P], S1[:, t, :], ident[:, :])
                            ins.then_inc(nd_tr_ps, 1)
                        pe.wait_ge(nd_tr_sb, done + len(TILE_GROUPS))
                        for b, tiles in enumerate(banks):
                            for j, t in enumerate(tiles):
                                ins = nc.tensor.matmul(PS[b][:, j * F:(j + 1) * F], xt[0:F, t * P:(t + 1) * P],
                                                       gcn_s[:, l - 2, :], start=True, stop=True)
                        ins.then_inc(mixed, 1)
                    else:
                        pe.wait_ge(begun, 1)

                @block.scalar
                def _(act):
                    if l >= 2:
                        act_untranspose(act, [PS[7], PS[7]], nd_tr_ps, nd_tr_sb, done)
                    if l != 2:
                        act.wait_ge(var_made, norm)
                        nc.scalar.activation(var[:, :], var[:, :], ACT.Sqrt).then_inc(root_made, 1)

                @block.vector
                def _(dve):
                    if l == 0:
                        ch.link(nc.vector.tensor_tensor(X[:, :, :], X[:, :, :], S1, ALU.add))
                    elif l == 1:
                        ch.link(nc.vector.tensor_tensor(S2, X[:, :, :], over_f(deg), ALU.mult))
                        ch.link(nc.vector.tensor_tensor(S1, S1, S2, ALU.add))
                        ch.link(nc.vector.tensor_tensor(S1, S1, over_f(inv), ALU.mult))
                        ch.link(nc.vector.tensor_tensor(S1, S1, X[:, :, :], ALU.add))
                        ch.link(nc.vector.tensor_tensor(X[:, :, :], S1, X[:, :, :], ALU.add))
                    else:
                        ch.link(nc.vector.tensor_tensor(S1, S1, S2, ALU.add))
                        nc.vector.tensor_tensor(S1, S1, over_f(dinv), ALU.mult).then_inc(u_made, 1)
                        dve.wait_ge(mixed, turn + 1)
                        for b, tiles in enumerate(banks):
                            bias = bias_s[:, l - 2:l - 1, :].to_broadcast([P, len(tiles), F])
                            ins = nc.vector.tensor_tensor(S3[:, tiles[0]:tiles[-1] + 1, :], bank3(b, len(tiles)), bias, ALU.add)
                        ch.link(ins)
                        ch.link(nc.vector.tensor_scalar(S3, S3, 0.0, None, ALU.max))
                        if l == 3:
                            ch.link(nc.vector.tensor_tensor(X[:, :, :], X[:, :, :], S3, ALU.add))
                    if l != 2:
                        layer_norm(dve, X[:, :, :], S1, norm)
                    if l in (1, 2):
                        ch.link(nc.vector.tensor_tensor(S2, X[:, :, :] if l == 1 else S3, over_f(dinv), ALU.mult))
                    nc.vector.tensor_copy(tot[:, 0:1], mean[:, 0:1]).then_inc(ready, 1)

                if l < 3:
                    @block.sync
                    def _(sp):
                        def body():
                            sp.wait_ge(ready, l + 1)
                            sp.dma_start(node_table[l].rearrange("(t p) f -> p t f", p=P), X[:, :, :] if l == 0 else S2)\
                                .then_inc(tabled, 16)
                            sp.wait_ge(tabled, 16 * (l + 1))
                        only_if(sp, irregular, body)

        def edge_tables():
            tr_ps, tr_sb, mm, got_p, got_q, stored, put, first = (
                sem(n) for n in ("et_tr_ps", "et_tr_sb", "et_mm", "et_p", "et_q", "et_stored", "et_put", "et_first"))
            Pn = node[:, 0:NT * H].rearrange("p (t h) -> p t h", h=H)
            Qn = cross[:, :].rearrange("p (t h) -> p t h", h=H)
            block = nc.Block()
            with block:
                @block.tensor
                def _(pe):
                    pe_transpose(pe, X, PS[0:2], tr_ps, tr_sb)
                    for g, tiles in enumerate(TILE_GROUPS):
                        pe.wait_ge(tr_sb, g + 1)
                        if g >= 2:
                            pe.wait_ge(got_p, g - 1)
                            pe.wait_ge(got_q, g - 1)
                        for a in range(2):
                            for j, t in enumerate(tiles):
                                ins = nc.tensor.matmul(PS[2 + 2 * a + g % 2][:, j * H:(j + 1) * H], xt[0:F, t * P:(t + 1) * P],
                                                       ew1_s[:, a * H:(a + 1) * H], start=True, stop=True)
                        ins.then_inc(mm, 1)

                def bank(a, g, tiles):
                    return PS[2 + 2 * a + g % 2][:, 0:len(tiles) * H].rearrange("p (t h) -> p t h", h=H)

                @block.scalar
                def _(act):
                    act_untranspose(act, PS[0:2], tr_ps, tr_sb)
                    for g, tiles in enumerate(TILE_GROUPS):
                        act.wait_ge(mm, g + 1)
                        nc.scalar.copy(Qn[:, tiles[0]:tiles[-1] + 1, :], bank(1, g, tiles)).then_inc(got_q, 1)

                @block.vector
                def _(dve):
                    for g, tiles in enumerate(TILE_GROUPS):
                        dve.wait_ge(mm, g + 1)
                        nc.vector.tensor_copy(Pn[:, tiles[0]:tiles[-1] + 1, :], bank(0, g, tiles)).then_inc(got_p, 1)
                    nc.vector.tensor_copy(same[:, 0:1], comes_in[:, :])

                @block.sync
                def _(sp):
                    sp.wait_ge(got_p, len(TILE_GROUPS))
                    sp.wait_ge(got_q, len(TILE_GROUPS))
                    sp.dma_start(p_table.rearrange("(t p) h -> p t h", p=P), Pn).then_inc(stored, 16)
                    sp.dma_start(q_table.rearrange("(t p) h -> p t h", p=P), Qn).then_inc(stored, 16)
                    sp.wait_ge(stored, 32)

                @block.gpsimd
                def _(pool):
                    pool.wait_ge(got_q, len(TILE_GROUPS))
                    for t in range(NT):
                        nc.gpsimd.indirect_dma_start(q_starts, rows(start_row[:, t:t + 1]), Qn[:, t, :], None).then_inc(put, 16)
                    pool.wait_ge(stored, 32)
                    nc.gpsimd.indirect_dma_start(q_in[:, :], None, q_table, rows(first_dst[:, 0:1])).then_inc(first, 16)
                    pool.wait_ge(put, 16 * NT)
                    pool.wait_ge(first, 16)

        def edge_mlp():
            got, attr_in, rows_in, q_landed, idx_ready = (
                [sem(f"{n}{u}") for u in range(2)] for n in ("e_got", "e_attr", "e_rows", "e_q", "e_idx"))
            q_done, added, z1_ps, eq_ps, h1_sb, eq_sb, z2_ps, z2_sb, m_sb, s_ps, s_sb = (
                sem(f"e_{n}") for n in ("q_done", "added", "z1_ps", "eq_ps", "h1_sb", "eq_sb", "z2_ps", "z2_sb", "m_sb",
                                        "s_ps", "s_sb"))
            put = [sem(f"e_put{j}") for j in range(GR)]
            placed, e_chain = sem("e_placed"), sem("e_chain")
            LINKS, LAG, Q_FROM = 4, 4, 2
            prior, n_prior, gap = xt[:, 4096:4608], xt[:, 4608:4608 + GR], xt[:, 4616:4616 + GR]
            attr_s = [cross[0:1 + A, 0:CE * P], node[0:1 + A, 0:CE * P]]
            src_rows = [node[0:2, CE * P + u * CE * P // 2:CE * P + (u + 1) * CE * P // 2].bitcast(bf16) for u in range(2)]
            h1, z2b, msg, equal = ([xt[:, 1024 * a + 512 * b:1024 * a + 512 * (b + 1)] for b in range(2)] for a in range(4))
            total = [node[:, 2 * CE * P + 512 * b:2 * CE * P + 512 * (b + 1)] for b in range(4)]
            q_rows = q_starts[0:EP, :].rearrange("(p k) h -> p k h", p=P)

            def slot(u, c, first, s, steps):
                for d, f in steps:
                    least = (0 if first else 2 * NG) + u * NG + s - d
                    if s >= d:
                        f(c, u, s - d, least % 2, least)
                    elif least >= 0:
                        f(c - 1, 1 - u, s - d + NG, least % 2, least)

            def slots(eng, head, *steps):
                def chunk(i, u, c, first):
                    head(i, u, c)
                    for s in range(NG):
                        slot(u, c, first, s, steps)
                by_pairs(eng, NCE, chunk)
                rest(steps)

            def rest(steps):
                for s in range(NG, NG + max(d for d, _ in steps)):
                    slot(1, NCE - 1, False, s, [(d, f) for d, f in steps if s - d < NG])

            block = nc.Block()
            with block:
                @block.sync
                def _(sp):
                    def chunk(i, u, c, first):
                        if not first:
                            wait_counts(sp, (added, (c - 1) * NG), (q_done, c))
                        sp.dma_start(QE[u], q_rows[:, ds(c * CE, CE), :]).then_inc(q_landed[u], 16)
                        if not first:
                            wait_counts(sp, (z1_ps, (c - 1) * NG), (eq_ps, (c - 1) * NG))
                        sp.dma_start(attr_s[u], edge_attr[:, ds(c * (CE * P), CE * P)]).then_inc(attr_in[u], 16)
                        sp.dma_start(src_rows[u], src_split[:, ds(c * (CE * P), CE * P)]).then_inc(rows_in[u], 16)
                    sp.wait_ge(attr_there, 16)
                    by_pairs(sp, NCE, chunk)

                @block.gpsimd
                def _(pool):
                    def fetch(i, u, c, first, g):
                        if g == 0:
                            if not first:
                                pool.wait_ge(got[u], i * (16 * CE))
                            nc.gpsimd.tensor_copy(get_rows[:, u, 0:CE], src_i[:, ds(c * CE, CE)]).then_inc(idx_ready[u], 1)
                            wait_counts(pool, (idx_ready[u], i + 1))
                        if not first:
                            wait_counts(pool, (z1_ps, (c - 2) * NG + (g + 1)))
                        for k in range(g * GR, (g + 1) * GR):
                            nc.gpsimd.indirect_dma_start(GE[u][:, k, :], None, p_table, rows(get_rows[:, u, k:k + 1]))\
                                .then_inc(got[u], 16)

                    def add_up(u, c, g, first):
                        wait_counts(pool, (s_sb, c * NG + (g + 1)), (placed, c * NG + (g + 1)))
                        for j in range(GR):
                            if not first:
                                wait_counts(pool, (put[j], c * (16 * NG) + 16 * g))
                            nc.gpsimd.indirect_dma_start(
                                agg_table[j], rows(put_rows[:, u, g * GR + j:g * GR + j + 1]),
                                total[g % 4][:, j * H:(j + 1) * H], None, compute_op=ALU.add).then_inc(put[j], 16)

                    def turn(i, u, c, first):
                        for g in range(NG):
                            fetch(i, u, c, first, g)
                            if g >= LAG and not (first and u == 0):
                                add_up(1 - u, c - 1, g - LAG, first and g == LAG)
                            elif g < LAG and not first:
                                add_up(u, c - 2, g + NG - LAG, False)
                    by_pairs(pool, NCE, turn)
                    for n in range((NCE - 1) * NG - LAG, NCE * NG):
                        add_up(n // NG % 2, n // NG, n % NG, False)
                    for j in range(GR):
                        pool.wait_ge(put[j], 16 * NG * NCE)

                @block.vector
                def _(dve):
                    def extend(u, c, low, high, start):
                        for h in range(low, high):
                            ins = nc.vector.tensor_tensor_scan(QE[u][:, :, h], same[:, ds(c * CE, CE)], QE[u][:, :, h],
                                                               start[:, h:h + 1], ALU.mult, ALU.add)
                        if high == H:
                            ins.then_inc(q_done, 1)

                    def add(c, u, g, b, least):
                        part = GE[u][:, g * GR:(g + 1) * GR, :]
                        nc.vector.tensor_tensor(part, part, QE[u][:, g * GR:(g + 1) * GR, :], ALU.add).then_inc(added, 1)

                    def compare(c, u, g, b, least):
                        dve.wait_ge(eq_ps, c * NG + (g + 1))
                        if least >= 2:
                            dve.wait_ge(s_ps, c * NG + (g - 1))
                        nc.vector.tensor_tensor(
                            equal[b].rearrange("p (j e) -> p j e", e=P), PS[2 + b][:, :].rearrange("p (j e) -> p j e", e=P),
                            src_i[:, ds(c * CE + g * GR, GR)].rearrange("p (j o) -> p j o", o=1).to_broadcast([P, GR, P]),
                            ALU.is_equal).then_inc(eq_sb, 1)

                    def place(c, u, g, b, least):
                        n = c * NG + g
                        here = src_i[:, ds(c * CE + g * GR, GR)]
                        dve.wait_ge(eq_sb, n + 1)
                        nc.vector.tensor_tensor(
                            prior.rearrange("p (j e) -> p j e", e=P), equal[b].rearrange("p (j e) -> p j e", e=P),
                            before[:, :].rearrange("p (o e) -> p o e", o=1).to_broadcast([P, GR, P]),
                            ALU.mult).then_inc(e_chain, 1)
                        if least:
                            dve.wait_ge(placed, n)
                        nc.vector.tensor_scalar(gap, here, -1.0, dump[:, 0:1], ALU.mult, ALU.add).then_inc(e_chain, 1)
                        dve.wait_ge(e_chain, n * LINKS + 2)
                        nc.vector.tensor_reduce(n_prior, prior.rearrange("p (j e) -> p j e", e=P), AX.X, ALU.add)\
                            .then_inc(e_chain, 1)
                        dve.wait_ge(e_chain, n * LINKS + 3)
                        nc.vector.scalar_tensor_tensor(out=gap, in0=n_prior, scalar=0.0, in1=gap, op0=ALU.is_gt,
                                                       op1=ALU.mult).then_inc(e_chain, 1)
                        dve.wait_ge(e_chain, n * LINKS + 4)
                        if g == 0 and least >= 2 * NG:
                            for j in range(GR):
                                dve.wait_ge(put[j], (c - 1) * (16 * NG))
                        nc.vector.tensor_tensor(put_rows[:, u, g * GR:(g + 1) * GR], gap, here, ALU.add).then_inc(placed, 1)

                    def bias(c, u, g, b, least):
                        dve.wait_ge(z2_ps, c * NG + (g + 1))
                        if least >= 2:
                            dve.wait_ge(m_sb, c * NG + (g - 1))
                        nc.vector.tensor_tensor(
                            z2b[b].rearrange("p (j h) -> p j h", h=H), PS[4 + b][:, :].rearrange("p (j h) -> p j h", h=H),
                            eb2_s[:, :].rearrange("p (o h) -> p o h", o=1).to_broadcast([P, GR, H]), ALU.add)\
                            .then_inc(z2_sb, 1)

                    steps = (0, add), (2, bias), (2, compare), (2, place)

                    def chunk(i, u, c, first, last=False):
                        dve.wait_ge(q_done, c + 1)
                        dve.wait_ge(got[u], (i + 1) * (16 * CE))
                        for s in range(NG):
                            slot(u, c, first, s, steps)
                            if s >= Q_FROM and not last:
                                if s == Q_FROM:
                                    dve.wait_ge(q_landed[1 - u], (i + 1 + u) * 16)
                                low, high = ((s - Q_FROM + k) * H // (NG - Q_FROM) for k in range(2))
                                extend(1 - u, c + 1, low, high, QE[u][:, CE - 1, :])

                    dve.wait_ge(q_landed[0], 16)
                    extend(0, 0, 0, H, q_in)
                    for u in range(2):
                        chunk(0, u, u, True)
                    with dve.Fori(1, NCE // 2 - 1) as i:
                        for u in range(2):
                            chunk(i, u, i * 2 + u, False)
                    for u in range(2):
                        chunk(NCE // 2 - 1, u, NCE - 2 + u, False, last=u == 1)
                    rest(steps)

                @block.tensor
                def _(pe):
                    def head(i, u, c):
                        pe.wait_ge(attr_in[u], (i + 1) * 16)

                    def layer1(c, u, g, b, least):
                        if least >= 2:
                            pe.wait_ge(h1_sb, c * NG + (g - 1))
                        nc.tensor.matmul(PS[b][:, :], we_s[:, :], attr_s[u][:, g * GR * P:(g + 1) * GR * P],
                                         start=True, stop=False)
                        pe.wait_ge(added, c * NG + (g + 1))
                        for j in range(GR):
                            ins = nc.tensor.matmul(PS[b][:, j * P:(j + 1) * P], GE[u][:, g * GR + j, :], ident[:, :],
                                                   start=False, stop=j == GR - 1)
                        ins.then_inc(z1_ps, 1)

                    def sources(c, u, g, b, least):
                        if g == 0:
                            pe.wait_ge(rows_in[u], (c - u) * 8 + 16)
                        if least >= 2:
                            pe.wait_ge(eq_sb, c * NG + (g - 1))
                        nc.tensor.matmul(PS[2 + b][:, :], ones_bf[:, :], src_rows[u][:, g * GR * P:(g + 1) * GR * P],
                                         start=True, stop=True).then_inc(eq_ps, 1)

                    def layer2(c, u, g, b, least):
                        pe.wait_ge(h1_sb, c * NG + (g + 1))
                        if least >= 2:
                            pe.wait_ge(z2_sb, c * NG + (g - 1))
                        for j in range(GR):
                            ins = nc.tensor.matmul(PS[4 + b][:, j * H:(j + 1) * H], h1[b][:, j * P:(j + 1) * P], ew2_s[:, :],
                                                   start=True, stop=True)
                        ins.then_inc(z2_ps, 1)

                    def combine(c, u, g, b, least):
                        pe.wait_ge(m_sb, c * NG + (g + 1))
                        pe.wait_ge(eq_sb, c * NG + (g + 1))
                        if least >= 2:
                            pe.wait_ge(s_sb, c * NG + (g - 1))
                        for j in range(GR):
                            ins = nc.tensor.matmul(PS[6 + b][:, j * H:(j + 1) * H], equal[b][:, j * P:(j + 1) * P],
                                                   msg[b][:, j * H:(j + 1) * H], start=True, stop=True)
                        ins.then_inc(s_ps, 1)
                    slots(pe, head, (0, layer1), (1, layer2), (1, sources), (3, combine))

                @block.scalar
                def _(act):
                    def silu1(c, u, g, b, least):
                        act.wait_ge(z1_ps, c * NG + (g + 1))
                        if least >= 2:
                            act.wait_ge(z2_ps, c * NG + (g - 1))
                        nc.scalar.activation(h1[b], PS[b][:, :], ACT.Silu, bias=hid_s[:, 0:1]).then_inc(h1_sb, 1)

                    def silu2(c, u, g, b, least):
                        act.wait_ge(z2_sb, c * NG + (g + 1))
                        if least >= 2:
                            act.wait_ge(s_ps, c * NG + (g - 1))
                        nc.scalar.activation(msg[b], z2b[b], ACT.Silu).then_inc(m_sb, 1)

                    def take(c, u, g, b, least):
                        act.wait_ge(s_ps, c * NG + (g + 1))
                        if least >= 3:
                            for j in range(GR):
                                act.wait_ge(put[j], c * (16 * NG) + 16 * (g - 2))
                        nc.scalar.copy(total[g % 4], PS[6 + b][:, :]).then_inc(s_sb, 1)
                    slots(act, lambda i, u, c: None, (0, silu1), (2, silu2), (3, take))

        def finish():
            tab, summed, a_ps, x_ps, a_sb, x_sb, h_ps, h_sb, u_ps, u_sb, normed, written = (
                sem(f"f_{n}") for n in ("tab", "summed", "a_ps", "x_ps", "a_sb", "x_sb", "h_ps", "h_sb", "u_ps", "u_sb",
                                        "normed", "written"))
            part = [cross[:, :], node[:, 0:NP], xt[:, :]]
            agg = cross[:, :].rearrange("p (t h) -> p t h", h=H)
            aT, xT, hT = ([b[:, w:w + 512] for b in gbuf] for w in (0, 512, 1024))
            block = nc.Block()
            with block:
                @block.sync
                def _(sp):
                    for j in range(GR):
                        if j == 3:
                            sp.wait_ge(summed, 1)
                        sp.dma_start(part[j if j < 3 else 1].rearrange("p (t h) -> p t h", h=H),
                                     agg_table[j][0:NP, :].rearrange("(t p) h -> p t h", p=P)).then_inc(tab, 16)
                    sp.wait_ge(normed, 1)
                    whole = N // P
                    sp.dma_start(out[0:whole * P, :].rearrange("(t p) f -> p t f", p=P), X[:, 0:whole, :]).then_inc(written, 16)
                    sp.dma_start(out[whole * P:N, :], X[0:N - whole * P, whole, :]).then_inc(written, 16)
                    sp.wait_ge(written, 32)

                @block.tensor
                def _(pe):
                    pe.wait_ge(summed, 3)
                    for g, tiles in enumerate(TILE_GROUPS):
                        b, n = g % 2, len(tiles)
                        if g >= 2:
                            pe.wait_ge(a_sb, g - 1)
                            pe.wait_ge(x_sb, g - 1)
                        for j, t in enumerate(tiles):
                            ins = nc.tensor.transpose(PS[b][:, j * P:(j + 1) * P], agg[:, t, :], ident[:, :])
                        ins.then_inc(a_ps, 1)
                        for j, t in enumerate(tiles):
                            ins = nc.tensor.transpose(PS[2 + b][0:F, j * P:(j + 1) * P], X[:, t, :], ident[:, :])
                        ins.then_inc(x_ps, 1)
                        pe.wait_ge(a_sb, g + 1)
                        pe.wait_ge(x_sb, g + 1)
                        if g >= 2:
                            pe.wait_ge(h_sb, g - 1)
                        nc.tensor.matmul(PS[4 + b][:, 0:n * P], nw1x_s[:, :], xT[b][0:F, 0:n * P], start=True, stop=False)
                        nc.tensor.matmul(PS[4 + b][:, 0:n * P], nw1a_s[:, :], aT[b][:, 0:n * P], start=False, stop=True)\
                            .then_inc(h_ps, 1)
                        pe.wait_ge(h_sb, g + 1)
                        if g >= 2:
                            pe.wait_ge(u_sb, g - 1)
                        for j in range(n):
                            ins = nc.tensor.matmul(PS[6 + b][:, j * F:(j + 1) * F], hT[b][:, j * P:(j + 1) * P], nw2_s[:, :],
                                                   start=True, stop=True)
                        ins.then_inc(u_ps, 1)

                @block.scalar
                def _(act):
                    for g, tiles in enumerate(TILE_GROUPS):
                        b, n = g % 2, len(tiles)
                        act.wait_ge(a_ps, g + 1)
                        if g >= 2:
                            act.wait_ge(h_ps, g - 1)
                        nc.scalar.copy(aT[b][:, 0:n * P], PS[b][:, 0:n * P]).then_inc(a_sb, 1)
                        act.wait_ge(h_ps, g + 1)
                        if g >= 2:
                            act.wait_ge(u_ps, g - 1)
                        nc.scalar.activation(hT[b][:, 0:n * P], PS[4 + b][:, 0:n * P], ACT.Silu, bias=hid_s[:, 1:2]).then_inc(h_sb, 1)
                    act.wait_ge(var_made, 4)
                    nc.scalar.activation(var[:, :], var[:, :], ACT.Sqrt).then_inc(root_made, 1)

                @block.vector
                def _(dve):
                    for j in range(1, GR):
                        dve.wait_ge(tab, 16 * (3 if j < 3 else 4))
                        nc.vector.tensor_tensor(part[0], part[0], part[j if j < 3 else 1], ALU.add).then_inc(summed, 1)
                        dve.wait_ge(summed, j)
                    for g, tiles in enumerate(TILE_GROUPS):
                        b, n = g % 2, len(tiles)
                        dve.wait_ge(x_ps, g + 1)
                        if g >= 2:
                            dve.wait_ge(h_ps, g - 1)
                        nc.vector.tensor_copy(xT[b][0:F, 0:n * P], PS[2 + b][0:F, 0:n * P]).then_inc(x_sb, 1)
                        dve.wait_ge(u_ps, g + 1)
                        nc.vector.tensor_tensor(S1[:, tiles[0]:tiles[-1] + 1, :],
                                                PS[6 + b][:, 0:n * F].rearrange("p (t f) -> p t f", f=F),
                                                bias_s[:, 2:3, :].to_broadcast([P, n, F]), ALU.add).then_inc(u_sb, 1)
                    dve.wait_ge(u_sb, len(TILE_GROUPS))
                    ch.link(nc.vector.tensor_tensor(S1, S1, X[:, :, :], ALU.add))
                    ch.link(nc.vector.tensor_tensor(X[:, :, :], S1, X[:, :, :], ALU.add))
                    layer_norm(dve, X[:, :, :], S1, 4)
                    nc.vector.tensor_copy(tot[:, 0:1], mean[:, 0:1]).then_inc(normed, 1)

        check_order()
        order_edges()
        edge_lists()
        relation_table()
        gather_pass(0, rel_table, row_idx)
        degrees()
        collect(0)
        node_stage(0)
        for l in (1, 2, 3):
            gather_pass(l, node_table[l - 1], src_i, irregular)
            collect(l, irregular)
            product(l, X[:, :, :] if l == 1 else S2)
            node_stage(l)
        edge_tables()
        edge_mlp()
        finish()


def kernel(**inputs):
    import numpy as np
    import concourse.bacc as bacc
    from concourse.bass_utils import run_bass_kernel_spmd

    a = {k: np.asarray(v) for k, v in inputs.items()}

    def edges(v, fill):
        full = np.full((EP,) + v.shape[1:], fill, v.dtype)
        full[:E] = v
        return full.reshape((P, KT) + v.shape[1:])

    src, dst = edges(a["src"], NP - 1), edges(a["dst"], N)
    dst.reshape(-1)[E:] = N + np.arange(EP - E) * (NP - N) // (EP - E)
    ew1 = a["L3_gnn_ew1"]
    bias_rows = np.stack([a["L2_gnn_b1"], a["L2_gnn_b2"], a["L3_gnn_nb2"]])
    weighted = np.concatenate([a["edge_weight"][:, None], a["edge_attr_16"]], 1)
    arrays = {
        "x": np.concatenate([a["x"], np.zeros((NP - N, F), a["x"].dtype)]),
        "src": src,
        "dst": dst,
        "etype": edges(a["edge_type_16"], 0),
        "src_t": src.T.reshape(P, KT),
        "dst_t": dst.T.reshape(1, EP),
        "attr_t": edges(weighted, 0).transpose(2, 1, 0).reshape(1 + A, EP),
        "attr_rows": edges(weighted, 0),
        "rel_w": a["L0_gnn_W"].transpose(2, 0, 1).reshape(F, RELS * F),
        "gcn_w": np.stack([a["L2_gnn_W1"], a["L2_gnn_W2"]], 1),
        "bias_rows": np.broadcast_to(bias_rows, (P, 3, F)),
        "ew1": np.concatenate([ew1[:F], ew1[F:2 * F]], 1),
        "we": np.concatenate([ew1[2 * F + A:], ew1[2 * F:2 * F + A]]),
        "ew2": a["L3_gnn_ew2"],
        "hid_b": np.stack([a["L3_gnn_eb1"], a["L3_gnn_nb1"]], 1),
        "eb2_rows": np.broadcast_to(a["L3_gnn_eb2"], (P, H)),
        "nw1x": a["L3_gnn_nw1"][:F],
        "nw1a": a["L3_gnn_nw1"][F:],
        "nw2": a["L3_gnn_nw2"],
    }
    arrays = {k: np.ascontiguousarray(v) for k, v in arrays.items()}
    nc = bacc.Bacc("TRN2", target_bir_lowering=False, num_devices=1)
    args = {k: nc.dram_tensor(f"in_{k}", v.shape, mybir.dt.from_np(v.dtype), kind="ExternalInput").ap() for k, v in arrays.items()}
    out = nc.dram_tensor("out", (N, F), mybir.dt.float32, kind="ExternalOutput").ap()
    gnn_kernel(nc, out=out, **args)
    r = run_bass_kernel_spmd(nc, [{f"in_{k}": v for k, v in arrays.items()}], core_ids=[0])
    return r.results[0]["out"]
```

```python
from contextlib import ExitStack

import concourse.bass as bass
from concourse import mybir

N, E, F, H, A, RELS = 6250, 200000, 64, 128, 16, 16
P = 128
NT = -(-N // P)
NP = NT * P
CH = 56
NCH = -(-E // (P * CH))
KT = NCH * CH
EP = KT * P
GR = 4
CE = 28
NCE = KT // CE
NG = CE // GR
HB = 8
NH = CH // HB
WN = 8
WJ = 3
WE = WJ * P
WC = WN * NT
WT = P // WN
BT = 4 * (NCH // 2 - 1)
WA, WB = BT * WT // 32, 32
WR = (BT + 4) * WT
WH = 16
EXACT = 256
PARTS = 3
EPS = 1e-5
CUTOFF = 5.0
assert BT >= NT and WA * WB == BT * WT and NT % 4 == 1 and KT % (2 * WH) == 0
assert NCH % 2 == 0 and NCE % 2 == 0 and NG % 2 == 1 and NH % 2 == 1
TILE_GROUPS = [list(range(t, min(t + GR, NT))) for t in range(0, NT, GR)]


def gnn_kernel(nc, x, src, dst, etype, src_t, dst_t, attr_t, attr_rows, rel_w, gcn_w, bias_rows, ew1, we, ew2, hid_b,
               eb2_rows, nw1x, nw1a, nw2, out):
    f32, bf16, i32 = mybir.dt.float32, mybir.dt.bfloat16, mybir.dt.int32
    ALU, ACT, AX = mybir.AluOpType, mybir.ActivationFunctionType, mybir.AxisListType
    ds = bass.ds
    ctx = ExitStack()
    with ctx, nc.allow_non_contiguous_dma(reason="columns of the edge lists"):
        def sb(name, shape, dt=f32):
            return ctx.enter_context(nc.sbuf_tensor(name, shape, dt))

        def sem(name):
            return ctx.enter_context(nc.semaphore(name))

        def rows(col):
            return bass.IndirectOffsetOnAxis(ap=col, axis=0)

        rel_table = nc.dram_tensor("rel_table", [NP * RELS, F], f32).ap()
        node_table = [nc.dram_tensor(f"node_table{i}", [NP, F], f32).ap() for i in range(3)]
        sums = [nc.dram_tensor(f"sums{i}", [P, KT, F], f32).ap() for i in range(4)]
        p_table = nc.dram_tensor("p_table", [NP, H], f32).ap()
        q_table = nc.dram_tensor("q_table", [NP, H], f32).ap()
        x_hidden = nc.dram_tensor("x_hidden", [H, NP], f32).ap()
        q_starts = nc.dram_tensor("q_starts", [EP + NP, H], f32).ap()
        agg_table = [nc.dram_tensor(f"agg_table{j}", [NP + P, H], f32).ap() for j in range(GR)]
        src_split = nc.dram_tensor("src_split", [2, EP], bf16).ap()

        by_dst = {n: nc.dram_tensor(f"by_dst_{n}", [EP, 1], i32).ap() for n in ("dst", "src", "type")}
        by_dst_src_t = nc.dram_tensor("by_dst_src_t", [P, KT], i32).ap()
        by_dst_rows = nc.dram_tensor("by_dst_rows", [EP, 1 + A], f32).ap()
        edge_attr = nc.dram_tensor("edge_attr", [1 + A, EP], f32).ap()
        cursor = nc.dram_tensor("cursor", [NP + P, 1], f32).ap()
        starts = nc.dram_tensor("starts", [NP, 1], f32).ap()

        keys = nc.dram_tensor("keys", [EP + 4 * P, 2], f32).ap()
        win_first = nc.dram_tensor("win_first", [WA * WB, 1], i32).ap()
        counts = nc.dram_tensor("counts", [BT, P, NT * P], bf16).ap()

        src_i = sb("src_i", [P, KT], i32)
        row_idx = sb("row_idx", [P, KT], i32)
        same = sb("same", [P, KT])
        dst_tile = sb("dst_tile", [P, KT], bf16)
        cross = sb("cross", [P, NP])
        xt = sb("xt", [P, NP])
        X = sb("X", [P, NT, F])
        node = sb("node", [P, 3 * NT * F])
        S1, S2, S3 = (node[:, i * NT * F:(i + 1) * NT * F].rearrange("p (t f) -> p t f", f=F) for i in range(3))
        gbuf = [sb(f"gbuf{u}", [P, CH * F]) for u in range(2)]
        rbuf = [sb(f"rbuf{u}", [P, CH * F]) for u in range(2)]
        G, R = ([b[:, :].rearrange("p (k f) -> p k f", f=F) for b in bufs] for bufs in (gbuf, rbuf))
        GE, QE = ([b[:, :].rearrange("p (k h) -> p k h", h=H) for b in bufs] for bufs in (gbuf, rbuf))
        get_rows = sb("get_rows", [P, 2, CH], i32)
        put_rows = sb("put_rows", [P, 2, CE], i32)
        ident = sb("ident", [P, P])
        before = sb("before", [P, P], bf16)
        upto = sb("upto", [P, P])
        ones = sb("ones", [P, P])
        ones_bf = sb("ones_bf", [2, P], bf16)
        count_i = sb("count_i", [P, P], i32)
        count_bf = sb("count_bf", [P, P], bf16)
        zeros = sb("zeros", [P, 512])
        zero_bf = sb("zero_bf", [P, P], bf16)
        dump_i = sb("dump_i", [P, 1 + NT], i32)
        dump = sb("dump", [P, 1 + NT])
        comes_in = sb("comes_in", [P, 1])
        goes_out = sb("goes_out", [P, 1])
        last_dst = sb("last_dst", [P, 1])
        near_dst = sb("near_dst", [P, 2], i32)
        first_dst = sb("first_dst", [P, 1], i32)
        deg, has, inv, dinv, tmp, tot, mean, var = (sb(n, [P, NT]) for n in ("deg", "has", "inv", "dinv", "tmp", "tot", "mean", "var"))
        end_row = sb("end_row", [P, NT], i32)
        start_row = sb("start_row", [P, NT], i32)
        q_in = sb("q_in", [P, H])
        gcn_s = sb("gcn_s", [F, 2, F])
        bias_s = sb("bias_s", [P, 3, F])
        eb2_s = sb("eb2_s", [P, H])
        ew1_s = sb("ew1_s", [F, 2 * H])
        we_s = sb("we_s", [1 + A, H])
        ew2_s = sb("ew2_s", [H, H])
        hid_s = sb("hid_s", [H, 2])
        nw1x_s = sb("nw1x_s", [F, H])
        nw1a_s = sb("nw1a_s", [H, H])
        nw2_s = sb("nw2_s", [H, F])
        win_hl = node[:, NP:NP + KT].bitcast(bf16).rearrange("p (a k) -> p a k", a=2)
        place_off = node[:, NP + KT:NP + 2 * KT]
        minus = sb("minus", [P, 8])
        lane = sb("lane", [P, WC], mybir.dt.float16)
        win_base = sb("win_base", [P, WT])
        win_most = sb("win_most", [P, 1])
        key_slot = sb("key_slot", [P, 4, WT, 2 * WJ])
        key_rel = sb("key_rel", [P, WT, WJ])
        irregular = sb("irregular", [P, 1], i32)
        shuffled = sb("shuffled", [P, 1], i32)
        attr_there = sem("attr_there")
        dst_i = rbuf[0][:, 0:KT].bitcast(i32)
        typ_i = rbuf[0][:, KT:2 * KT].bitcast(i32)
        srt_i = node[:, 2 * KT:3 * KT].bitcast(i32)
        PS = [ctx.enter_context(nc.psum_tensor(f"PS{i}", [P, 512], f32)) for i in range(8)]

        def over_f(col):
            return col[:, :].rearrange("p (t o) -> p t o", o=1).to_broadcast([P, NT, F])

        begun = sem("begun")

        def wait_counts(eng, *waits):
            counts = [n if isinstance(n, int) else eng.to_reg(n) for _, n in waits]
            eng.wait_ge(begun, 1)
            for (signal, _), n in zip(waits, counts):
                eng.wait_ge(signal, n)

        def by_pairs(eng, n, body):
            for u in range(2):
                body(0, u, u, True)
            with eng.Fori(1, n // 2) as i:
                for u in range(2):
                    body(i, u, i * 2 + u, False)

        class Chain:

            def __init__(self):
                self.sem, self.n = sem("dve_chain"), 0

            def link(self, ins):
                self.n += 1
                ins.then_inc(self.sem, 1)
                nc.vector.wait_ge(self.sem, self.n)

        ch = Chain()
        fetched, carried, ready, tabled, var_made, root_made, nd_tr_ps, nd_tr_sb, mixed = (
            sem(n) for n in ("fetched", "carried", "ready", "tabled", "var_made", "root_made", "nd_tr_ps", "nd_tr_sb",
                             "mixed"))

        def check_order():
            loaded, weights, preset, near, made, summed, flagged = (
                sem(n) for n in ("loaded", "weights", "preset", "near", "made", "viol_sum", "flagged"))
            falls = rbuf[1][:, 0:KT]
            block = nc.Block()
            with block:
                @block.sync
                def _(sp):
                    sp.dma_start(dst_i, dst).then_inc(loaded, 16)
                    sp.dma_start(src_i[:, :], src).then_inc(loaded, 16)
                    sp.dma_start(typ_i, etype).then_inc(loaded, 16)
                    sp.dma_start(X[:, :, :], x.rearrange("(t p) f -> p t f", p=P)).then_inc(loaded, 16)
                    sp.wait_ge(preset, 1)
                    sp.dma_start(near_dst[1:P, 0:1], dst[0:P - 1, KT - 1:KT]).then_inc(near, 16)
                    sp.wait_ge(loaded, 16 * 4)

                @block.scalar
                def _(act):
                    for a, b in ((cross[0:F, 0:RELS * F], rel_w), (gcn_s[:, :, :], gcn_w), (bias_s[:, :, :], bias_rows),
                                 (eb2_s[:, :], eb2_rows), (ew1_s[:, :], ew1), (we_s[:, :], we), (ew2_s[:, :], ew2),
                                 (hid_s[:, :], hid_b), (nw1x_s[:, :], nw1x), (nw1a_s[:, :], nw1a), (nw2_s[:, :], nw2)):
                        act.dma_start(a, b).then_inc(weights, 16)
                    act.wait_ge(weights, 16 * 11)

                @block.gpsimd
                def _(pool):
                    nc.gpsimd.memset(near_dst[:, :], -1).then_inc(preset, 1)
                    nc.gpsimd.memset(zeros[:, :], 0.0).then_inc(begun, 1)
                    nc.gpsimd.memset(zero_bf[:, :], 0.0)
                    nc.gpsimd.memset(ones[:, :], 1.0).then_inc(made, 1)
                    nc.gpsimd.memset(ones_bf[:, :], 1.0)
                    nc.gpsimd.memset(minus[:, :], -1.0)
                    nc.gpsimd.memset(win_most[:, :], 0.0)
                    nc.gpsimd.iota(lane[:, :], pattern=[[1, WC]], base=0, channel_multiplier=0,
                                   allow_small_or_imprecise_dtypes=True)
                    nc.gpsimd.iota(win_base[:, :], pattern=[[WC, WT]], base=0, channel_multiplier=0,
                                   allow_small_or_imprecise_dtypes=True)
                    nc.gpsimd.iota(dump_i[:, 0:1], pattern=[[0, 1]], base=NP, channel_multiplier=1)
                    nc.gpsimd.iota(dump_i[:, 1:1 + NT], pattern=[[P, NT]], base=EP, channel_multiplier=1)
                    nc.gpsimd.iota(count_i[:, :], pattern=[[1, P]], base=0, channel_multiplier=0).then_inc(made, 1)
                    pool.wait_ge(made, 2)
                    nc.gpsimd.affine_select(out=ident[:, :], in_=ones[:, :], compare_op=ALU.is_equal, fill=0.0,
                                            base=0, pattern=[[-1, P]], channel_multiplier=1)
                    nc.gpsimd.affine_select(out=before[:, :], in_=ones[:, :], compare_op=ALU.is_gt, fill=0.0,
                                            base=0, pattern=[[-1, P]], channel_multiplier=1)
                    nc.gpsimd.affine_select(out=upto[:, :], in_=ones[:, :], compare_op=ALU.is_ge, fill=0.0,
                                            base=0, pattern=[[1, P]], channel_multiplier=-1)

                @block.vector
                def _(dve):
                    dve.wait_ge(made, 2)
                    nc.vector.tensor_copy(count_bf[:, :], count_i[:, :])
                    nc.vector.tensor_copy(dump[:, :], dump_i[:, :])
                    dve.wait_ge(weights, 16 * 11)
                    nc.vector.tensor_scalar(we_s[0:1, :], we_s[0:1, :], 1.0 / CUTOFF, None, ALU.mult)
                    dve.wait_ge(loaded, 16 * 4)
                    nc.vector.tensor_tensor(falls[:, 1:KT], dst_i[:, 1:KT], dst_i[:, 0:KT - 1], ALU.is_lt)
                    dve.wait_ge(near, 16)
                    ch.link(nc.vector.tensor_tensor(falls[:, 0:1], dst_i[:, 0:1], near_dst[:, 0:1], ALU.is_lt))
                    nc.vector.tensor_reduce(tmp[:, 0:1], falls, AX.X, ALU.max).then_inc(flagged, 1)
                    dve.wait_ge(summed, 1)
                    nc.vector.tensor_scalar(shuffled[:, :], PS[0][:, 0:1], 1.0, None, ALU.min)

                @block.tensor
                def _(pe):
                    pe.wait_ge(made, 2)
                    pe.wait_ge(flagged, 1)
                    nc.tensor.matmul(PS[0][:, 0:1], ones[:, :], tmp[:, 0:1], start=True, stop=True).then_inc(summed, 1)

        def order_edges():
            srt_in, init, row_in, row_used, idx, cur_in, made, put, totals, table_in, pre, start_out = (
                sem(f"o_{n}") for n in ("srt", "init", "row", "row_used", "idx", "cur", "made", "put", "totals",
                                        "table_in", "pre", "start_out"))
            rec_in, relaid, chain, idx2, cur2, made2 = (
                sem(f"o_{n}") for n in ("rec_in", "relaid", "chain", "idx2", "cur2", "made2"))
            moved = [sem(f"o_moved{a}") for a in range(4)]
            rank = rbuf[1][:, 0:KT]
            row = node[:, 0:P].bitcast(i32)
            same_t, prior = node[:, P:2 * P], node[:, 2 * P:3 * P]
            col = [node[:, 3 * P + 8 * j:3 * P + 8 * j + 1] for j in range(12)]
            col_i = [c.bitcast(i32) for c in col]
            at, target, place, v_dst, v_src, v_typ = col_i[0:6]
            met, n_prior, n_same, count, gap, begin = col[6:12]
            rec = node[:, 512:512 + 1 + A]
            LINKS = 7
            block = nc.Block()

            def steps(eng, body):
                body(0, True)
                with eng.Fori(1, KT) as k:
                    body(k, False)

            with block:
                @block.sync
                def _(sp):
                    flag = sp.value_load(shuffled[0:1, 0:1], min_val=0, max_val=1)
                    with sp.If(flag != 0):
                        sp.dma_start(cursor.rearrange("(p a) o -> p (a o)", p=P), zeros[:, 0:(NP + P) // P]).then_inc(init, 16)

                        def targets(k, first):
                            if not first:
                                wait_counts(sp, (row_used, k * 1))
                            sp.dma_start(row, dst_t[0:1, ds(k * P, P)].to_broadcast([P, P])).then_inc(row_in, 16)
                        steps(sp, targets)
                        sp.wait_ge(put, 16 * KT)
                        sp.dma_start(deg[:, :], cursor[0:NP, :].rearrange("(t p) o -> p (t o)", p=P)).then_inc(table_in, 16)
                        sp.wait_ge(pre, 2)
                        sp.dma_start(starts.rearrange("(t p) o -> p (t o)", p=P), tmp[:, :]).then_inc(start_out, 16)

                        def records(k, first):
                            if not first:
                                wait_counts(sp, (moved[3], k * 16))
                            sp.dma_start(rec, attr_rows[:, ds(k, 1), :].rearrange("p o a -> p (o a)")).then_inc(rec_in, 16)
                        steps(sp, records)
                        for a in range(4):
                            sp.wait_ge(moved[a], 16 * KT)
                        sp.dma_start(by_dst_src_t.rearrange("p k -> (p k)").rearrange("(k p) -> k p", p=P),
                                     by_dst["src"].rearrange("(p k) o -> k (p o)", p=P)).then_inc(relaid, 16)
                        for a in range(1 + A):
                            sp.dma_start(edge_attr[a, :].rearrange("(k p) -> k p", p=P),
                                         by_dst_rows[:, a:a + 1].rearrange("(p k) o -> k (p o)", p=P)).then_inc(relaid, 16)
                        for to, n in ((dst_i, "dst"), (src_i[:, :], "src"), (typ_i, "type")):
                            sp.dma_start(to, by_dst[n].rearrange("(p k) o -> p (k o)", p=P)).then_inc(relaid, 16)
                        sp.wait_ge(relaid, 16 * (2 + A + 3))
                        sp.dma_start(srt_i, by_dst_src_t).then_inc(srt_in, 16)
                        sp.sem_inc(attr_there, 16)
                    with sp.Else():
                        sp.dma_start(edge_attr, attr_t).then_inc(attr_there, 16)
                        sp.dma_start(srt_i, src_t).then_inc(srt_in, 16)
                    sp.wait_ge(srt_in, 16)

                @block.gpsimd
                def _(pool):
                    flag = pool.value_load(shuffled[0:1, 0:1], min_val=0, max_val=1)
                    with pool.If(flag != 0):
                        pool.wait_ge(init, 16)

                        def count_step(k, first):
                            nc.gpsimd.tensor_copy(at, dst_i[:, ds(k, 1)]).then_inc(idx, 1)
                            waits = [(idx, k + 1)]
                            if not first:
                                waits.append((put, k * 16))
                            wait_counts(pool, *waits)
                            nc.gpsimd.indirect_dma_start(met, None, cursor, rows(at)).then_inc(cur_in, 16)
                            wait_counts(pool, (made, k + 1))
                            nc.gpsimd.indirect_dma_start(cursor, rows(target), count, None).then_inc(put, 16)
                        steps(pool, count_step)
                        pool.wait_ge(start_out, 16)

                        def move_step(k, first):
                            if not first:
                                for a in range(4):
                                    pool.wait_ge(moved[a], k * 16)
                            for to, of in ((at, dst_i), (v_dst, dst_i), (v_src, src_i), (v_typ, typ_i)):
                                ins = nc.gpsimd.tensor_copy(to, of[:, ds(k, 1)])
                            ins.then_inc(idx2, 1)
                            wait_counts(pool, (idx2, k + 1))
                            nc.gpsimd.indirect_dma_start(begin, None, starts, rows(at)).then_inc(cur2, 16)
                            wait_counts(pool, (made2, k + 1), (rec_in, k * 16 + 16))
                            for a, (to, of) in enumerate(((by_dst["dst"], v_dst), (by_dst["src"], v_src),
                                                          (by_dst["type"], v_typ), (by_dst_rows, rec))):
                                nc.gpsimd.indirect_dma_start(to, rows(place), of, None).then_inc(moved[a], 16)
                        steps(pool, move_step)
                        for a in range(4):
                            pool.wait_ge(moved[a], 16 * KT)
                    with pool.Else():
                        pool.wait_ge(begun, 1)

                @block.vector
                def _(dve):
                    flag = dve.value_load(shuffled[0:1, 0:1], min_val=0, max_val=1)
                    with dve.If(flag != 0):
                        def count_step(k, first):
                            done = [0]

                            def link(ins):
                                done[0] += 1
                                ins.then_inc(chain, 1)
                                dve.wait_ge(chain, k * LINKS + done[0])
                            here = dst_i[:, ds(k, 1)]
                            dve.wait_ge(row_in, k * 16 + 16)
                            nc.vector.tensor_tensor(same_t, row, here.to_broadcast([P, P]), ALU.is_equal).then_inc(row_used, 1)
                            dve.wait_ge(row_used, k + 1)
                            link(nc.vector.tensor_tensor(prior, same_t, before[:, :], ALU.mult))
                            link(nc.vector.tensor_reduce(n_prior, prior, AX.X, ALU.add))
                            link(nc.vector.tensor_reduce(n_same, same_t, AX.X, ALU.add))
                            link(nc.vector.tensor_scalar(gap, here, -1.0, dump[:, 0:1], ALU.mult, ALU.add))
                            link(nc.vector.scalar_tensor_tensor(out=gap, in0=n_prior, scalar=0.0, in1=gap, op0=ALU.is_gt,
                                                                op1=ALU.mult))
                            dve.wait_ge(cur_in, k * 16 + 16)
                            nc.vector.tensor_tensor(target, gap, here, ALU.add)
                            link(nc.vector.tensor_tensor(rank[:, ds(k, 1)], met, n_prior, ALU.add))
                            link(nc.vector.tensor_tensor(count, met, n_same, ALU.add))
                            nc.vector.tensor_copy(n_same, count).then_inc(made, 1)
                        steps(dve, count_step)
                        dve.wait_ge(totals, 1)
                        nc.vector.tensor_copy(tot[:, :], PS[1][:, 0:NT]).then_inc(row_used, 1)
                        dve.wait_ge(row_used, KT + 1)
                        nc.vector.tensor_tensor_scan(tmp[:, :], ones[:, 0:NT], tot[:, :], 0.0, ALU.mult, ALU.add).then_inc(row_used, 1)
                        dve.wait_ge(row_used, KT + 2)
                        nc.vector.tensor_tensor(tmp[:, :], tmp[:, :], tot[:, :], ALU.subtract).then_inc(row_used, 1)
                        dve.wait_ge(row_used, KT + 3)
                        nc.vector.tensor_tensor(tmp[:, :], tmp[:, :], PS[0][:, 0:NT], ALU.add).then_inc(pre, 1)
                        dve.wait_ge(pre, 1)
                        nc.vector.tensor_tensor(tmp[:, :], tmp[:, :], deg[:, :], ALU.subtract).then_inc(pre, 1)

                        def place_step(k, first):
                            dve.wait_ge(cur2, k * 16 + 16)
                            if not first:
                                for a in range(4):
                                    dve.wait_ge(moved[a], k * 16)
                            nc.vector.tensor_tensor(place, begin, rank[:, ds(k, 1)], ALU.add).then_inc(made2, 1)
                        steps(dve, place_step)
                    with dve.Else():
                        dve.wait_ge(begun, 1)

                @block.tensor
                def _(pe):
                    flag = pe.value_load(shuffled[0:1, 0:1], min_val=0, max_val=1)
                    with pe.If(flag != 0):
                        pe.wait_ge(table_in, 16)
                        nc.tensor.matmul(PS[0][:, 0:NT], upto[:, :], deg[:, :], start=True, stop=True)
                        nc.tensor.matmul(PS[1][:, 0:NT], ones[:, :], deg[:, :], start=True, stop=True).then_inc(totals, 1)
                    with pe.Else():
                        pe.wait_ge(begun, 1)

        def pe_transpose(pe, rows3, banks, ps_sem, sb_sem):
            for g, tiles in enumerate(TILE_GROUPS):
                if g >= 2:
                    pe.wait_ge(sb_sem, g - 1)
                for j, t in enumerate(tiles):
                    ins = nc.tensor.transpose(banks[g % 2][0:F, j * P:(j + 1) * P], rows3[:, t, :], ident[:, :])
                ins.then_inc(ps_sem, 1)

        def act_untranspose(act, banks, ps_sem, sb_sem, done=0):
            for g, tiles in enumerate(TILE_GROUPS):
                act.wait_ge(ps_sem, done + g + 1)
                n = len(tiles) * P
                nc.scalar.copy(xt[0:F, g * GR * P:g * GR * P + n], banks[g % 2][0:F, 0:n]).then_inc(sb_sem, 1)

        rel_tr_ps, rel_tr_sb, rel_mm, rel_sb = (sem(f"rel_{n}") for n in ("tr_ps", "tr_sb", "mm", "sb"))
        STAGES, BANKS = 4, 3
        rel_put = [sem(f"rel_put{u}") for u in range(STAGES)]
        stage = [gbuf[u // 2][:, u % 2 * RELS * F:(u % 2 + 1) * RELS * F] for u in range(STAGES)]

        def pe_relations(pe):
            pe_transpose(pe, X, PS[0:2], rel_tr_ps, rel_tr_sb)
            for t in range(NT):
                pe.wait_ge(rel_tr_sb, t // GR + 1)
                if t >= BANKS:
                    pe.wait_ge(rel_sb, 2 * (t - BANKS + 1))
                for h in range(2):
                    ins = nc.tensor.matmul(PS[2 + 2 * (t % BANKS) + h][:, :], xt[0:F, t * P:(t + 1) * P],
                                           cross[0:F, h * 512:(h + 1) * 512], start=True, stop=True)
                ins.then_inc(rel_mm, 1)

        def act_relations(act):
            act_untranspose(act, PS[0:2], rel_tr_ps, rel_tr_sb)
            for t in range(NT):
                u = t % STAGES
                act.wait_ge(rel_mm, t + 1)
                if t >= STAGES:
                    act.wait_ge(rel_put[u], 16 * (t // STAGES))
                for h in range(2):
                    nc.scalar.copy(stage[u][:, h * 512:(h + 1) * 512], PS[2 + 2 * (t % BANKS) + h][:, :]).then_inc(rel_sb, 1)
                act.wait_ge(rel_sb, 2 * (t + 1))
                act.dma_start(rel_table[t * P * RELS:(t + 1) * P * RELS, :].rearrange("(p r) f -> p (r f)", r=RELS),
                              stage[u]).then_inc(rel_put[u], 16)
            for u in range(STAGES):
                act.wait_ge(rel_put[u], 16 * len(range(u, NT, STAGES)))

        def edge_lists():
            preset, near, wide_done, split, first_in = (sem(f"l_{n}") for n in ("preset", "near", "wide", "split", "first"))
            part_i = rbuf[1][:, 0:KT].bitcast(i32)
            srt_bf = node[:, 3 * KT:4 * KT].bitcast(bf16).rearrange("p (a k) -> p a k", a=2)
            block = nc.Block()
            with block:
                @block.tensor
                def _(pe):
                    pe_relations(pe)

                @block.scalar
                def _(act):
                    act_relations(act)

                @block.gpsimd
                def _(pool):
                    nc.gpsimd.memset(near_dst[:, :], -1).then_inc(preset, 1)

                @block.sync
                def _(sp):
                    sp.wait_ge(preset, 1)
                    sp.dma_start(near_dst[1:P, 0:1], dst_i[0:P - 1, KT - 1:KT]).then_inc(near, 16)
                    sp.dma_start(near_dst[0:P - 1, 1:2], dst_i[1:P, 0:1]).then_inc(near, 16)
                    sp.wait_ge(split, 2)
                    sp.dma_start(src_split.rearrange("a (p k) -> p a k", p=P), srt_bf).then_inc(wide_done, 16)
                    sp.dma_start(keys[EP:EP + 4 * P, :].rearrange("(p a) b -> p (a b)", p=P), minus[:, :]).then_inc(wide_done, 16)
                    sp.wait_ge(split, 3)
                    sp.dma_start(keys[0:EP, :].rearrange("(p k) b -> p (k b)", p=P), node[:, 0:2 * KT]).then_inc(wide_done, 16)
                    sp.wait_ge(wide_done, 48)

                @block.vector
                def _(dve):
                    for a, mask in enumerate((~127, 127)):
                        ch.link(nc.vector.tensor_scalar(part_i, srt_i, mask, None, ALU.bitwise_and))
                        ch.link(nc.vector.tensor_copy(srt_bf[:, a, :], part_i))
                    nc.vector.tensor_scalar(row_idx[:, :], src_i[:, :], float(RELS), None, ALU.mult).then_inc(split, 2)
                    dve.wait_ge(split, 2)
                    nc.vector.tensor_tensor(same[:, 1:KT], dst_i[:, 1:KT], dst_i[:, 0:KT - 1], ALU.is_equal)
                    nc.vector.tensor_tensor(row_idx[:, :], row_idx[:, :], typ_i, ALU.add)
                    nc.vector.memset(same[:, 0:1], 0.0)
                    ch.link(nc.vector.tensor_scalar(part_i, dst_i, 7, None, ALU.logical_shift_right))
                    ch.link(nc.vector.tensor_copy(dst_tile[:, :], part_i))
                    ch.link(nc.vector.tensor_scalar(part_i, dst_i, P - 1, None, ALU.bitwise_and))
                    ch.link(nc.vector.tensor_scalar(place_off, part_i, -1.0, 0.5, ALU.mult, ALU.add))
                    for a, (shift, mask) in enumerate(((8, 31), (3, 31))):
                        ch.link(nc.vector.tensor_scalar(part_i, dst_i, shift, mask, ALU.logical_shift_right, ALU.bitwise_and))
                        ch.link(nc.vector.tensor_copy(win_hl[:, a, :], part_i))
                    pair = node[:, 0:2 * KT].rearrange("p (k b) -> p k b", b=2)
                    ch.link(nc.vector.tensor_scalar(part_i, src_i[:, :], 7, None, ALU.logical_shift_right))
                    ch.link(nc.vector.scalar_tensor_tensor(out=pair[:, :, 0], in0=dst_i, scalar=float(NT), in1=part_i,
                                                           op0=ALU.mult, op1=ALU.add))
                    ch.link(nc.vector.tensor_scalar(part_i, src_i[:, :], P - 1, None, ALU.bitwise_and))
                    nc.vector.tensor_copy(pair[:, :, 1], part_i).then_inc(split, 1)
                    dve.wait_ge(split, 3)
                    nc.vector.tensor_copy(last_dst[:, :], dst_i[:, KT - 1:KT])
                    nc.vector.tensor_copy(first_dst[:, :], dst_i[:, 0:1])
                    dve.wait_ge(near, 32)
                    nc.vector.tensor_tensor(comes_in[:, :], near_dst[:, 0:1], dst_i[:, 0:1], ALU.is_equal)
                    nc.vector.tensor_tensor(goes_out[:, :], near_dst[:, 1:2], dst_i[:, KT - 1:KT], ALU.is_equal)

        def only_if(eng, flag, body):
            if flag is None:
                body()
                return
            value = eng.value_load(flag[0:1, 0:1], min_val=0, max_val=1)
            with eng.If(value != 0):
                body()
            with eng.Else():
                eng.wait_ge(begun, 1)

        idx_ready, gathered, scanned, stored = (
            [sem(f"{n}{u}") for u in range(2)] for n in ("idx_ready", "gathered", "scanned", "stored"))

        def gather_pass(l, table, index, flag=None):
            past = l * (NCH // 2)
            block = nc.Block()
            with block:
                @block.gpsimd
                def _(pool):
                    def chunk(i, u, c, first):
                        if not first:
                            pool.wait_ge(gathered[u], (i + past) * (16 * CH))
                            pool.wait_ge(scanned[u], i + past)
                        nc.gpsimd.tensor_copy(get_rows[:, u, :], index[:, ds(c * CH, CH)]).then_inc(idx_ready[u], 1)
                        wait_counts(pool, (idx_ready[u], i + (past + 1)))
                        for k in range(CH):
                            nc.gpsimd.indirect_dma_start(G[u][:, k, :], None, table, rows(get_rows[:, u, k:k + 1]))\
                                .then_inc(gathered[u], 16)
                    only_if(pool, flag, lambda: by_pairs(pool, NCH, chunk))
                    if l == 0:
                        nc.gpsimd.iota(cross[:, :], pattern=[[1, NP]], base=0, channel_multiplier=0,
                                       allow_small_or_imprecise_dtypes=True).then_inc(counted, 1)

                @block.vector
                def _(dve):
                    def chunk(i, u, c, first):
                        if l == 0:
                            dve_counts(dve, i, u, c, first)
                        dve.wait_ge(gathered[u], (i + (past + 1)) * (16 * CH))
                        if not first:
                            dve.wait_ge(stored[u], (i + past) * 16)
                        if u == 1:
                            dve.wait_ge(scanned[0], i + (past + 1))
                        elif not first:
                            dve.wait_ge(scanned[1], i + past)
                        for f in range(F):
                            start = 0.0 if first and u == 0 else R[1 - u][:, CH - 1, f:f + 1]
                            ins = nc.vector.tensor_tensor_scan(R[u][:, :, f], same[:, ds(c * CH, CH)], G[u][:, :, f],
                                                               start, ALU.mult, ALU.add)
                        ins.then_inc(scanned[u], 1)
                    if l == 0:
                        dve_windows(dve)
                    only_if(dve, flag, lambda: by_pairs(dve, NCH, chunk))

                @block.sync
                def _(sp):
                    def chunk(i, u, c, first):
                        if l == 0:
                            sp_keys(sp, i, u, c, first)
                        wait_counts(sp, (scanned[u], i + (past + 1)))
                        sp.dma_start(sums[l][:, ds(c * CH, CH), :], R[u]).then_inc(stored[u], 16)

                    def body():
                        by_pairs(sp, NCH, chunk)
                        for u in range(2):
                            sp.wait_ge(stored[u], 16 * (past + NCH // 2))
                    if l == 0:
                        sp_windows(sp)
                    only_if(sp, flag, body)

                if l == 0:
                    @block.scalar
                    def _(act):
                        wide = zeros[:, :].rearrange("p (o n) -> p o n", o=1)
                        per = EP // P // NCH * H // 512
                        for u in range(2):
                            act.sem_inc(counts_out[u], 16)
                        for _ in range(4):
                            act.sem_inc(win_taken, 1)

                        def chunk(i, u, c, first):
                            act.dma_start(
                                q_starts[ds(c * (CH * P), CH * P), :].rearrange("(p a b) h -> p a (b h)", p=P, b=4),
                                wide.to_broadcast([P, per, 512])).then_inc(zeroed, 16)
                            if first:
                                for s in range(NH):
                                    act_degrees(act, c, u, s, True)
                                act.wait_ge(gathered[u], 16 * CH)
                            else:
                                act_counts(act, i, u, c)
                        for j in range(GR):
                            act.dma_start(agg_table[j].rearrange("(p a) h -> p a h", p=P),
                                          zeros[:, 0:H].rearrange("p (o n) -> p o n", o=1).to_broadcast([P, (NP + P) // P, H]))\
                                .then_inc(zeroed, 16)
                        act.wait_ge(win_sum, 1)
                        by_pairs(act, NCH, chunk)
                        act.wait_ge(zeroed, 16 * (NCH + GR))
                        for u in range(2):
                            act.wait_ge(counts_out[u], 16 * (BT // 2 + 1))

                    @block.tensor
                    def _(pe):
                        for _ in range(4):
                            pe.sem_inc(win_used, 1)
                        pe_windows(pe)
                        nc.tensor.matmul(PS[7][:, 0:NT], zero_bf[:, :], zero_bf[:, 0:NT], start=True, stop=False)

                        def chunk(i, u, c, first):
                            if first:
                                for s in range(NH):
                                    pe_degrees(pe, c, u, s)
                            else:
                                pe_counts(pe, i, u, c)
                        by_pairs(pe, NCH, chunk)
                        nc.tensor.matmul(PS[7][:, 0:NT], zero_bf[:, :], zero_bf[:, 0:NT], start=False, stop=True)

        counted = sem("counted")
        hot_ready, sign_ready, hot_used, zeroed = (sem(n) for n in ("hot_ready", "sign_ready", "hot_used", "zeroed"))
        wh_ready, wh_used, win_sum, win_sb, win_pre, win_made, win_there = (
            sem(n) for n in ("wh_ready", "wh_used", "win_sum", "win_sb", "win_pre", "win_made", "win_there"))
        keys_in = [sem(f"keys_in{q}") for q in range(4)]
        keys_used, win_ready, win_used, win_taken, rel_made = (
            sem(n) for n in ("keys_used", "win_ready", "win_used", "win_taken", "rel_made"))
        counts_out = [sem(f"counts_out{u}") for u in range(2)]
        hot = [xt[:, u * 1024:(u + 1) * 1024].bitcast(bf16) for u in range(2)]
        W0 = 2048
        key_hot = [xt[:, W0 + b * (WJ * WC // 2):W0 + (b + 1) * (WJ * WC // 2)].bitcast(bf16).rearrange("p (j n) -> p j n", j=WJ)
                   for b in range(4)]
        W1 = W0 + 4 * (WJ * WC // 2)
        place_hot = [xt[:, W1 + b * (WJ * P // 2):W1 + (b + 1) * (WJ * P // 2)].bitcast(bf16).rearrange("p (j n) -> p j n", j=WJ)
                     for b in range(4)]
        W2 = W1 + 4 * (WJ * P // 2)
        assert W2 + WR <= NP
        win_row = xt[0:1, W2:W2 + WR].bitcast(i32)
        tile_counts = [node[:, u * NP // 2:(u + 1) * NP // 2].bitcast(bf16) for u in range(2)]

        def batch_at(h, w):
            s, rest = divmod(h * WT + w, 4)
            return s if rest == 0 and s < NH else None

        def win_hot(b, a, n):
            at = 0 if a else WH * WB
            return hot[b][:, at:at + WH * n].rearrange("p (k e) -> p k e", e=n)

        def dve_windows(dve):
            def batch(i, u, c, first):
                if not first:
                    dve.wait_ge(wh_used, c - 1)
                for a, n in ((0, WA), (1, WB)):
                    ins = nc.vector.tensor_tensor(
                        win_hot(u, a, n),
                        win_hl[:, a, ds(c * WH, WH)].rearrange("p (k o) -> p k o", o=1).to_broadcast([P, WH, n]),
                        count_bf[:, 0:n].rearrange("p (o e) -> p o e", o=1).to_broadcast([P, WH, n]), ALU.is_equal)
                ins.then_inc(wh_ready, 1)
            by_pairs(dve, KT // WH, batch)
            size, base, both = deg[0:WB, 0:WA], tot[0:WB, 0:WA], tmp[0:WB, 0:WA]
            dve.wait_ge(win_sum, 1)
            nc.vector.tensor_copy(size, PS[6][0:WB, 0:WA]).then_inc(win_sb, 1)
            dve.wait_ge(win_sb, 1)
            nc.vector.tensor_reduce(win_most[0:WB, :], size, AX.X, ALU.max)
            dve.wait_ge(win_pre, 1)
            ch.link(nc.vector.tensor_copy(both, PS[5][0:WB, 0:WA]))
            ch.link(nc.vector.tensor_tensor_scan(base, ones[0:WB, 0:WA], both, 0.0, ALU.mult, ALU.add))
            ch.link(nc.vector.tensor_tensor(base, base, both, ALU.subtract))
            ch.link(nc.vector.tensor_tensor(base, base, PS[4][0:WB, 0:WA], ALU.add))
            nc.vector.tensor_tensor(end_row[0:WB, 0:WA], base, size, ALU.subtract).then_inc(win_made, 1)
            for _ in range(4):
                dve.sem_inc(keys_used, 1)

        def pe_windows(pe):
            nc.tensor.matmul(PS[6][0:WB, 0:WA], zero_bf[:, 0:WB], zero_bf[:, 0:WA], start=True, stop=False)

            def batch(i, u, c, first):
                pe.wait_ge(wh_ready, c + 1)
                for k in range(WH):
                    ins = nc.tensor.matmul(PS[6][0:WB, 0:WA], win_hot(u, 1, WB)[:, k, :], win_hot(u, 0, WA)[:, k, :],
                                           start=False, stop=False)
                ins.then_inc(wh_used, 1)
            by_pairs(pe, KT // WH, batch)
            nc.tensor.matmul(PS[6][0:WB, 0:WA], zero_bf[:, 0:WB], zero_bf[:, 0:WA], start=False, stop=True).then_inc(win_sum, 1)
            pe.wait_ge(win_sb, 1)
            nc.tensor.matmul(PS[4][0:WB, 0:WA], upto[0:WB, 0:WB], deg[0:WB, 0:WA], start=True, stop=True)
            nc.tensor.matmul(PS[5][0:WB, 0:WA], ones[0:WB, 0:WB], deg[0:WB, 0:WA], start=True, stop=True).then_inc(win_pre, 1)

        def sp_windows(sp):
            sp.wait_ge(win_made, 1)
            sp.dma_start(win_first.rearrange("(a b) o -> b (a o)", b=WB), end_row[0:WB, 0:WA]).then_inc(win_there, 16)
            sp.wait_ge(win_there, 16)
            sp.dma_start(win_row[:, 0:WA * WB], win_first.rearrange("n o -> o n")).then_inc(win_there, 16)
            sp.dma_start(win_row[:, WA * WB:WR], win_first[0:WR - WA * WB, :].rearrange("n o -> o n")).then_inc(win_there, 16)
            sp.wait_ge(win_there, 48)

        def sp_keys(sp, i, u, c, first):
            if first and u == 0:
                return
            for h in range(2):
                q = h if first else (2 * u + 2 + h) % 4
                t = h if first else i * 4 + (2 * u + h - 2)
                if not first:
                    wait_counts(sp, (keys_used, t + 1))
                for w0 in range(0, WT, 4):
                    regs = [sp.value_load(win_row[0:1, ds(t * WT + w, 1)], min_val=0, max_val=EP) for w in range(w0, w0 + 4)]
                    for w, at in zip(range(w0, w0 + 4), regs):
                        sp.dma_start(key_slot[:, q, w, :], keys[ds(at, WE), :].rearrange("(p j) b -> p (j b)", p=P))\
                            .then_inc(keys_in[q], 16)

        def dve_counts(dve, i, u, c, first):
            def batch(s):
                b = (u + s) % 2
                if not first or u * NH + s >= 2:
                    dve.wait_ge(hot_used, c * NH + (s - 1))
                nc.vector.tensor_tensor(
                    hot[b][:, HB * P:HB * (P + NT)].rearrange("p (k e) -> p k e", e=NT),
                    dst_tile[:, ds(c * CH + s * HB, HB)].rearrange("p (k o) -> p k o", o=1).to_broadcast([P, HB, NT]),
                    count_bf[:, 0:NT].rearrange("p (o e) -> p o e", o=1).to_broadcast([P, HB, NT]), ALU.is_equal)\
                    .then_inc(hot_ready, 1)
            if first:
                for s in range(NH):
                    batch(s)
                return
            for h in range(2):
                q = 2 * u + h
                t = i * 4 + (q - 4)
                dve.wait_ge(keys_in[q], i * (16 * WT))
                slot = key_slot[:, q, :, :].rearrange("p w (j b) -> p w j b", b=2)
                nc.vector.tensor_tensor(key_rel[:, :, :], slot[:, :, :, 0],
                                        win_base[:, :].rearrange("p (w o) -> p w o", o=1).to_broadcast([P, WT, WJ]),
                                        ALU.subtract).then_inc(rel_made, 1)
                dve.wait_ge(rel_made, t * 2 + 1)
                nc.vector.tensor_scalar(win_base[:, :], win_base[:, :], float(WT * WC), None, ALU.add).then_inc(rel_made, 1)
                for w in range(WT):
                    if batch_at(h, w) is not None:
                        batch(batch_at(h, w))
                    b = w % 4
                    dve.wait_ge(win_used, t * WT + (w + 1))
                    for j in range(WJ):
                        ins = nc.vector.tensor_scalar(place_hot[b][:, j, :], count_bf[:, :], key_slot[:, q, w, 2 * j + 1:2 * j + 2],
                                                      None, ALU.is_equal)
                        if w == WT - 1 and j == WJ - 1:
                            ins.then_inc(keys_used, 1)
                        ins = nc.vector.tensor_scalar(key_hot[b][:, j, :], lane[:, :], key_rel[:, w, j:j + 1], None, ALU.is_equal)
                    ins.then_inc(win_ready, 1)
                dve.wait_ge(win_ready, t * WT + WT)
                dve.wait_ge(rel_made, t * 2 + 2)

        def pe_degrees(pe, c, u, s):
            b = (u + s) % 2
            pe.wait_ge(hot_ready, c * NH + (s + 1))
            pe.wait_ge(sign_ready, c * NH + (s + 1))
            for k in range(HB):
                ins = nc.tensor.matmul(PS[7][:, 0:NT], hot[b][:, k * P:(k + 1) * P],
                                       hot[b][:, HB * P + k * NT:HB * P + (k + 1) * NT], start=False, stop=False)
            ins.then_inc(hot_used, 1)

        def pe_counts(pe, i, u, c):
            for h in range(2):
                t = i * 4 + (2 * u + h - 4)
                for w in range(WT):
                    if batch_at(h, w - 3) is not None:
                        pe_degrees(pe, c, u, batch_at(h, w - 3))
                    b = w % 4
                    pe.wait_ge(win_ready, t * WT + (w + 1))
                    pe.wait_ge(win_taken, t * WT + (w + 1))
                    for j in range(WJ):
                        ins = nc.tensor.matmul(PS[b][:, 0:WC], place_hot[b][:, j, :], key_hot[b][:, j, :],
                                               start=j == 0, stop=j == WJ - 1)
                    ins.then_inc(win_used, 1)

        def act_degrees(act, c, u, s, first):
            b = (u + s) % 2
            if not first or u * NH + s >= 2:
                act.wait_ge(hot_used, c * NH + (s - 1))
            for k in range(HB):
                ins = nc.scalar.activation(hot[b][:, k * P:(k + 1) * P], count_bf[:, :], ACT.Sign,
                                           bias=place_off[:, ds(c * CH + (s * HB + k), 1)])
            ins.then_inc(sign_ready, 1)

        def act_counts(act, i, u, c):
            for h in range(2):
                q = 2 * u + h
                t = i * 4 + (q - 4)
                act.wait_ge(counts_out[h], i * 32 + (16 * (u + 1) - 32))
                for w in range(WT):
                    if batch_at(h, w) is not None:
                        act_degrees(act, c, u, batch_at(h, w), False)
                    act.wait_ge(win_used, t * WT + (w + 5))
                    nc.scalar.copy(
                        tile_counts[h].rearrange("p (s d) -> p d s", d=P)[:, w * WN:(w + 1) * WN, :],
                        PS[w % 4][:, 0:WC].rearrange("p (d s) -> p d s", s=NT)).then_inc(win_taken, 1)
                wait_counts(act, (win_taken, t * WT + (WT + 4)))
                act.dma_start(counts[ds(t, 1), :, :].rearrange("o p n -> (o p) n"), tile_counts[h]).then_inc(counts_out[h], 16)

        own_made, whole_made = sem("own_made"), sem("whole_made")

        def own_part(dve, l):
            if l == 1:
                nc.vector.tensor_tensor(tot[:, :], deg[:, :], inv[:, :], ALU.mult).then_inc(own_made, 1)
                dve.wait_ge(own_made, 1)
                nc.vector.tensor_scalar(tot[:, :], tot[:, :], 2.0, None, ALU.add).then_inc(own_made, 1)
                dve.wait_ge(own_made, 2)
                nc.vector.tensor_tensor(S3, X[:, :, :], over_f(tot), ALU.mult).then_inc(own_made, 1)
            else:
                nc.vector.tensor_tensor(S3, S2, over_f(dinv), ALU.mult).then_inc(own_made, 1)
            dve.wait_ge(own_made, l + 2)

        def collect(l, flag=None):
            banks = [list(range(t, min(t + 8, NT))) for t in range(0, NT, 8)]
            block = nc.Block()
            with block:
                @block.gpsimd
                def _(pool):
                    by_edge = sums[l].rearrange("p k f -> (p k) f")

                    def body():
                        for t in range(NT):
                            nc.gpsimd.indirect_dma_start(S1[:, t, :], None, by_edge, rows(end_row[:, t:t + 1])).then_inc(fetched, 16)
                    only_if(pool, flag, body)

                @block.tensor
                def _(pe):
                    def body():
                        for b, tiles in enumerate(banks):
                            for j, t in enumerate(tiles):
                                ins = nc.tensor.matmul(PS[b][:, j * F:(j + 1) * F], cross[:, t * P:(t + 1) * P],
                                                       R[1][:, CH - 1, :], start=True, stop=True)
                        ins.then_inc(carried, 1)
                    only_if(pe, flag, body)

                @block.vector
                def _(dve):
                    def body():
                        dve.wait_ge(fetched, 16 * NT * (l + 1))
                        nc.vector.tensor_tensor(S1, S1, over_f(has), ALU.mult).then_inc(masked, 1)
                        dve.wait_ge(masked, l + 1)
                        dve.wait_ge(carried, l + 1)
                        for b, tiles in enumerate(banks):
                            part = S1[:, tiles[0]:tiles[-1] + 1, :]
                            ins = nc.vector.tensor_tensor(
                                part, part, PS[b][:, 0:len(tiles) * F].rearrange("p (t f) -> p t f", f=F), ALU.add)
                        if l:
                            ins.then_inc(whole_made, 1)
                            dve.wait_ge(whole_made, 2 * l - 1)
                            own_part(dve, l)
                            nc.vector.tensor_tensor(S1, S1, over_f(inv if l == 1 else dinv), ALU.mult).then_inc(whole_made, 1)
                            dve.wait_ge(whole_made, 2 * l)
                            nc.vector.tensor_tensor(S1, S1, S3, ALU.add)
                    only_if(dve, flag, body)

        masked, parted, product_ps, product_sb = (sem(n) for n in ("masked", "parted", "product_ps", "product_sb"))
        tile_in = [sem(f"tile_in{s}") for s in range(4)]

        def product(l, values):
            turn = l - 1
            before_t = turn * NT
            parts = xt[:, 0:NT * PARTS * F // 2].bitcast(bf16).rearrange("p (t a f) -> p t a f", a=PARTS, f=F)
            rest = node[:, 2 * NT * F:3 * NT * F].rearrange("p (t f) -> p t f", f=F)
            bufs = [b[:, 0:NP // 2].bitcast(bf16) for b in gbuf + rbuf]

            def in_fours(eng, body):
                for s in range(4):
                    body(0, s, s, True)
                with eng.Fori(1, NT // 4) as i:
                    for s in range(4):
                        body(i, s, i * 4 + s, False)
                body(NT // 4, 0, NT - 1, False)

            def unless(eng, body):
                value = eng.value_load(irregular[0:1, 0:1], min_val=0, max_val=1)
                with eng.If(value == 0):
                    body()
                with eng.Else():
                    eng.wait_ge(begun, 1)

            block = nc.Block()
            with block:
                @block.sync
                def _(sp):
                    def tile(i, s, t, first):
                        if not first:
                            wait_counts(sp, (product_ps, t + (before_t - 3)))
                        sp.dma_start(bufs[s], counts[ds(t, 1), :, :].rearrange("o p n -> (o p) n")).then_inc(tile_in[s], 16)
                    unless(sp, lambda: in_fours(sp, tile))

                @block.tensor
                def _(pe):
                    def tile(i, s, t, first):
                        past = turn * (NT // 4 + (s == 0))
                        pe.wait_ge(tile_in[s], i * 16 + 16 * (past + 1))
                        if not first:
                            pe.wait_ge(product_sb, t + (before_t - 3))
                        for k in range(NT):
                            ins = nc.tensor.matmul(PS[s][:, 0:PARTS * F], bufs[s][:, k * P:(k + 1) * P],
                                                   parts[:, k, :, :].rearrange("p a f -> p (a f)"),
                                                   start=k == 0, stop=k == NT - 1)
                        ins.then_inc(product_ps, 1)

                    def body():
                        pe.wait_ge(parted, 5 * (turn + 1))
                        in_fours(pe, tile)
                    unless(pe, body)

                @block.vector
                def _(dve):
                    def tile(i, s, t, first):
                        dve.wait_ge(product_ps, t + (before_t + 1))
                        nc.vector.tensor_reduce(S1[:, ds(t, 1), :].rearrange("p o f -> p (o f)"),
                                                PS[s][:, 0:PARTS * F].rearrange("p (a f) -> p f a", f=F),
                                                AX.X, ALU.add).then_inc(product_sb, 1)
                        dve.wait_ge(product_sb, t + (before_t + 1))
                        nc.vector.scalar_tensor_tensor(out=S1[:, ds(t, 1), :], in0=S1[:, ds(t, 1), :],
                                                       scalar=(inv if l == 1 else dinv)[:, ds(t, 1)], in1=S3[:, ds(t, 1), :],
                                                       op0=ALU.mult, op1=ALU.add)

                    def body():
                        steps = ((parts[:, :, 0, :], values, None), (rest, values, parts[:, :, 0, :]),
                                 (parts[:, :, 1, :], rest, None), (rest, rest, parts[:, :, 1, :]), (parts[:, :, 2, :], rest, None))
                        for n, (to, of, less) in enumerate(steps):
                            if less is None:
                                ins = nc.vector.tensor_copy(to, of)
                            else:
                                ins = nc.vector.tensor_tensor(to, of, less, ALU.subtract)
                            ins.then_inc(parted, 1)
                            dve.wait_ge(parted, 5 * turn + n + 1)
                        own_part(dve, l)
                        in_fours(dve, tile)
                    unless(dve, body)

        def degrees():
            cum_sb, doubled, deg_sb, prefix, root, rooted, over, overs = (
                sem(n) for n in ("cum_sb", "doubled", "deg_sb", "prefix", "root", "rooted", "over", "overs"))
            steps = gbuf[0][:, 0:P]
            block = nc.Block()
            with block:
                @block.tensor
                def _(pe):
                    pe.wait_ge(cum_sb, 2)
                    nc.tensor.matmul(PS[3][:, 0:NT], steps, tot[:, :], start=True, stop=True).then_inc(doubled, 1)
                    pe.wait_ge(deg_sb, 1)
                    nc.tensor.matmul(PS[0][:, 0:NT], upto[:, :], deg[:, :], start=True, stop=True)
                    nc.tensor.matmul(PS[1][:, 0:NT], ones[:, :], deg[:, :], start=True, stop=True).then_inc(prefix, 1)
                    pe.wait_ge(over, 1)
                    nc.tensor.matmul(PS[2][:, 0:1], ones[:, :], mean[:, 0:1], start=True, stop=True).then_inc(overs, 1)

                @block.scalar
                def _(act):
                    act.wait_ge(root, 1)
                    nc.scalar.activation(tmp[:, :], tmp[:, :], ACT.Sqrt).then_inc(rooted, 1)

                @block.vector
                def _(dve):
                    nc.vector.tensor_tensor(steps[:, 1:P], ident[:, 1:P], ident[:, 0:P - 1], ALU.subtract)
                    nc.vector.tensor_tensor(steps[:, 0:1], ident[:, 0:1], ident[:, P - 1:P], ALU.add).then_inc(cum_sb, 1)
                    nc.vector.tensor_scalar(tot[:, :], PS[7][:, 0:NT], 0.5, None, ALU.mult).then_inc(cum_sb, 1)
                    dve.wait_ge(doubled, 1)
                    nc.vector.tensor_copy(deg[:, :], PS[3][:, 0:NT]).then_inc(deg_sb, 1)
                    dve.wait_ge(deg_sb, 1)
                    nc.vector.tensor_scalar(has[:, :], deg[:, :], 1.0, None, ALU.min)
                    ch.link(nc.vector.tensor_scalar(inv[:, :], deg[:, :], 1.0, None, ALU.max))
                    ch.link(nc.vector.reciprocal(inv[:, :], inv[:, :]))
                    nc.vector.tensor_scalar(tmp[:, :], deg[:, :], 1.0, None, ALU.add).then_inc(root, 1)
                    dve.wait_ge(rooted, 1)
                    ch.link(nc.vector.reciprocal(dinv[:, :], tmp[:, :]))
                    ch.link(nc.vector.tensor_reduce(var[:, 0:1], deg[:, :], AX.X, ALU.max))
                    ch.link(nc.vector.tensor_scalar(var[:, 0:1], var[:, 0:1], float(EXACT), None, ALU.is_gt))
                    nc.vector.scalar_tensor_tensor(out=mean[:, 0:1], in0=win_most[:, :], scalar=float(WE), in1=var[:, 0:1],
                                                   op0=ALU.is_gt, op1=ALU.max).then_inc(over, 1)
                    dve.wait_ge(overs, 1)
                    ch.link(nc.vector.tensor_scalar(irregular[:, :], PS[2][:, 0:1], 1.0, None, ALU.min))
                    dve.wait_ge(prefix, 1)
                    ch.link(nc.vector.tensor_copy(tot[:, :], PS[1][:, 0:NT]))
                    ch.link(nc.vector.tensor_tensor_scan(tmp[:, :], ones[:, 0:NT], tot[:, :], 0.0, ALU.mult, ALU.add))
                    ch.link(nc.vector.tensor_tensor(tmp[:, :], tmp[:, :], tot[:, :], ALU.subtract))
                    ch.link(nc.vector.tensor_tensor(tmp[:, :], tmp[:, :], PS[0][:, 0:NT], ALU.add))
                    nc.vector.tensor_scalar(end_row[:, :], tmp[:, :], -1.0, 0.0, ALU.add, ALU.max)
                    ch.link(nc.vector.tensor_tensor(tmp[:, :], tmp[:, :], deg[:, :], ALU.subtract))
                    ch.link(nc.vector.tensor_tensor(tot[:, :], dump[:, 1:1 + NT], tmp[:, :], ALU.subtract))
                    ch.link(nc.vector.tensor_scalar(mean[:, :], has[:, :], -1.0, 1.0, ALU.mult, ALU.add))
                    ch.link(nc.vector.tensor_tensor(tot[:, :], tot[:, :], mean[:, :], ALU.mult))
                    nc.vector.tensor_tensor(start_row[:, :], tmp[:, :], tot[:, :], ALU.add)
                    dve.wait_ge(counted, 1)
                    nc.vector.tensor_scalar(cross[:, :], cross[:, :], last_dst[:, 0:1], goes_out[:, 0:1],
                                            ALU.is_equal, ALU.mult)

        def centre(Y, scratch, first=0, last=NT):
            n = [P, last - first, F]
            over = mean[:, first:last].rearrange("p (t o) -> p t o", o=1).to_broadcast(n)
            ch.link(nc.vector.tensor_reduce(mean[:, first:last], Y, AX.X, ALU.add))
            ch.link(nc.vector.tensor_scalar(mean[:, first:last], mean[:, first:last], 1.0 / F, None, ALU.mult))
            ch.link(nc.vector.tensor_tensor(Y, Y, over, ALU.subtract))
            ch.link(nc.vector.tensor_tensor(scratch, Y, Y, ALU.mult))
            ch.link(nc.vector.tensor_reduce(var[:, first:last], scratch, AX.X, ALU.add))

        def scale(dve, Y, n, to):
            nc.vector.tensor_scalar(var[:, :], var[:, :], 1.0 / F, EPS, ALU.mult, ALU.add).then_inc(var_made, 1)
            dve.wait_ge(root_made, n)
            ch.link(nc.vector.reciprocal(var[:, :], var[:, :]))
            ch.link(nc.vector.tensor_tensor(to, Y, over_f(var), ALU.mult))

        def layer_norm(dve, Y, scratch, n, to=None):
            centre(Y, scratch)
            scale(dve, Y, n, Y if to is None else to)

        def node_stage(l):
            turn = l - 2
            done = max(turn, 0) * len(TILE_GROUPS)
            norm = min(l, 2) + 1
            banks = [list(range(t, min(t + 8, NT))) for t in range(0, NT, 8)]
            block = nc.Block()

            def bank3(b, n):
                return PS[b][:, 0:n * F].rearrange("p (t f) -> p t f", f=F)

            with block:
                @block.tensor
                def _(pe):
                    if l >= 2:
                        for g, tiles in enumerate(TILE_GROUPS):
                            if g >= 2:
                                pe.wait_ge(nd_tr_sb, done + g - 1)
                            for j, t in enumerate(tiles):
                                ins = nc.tensor.transpose(PS[6 + g % 2][0:F, j * P:(j + 1) * P], S1[:, t, :], ident[:, :])
                            ins.then_inc(nd_tr_ps, 1)
                        pe.wait_ge(nd_tr_sb, done + len(TILE_GROUPS))
                        for b, tiles in enumerate(banks):
                            for j, t in enumerate(tiles):
                                ins = nc.tensor.matmul(PS[b][:, j * F:(j + 1) * F], xt[0:F, t * P:(t + 1) * P],
                                                       gcn_s[:, l - 2, :], start=True, stop=True)
                        ins.then_inc(mixed, 1)
                    else:
                        pe.wait_ge(begun, 1)

                @block.scalar
                def _(act):
                    if l >= 2:
                        act_untranspose(act, PS[6:8], nd_tr_ps, nd_tr_sb, done)
                    if l != 2:
                        act.wait_ge(var_made, norm)
                        nc.scalar.activation(var[:, :], var[:, :], ACT.Sqrt).then_inc(root_made, 1)

                @block.vector
                def _(dve):
                    if l == 0:
                        ch.link(nc.vector.tensor_tensor(X[:, :, :], X[:, :, :], S1, ALU.add))
                    elif l >= 2:
                        dve.wait_ge(mixed, turn + 1)
                        for b, tiles in enumerate(banks):
                            bias = bias_s[:, l - 2:l - 1, :].to_broadcast([P, len(tiles), F])
                            ins = nc.vector.tensor_tensor(S3[:, tiles[0]:tiles[-1] + 1, :], bank3(b, len(tiles)), bias, ALU.add)
                        ch.link(ins)
                        ch.link(nc.vector.tensor_scalar(S3, S3, 0.0, None, ALU.max))
                        if l == 3:
                            ch.link(nc.vector.tensor_tensor(X[:, :, :], X[:, :, :], S3, ALU.add))
                    if l == 1:
                        layer_norm(dve, S1, S3, norm, X[:, :, :])
                    elif l != 2:
                        layer_norm(dve, X[:, :, :], S1, norm)
                    if l in (1, 2):
                        ch.link(nc.vector.tensor_tensor(S2, X[:, :, :] if l == 1 else S3, over_f(dinv), ALU.mult))
                    nc.vector.tensor_copy(tot[:, 0:1], mean[:, 0:1]).then_inc(ready, 1)

                if l < 3:
                    @block.sync
                    def _(sp):
                        def body():
                            sp.wait_ge(ready, l + 1)
                            sp.dma_start(node_table[l].rearrange("(t p) f -> p t f", p=P), X[:, :, :] if l == 0 else S2)\
                                .then_inc(tabled, 16)
                            sp.wait_ge(tabled, 16 * (l + 1))
                        only_if(sp, irregular, body)

        OWN_HALVES = [list(range(0, CH // 8)), list(range(CH // 8, len(TILE_GROUPS)))]

        def own(g):
            half = g // (CH // 8)
            at = (g - half * (CH // 8)) * GR * P
            return gbuf[half][:, at:at + len(TILE_GROUPS[g]) * P]

        def edge_tables():
            tr_ps, tr_sb, mm, got_p, got_q, stored, put, first, own_ps, own_sb, own_stored = (
                sem(f"et_{n}") for n in ("tr_ps", "tr_sb", "mm", "p", "q", "stored", "put", "first", "own_ps", "own_sb",
                                         "own_stored"))
            Pn = node[:, 0:NT * H].rearrange("p (t h) -> p t h", h=H)
            Qn = cross[:, :].rearrange("p (t h) -> p t h", h=H)
            block = nc.Block()
            with block:
                @block.tensor
                def _(pe):
                    pe_transpose(pe, X, PS[0:2], tr_ps, tr_sb)
                    for g, tiles in enumerate(TILE_GROUPS):
                        pe.wait_ge(tr_sb, g + 1)
                        if g >= 2:
                            pe.wait_ge(got_p, g - 1)
                            pe.wait_ge(got_q, g - 1)
                        for a in range(2):
                            for j, t in enumerate(tiles):
                                ins = nc.tensor.matmul(PS[2 + 2 * a + g % 2][:, j * H:(j + 1) * H], xt[0:F, t * P:(t + 1) * P],
                                                       ew1_s[:, a * H:(a + 1) * H], start=True, stop=True)
                        ins.then_inc(mm, 1)
                    for g, tiles in enumerate(TILE_GROUPS):
                        if g >= 2:
                            pe.wait_ge(own_sb, g - 1)
                        n = len(tiles) * P
                        nc.tensor.matmul(PS[6 + g % 2][:, 0:n], nw1x_s[:, :], xt[0:F, g * GR * P:g * GR * P + n],
                                         start=True, stop=True).then_inc(own_ps, 1)

                def bank(a, g, tiles):
                    return PS[2 + 2 * a + g % 2][:, 0:len(tiles) * H].rearrange("p (t h) -> p t h", h=H)

                @block.scalar
                def _(act):
                    act_untranspose(act, PS[0:2], tr_ps, tr_sb)
                    for g, tiles in enumerate(TILE_GROUPS):
                        act.wait_ge(mm, g + 1)
                        nc.scalar.copy(Qn[:, tiles[0]:tiles[-1] + 1, :], bank(1, g, tiles)).then_inc(got_q, 1)
                    for g, tiles in enumerate(TILE_GROUPS):
                        act.wait_ge(own_ps, g + 1)
                        nc.scalar.copy(own(g), PS[6 + g % 2][:, 0:len(tiles) * P]).then_inc(own_sb, 1)

                @block.vector
                def _(dve):
                    for g, tiles in enumerate(TILE_GROUPS):
                        dve.wait_ge(mm, g + 1)
                        nc.vector.tensor_copy(Pn[:, tiles[0]:tiles[-1] + 1, :], bank(0, g, tiles)).then_inc(got_p, 1)
                    dve.wait_ge(tr_ps, len(TILE_GROUPS))
                    nc.vector.scalar_tensor_tensor(out=X[:, :, :], in0=X[:, :, :], scalar=2.0,
                                                   in1=bias_s[:, 2:3, :].to_broadcast([P, NT, F]), op0=ALU.mult, op1=ALU.add)
                    nc.vector.tensor_copy(same[:, 0:1], comes_in[:, :])

                @block.sync
                def _(sp):
                    sp.wait_ge(got_p, len(TILE_GROUPS))
                    sp.wait_ge(got_q, len(TILE_GROUPS))
                    sp.dma_start(p_table.rearrange("(t p) h -> p t h", p=P), Pn).then_inc(stored, 16)
                    sp.dma_start(q_table.rearrange("(t p) h -> p t h", p=P), Qn).then_inc(stored, 16)
                    sp.wait_ge(own_sb, len(TILE_GROUPS))
                    for half in OWN_HALVES:
                        low, high = half[0] * GR * P, min((half[-1] + 1) * GR * P, NP)
                        sp.dma_start(x_hidden[:, low:high], gbuf[half[0] > 0][:, 0:high - low]).then_inc(own_stored, 16)
                    sp.wait_ge(stored, 32)
                    sp.wait_ge(own_stored, 32)

                @block.gpsimd
                def _(pool):
                    pool.wait_ge(got_q, len(TILE_GROUPS))
                    for t in range(NT):
                        nc.gpsimd.indirect_dma_start(q_starts, rows(start_row[:, t:t + 1]), Qn[:, t, :], None).then_inc(put, 16)
                    pool.wait_ge(stored, 32)
                    nc.gpsimd.indirect_dma_start(q_in[:, :], None, q_table, rows(first_dst[:, 0:1])).then_inc(first, 16)
                    pool.wait_ge(put, 16 * NT)
                    pool.wait_ge(first, 16)

        def edge_mlp():
            got, attr_in, rows_in, q_landed, idx_ready = (
                [sem(f"{n}{u}") for u in range(2)] for n in ("e_got", "e_attr", "e_rows", "e_q", "e_idx"))
            q_done, added, z1_ps, eq_ps, h1_sb, eq_sb, z2_ps, z2_sb, m_sb, s_ps, s_sb = (
                sem(f"e_{n}") for n in ("q_done", "added", "z1_ps", "eq_ps", "h1_sb", "eq_sb", "z2_ps", "z2_sb", "m_sb",
                                        "s_ps", "s_sb"))
            put = [sem(f"e_put{j}") for j in range(GR)]
            placed, e_chain = sem("e_placed"), sem("e_chain")
            LINKS, LAG, Q_FROM = 4, 4, 2
            prior, n_prior, gap = xt[:, 4096:4608], xt[:, 4608:4608 + GR], xt[:, 4616:4616 + GR]
            attr_s = [cross[0:1 + A, 0:CE * P], node[0:1 + A, 0:CE * P]]
            src_rows = [node[0:2, CE * P + u * CE * P // 2:CE * P + (u + 1) * CE * P // 2].bitcast(bf16) for u in range(2)]
            h1, z2b, msg, equal = ([xt[:, 1024 * a + 512 * b:1024 * a + 512 * (b + 1)] for b in range(2)] for a in range(4))
            total = [node[:, 2 * CE * P + 512 * b:2 * CE * P + 512 * (b + 1)] for b in range(4)]
            q_rows = q_starts[0:EP, :].rearrange("(p k) h -> p k h", p=P)

            def slot(u, c, first, s, steps):
                for d, f in steps:
                    least = (0 if first else 2 * NG) + u * NG + s - d
                    if s >= d:
                        f(c, u, s - d, least % 2, least)
                    elif least >= 0:
                        f(c - 1, 1 - u, s - d + NG, least % 2, least)

            def slots(eng, head, *steps):
                def chunk(i, u, c, first):
                    head(i, u, c)
                    for s in range(NG):
                        slot(u, c, first, s, steps)
                by_pairs(eng, NCE, chunk)
                rest(steps)

            def rest(steps):
                for s in range(NG, NG + max(d for d, _ in steps)):
                    slot(1, NCE - 1, False, s, [(d, f) for d, f in steps if s - d < NG])

            block = nc.Block()
            with block:
                @block.sync
                def _(sp):
                    def chunk(i, u, c, first):
                        if not first:
                            wait_counts(sp, (added, (c - 1) * NG), (q_done, c))
                        sp.dma_start(QE[u], q_rows[:, ds(c * CE, CE), :]).then_inc(q_landed[u], 16)
                        if not first:
                            wait_counts(sp, (z1_ps, (c - 1) * NG), (eq_ps, (c - 1) * NG))
                        sp.dma_start(attr_s[u], edge_attr[:, ds(c * (CE * P), CE * P)]).then_inc(attr_in[u], 16)
                        sp.dma_start(src_rows[u], src_split[:, ds(c * (CE * P), CE * P)]).then_inc(rows_in[u], 16)
                    sp.wait_ge(attr_there, 16)
                    by_pairs(sp, NCE, chunk)

                @block.gpsimd
                def _(pool):
                    def fetch(i, u, c, first, g):
                        if g == 0:
                            if not first:
                                pool.wait_ge(got[u], i * (16 * CE))
                            nc.gpsimd.tensor_copy(get_rows[:, u, 0:CE], src_i[:, ds(c * CE, CE)]).then_inc(idx_ready[u], 1)
                            wait_counts(pool, (idx_ready[u], i + 1))
                        if not first:
                            wait_counts(pool, (z1_ps, (c - 2) * NG + (g + 1)))
                        for k in range(g * GR, (g + 1) * GR):
                            nc.gpsimd.indirect_dma_start(GE[u][:, k, :], None, p_table, rows(get_rows[:, u, k:k + 1]))\
                                .then_inc(got[u], 16)

                    def add_up(u, c, g, first):
                        wait_counts(pool, (s_sb, c * NG + (g + 1)), (placed, c * NG + (g + 1)))
                        for j in range(GR):
                            if not first:
                                wait_counts(pool, (put[j], c * (16 * NG) + 16 * g))
                            nc.gpsimd.indirect_dma_start(
                                agg_table[j], rows(put_rows[:, u, g * GR + j:g * GR + j + 1]),
                                total[g % 4][:, j * H:(j + 1) * H], None, compute_op=ALU.add).then_inc(put[j], 16)

                    def turn(i, u, c, first):
                        for g in range(NG):
                            fetch(i, u, c, first, g)
                            if g >= LAG and not (first and u == 0):
                                add_up(1 - u, c - 1, g - LAG, first and g == LAG)
                            elif g < LAG and not first:
                                add_up(u, c - 2, g + NG - LAG, False)
                    by_pairs(pool, NCE, turn)
                    for n in range((NCE - 1) * NG - LAG, NCE * NG):
                        add_up(n // NG % 2, n // NG, n % NG, False)
                    for j in range(GR):
                        pool.wait_ge(put[j], 16 * NG * NCE)

                @block.vector
                def _(dve):
                    def extend(u, c, low, high, start):
                        for h in range(low, high):
                            ins = nc.vector.tensor_tensor_scan(QE[u][:, :, h], same[:, ds(c * CE, CE)], QE[u][:, :, h],
                                                               start[:, h:h + 1], ALU.mult, ALU.add)
                        if high == H:
                            ins.then_inc(q_done, 1)

                    def add(c, u, g, b, least):
                        part = GE[u][:, g * GR:(g + 1) * GR, :]
                        nc.vector.tensor_tensor(part, part, QE[u][:, g * GR:(g + 1) * GR, :], ALU.add).then_inc(added, 1)

                    def compare(c, u, g, b, least):
                        dve.wait_ge(eq_ps, c * NG + (g + 1))
                        if least >= 2:
                            dve.wait_ge(s_ps, c * NG + (g - 1))
                        nc.vector.tensor_tensor(
                            equal[b].rearrange("p (j e) -> p j e", e=P), PS[2 + b][:, :].rearrange("p (j e) -> p j e", e=P),
                            src_i[:, ds(c * CE + g * GR, GR)].rearrange("p (j o) -> p j o", o=1).to_broadcast([P, GR, P]),
                            ALU.is_equal).then_inc(eq_sb, 1)

                    def place(c, u, g, b, least):
                        n = c * NG + g
                        here = src_i[:, ds(c * CE + g * GR, GR)]
                        dve.wait_ge(eq_sb, n + 1)
                        nc.vector.tensor_tensor(
                            prior.rearrange("p (j e) -> p j e", e=P), equal[b].rearrange("p (j e) -> p j e", e=P),
                            before[:, :].rearrange("p (o e) -> p o e", o=1).to_broadcast([P, GR, P]),
                            ALU.mult).then_inc(e_chain, 1)
                        if least:
                            dve.wait_ge(placed, n)
                        nc.vector.tensor_scalar(gap, here, -1.0, dump[:, 0:1], ALU.mult, ALU.add).then_inc(e_chain, 1)
                        dve.wait_ge(e_chain, n * LINKS + 2)
                        nc.vector.tensor_reduce(n_prior, prior.rearrange("p (j e) -> p j e", e=P), AX.X, ALU.add)\
                            .then_inc(e_chain, 1)
                        dve.wait_ge(e_chain, n * LINKS + 3)
                        nc.vector.scalar_tensor_tensor(out=gap, in0=n_prior, scalar=0.0, in1=gap, op0=ALU.is_gt,
                                                       op1=ALU.mult).then_inc(e_chain, 1)
                        dve.wait_ge(e_chain, n * LINKS + 4)
                        if g == 0 and least >= 2 * NG:
                            for j in range(GR):
                                dve.wait_ge(put[j], (c - 1) * (16 * NG))
                        nc.vector.tensor_tensor(put_rows[:, u, g * GR:(g + 1) * GR], gap, here, ALU.add).then_inc(placed, 1)

                    def bias(c, u, g, b, least):
                        dve.wait_ge(z2_ps, c * NG + (g + 1))
                        if least >= 2:
                            dve.wait_ge(m_sb, c * NG + (g - 1))
                        nc.vector.tensor_tensor(
                            z2b[b].rearrange("p (j h) -> p j h", h=H), PS[4 + b][:, :].rearrange("p (j h) -> p j h", h=H),
                            eb2_s[:, :].rearrange("p (o h) -> p o h", o=1).to_broadcast([P, GR, H]), ALU.add)\
                            .then_inc(z2_sb, 1)

                    steps = (0, add), (2, bias), (2, compare), (2, place)

                    def chunk(i, u, c, first, last=False):
                        dve.wait_ge(q_done, c + 1)
                        dve.wait_ge(got[u], (i + 1) * (16 * CE))
                        for s in range(NG):
                            slot(u, c, first, s, steps)
                            if s >= Q_FROM and not last:
                                if s == Q_FROM:
                                    dve.wait_ge(q_landed[1 - u], (i + 1 + u) * 16)
                                low, high = ((s - Q_FROM + k) * H // (NG - Q_FROM) for k in range(2))
                                extend(1 - u, c + 1, low, high, QE[u][:, CE - 1, :])

                    dve.wait_ge(q_landed[0], 16)
                    extend(0, 0, 0, H, q_in)
                    for u in range(2):
                        chunk(0, u, u, True)
                    with dve.Fori(1, NCE // 2 - 1) as i:
                        for u in range(2):
                            chunk(i, u, i * 2 + u, False)
                    for u in range(2):
                        chunk(NCE // 2 - 1, u, NCE - 2 + u, False, last=u == 1)
                    rest(steps)

                @block.tensor
                def _(pe):
                    def head(i, u, c):
                        pe.wait_ge(attr_in[u], (i + 1) * 16)

                    def layer1(c, u, g, b, least):
                        if least >= 2:
                            pe.wait_ge(h1_sb, c * NG + (g - 1))
                        nc.tensor.matmul(PS[b][:, :], we_s[:, :], attr_s[u][:, g * GR * P:(g + 1) * GR * P],
                                         start=True, stop=False)
                        pe.wait_ge(added, c * NG + (g + 1))
                        for j in range(GR):
                            ins = nc.tensor.matmul(PS[b][:, j * P:(j + 1) * P], GE[u][:, g * GR + j, :], ident[:, :],
                                                   start=False, stop=j == GR - 1)
                        ins.then_inc(z1_ps, 1)

                    def sources(c, u, g, b, least):
                        if g == 0:
                            pe.wait_ge(rows_in[u], (c - u) * 8 + 16)
                        if least >= 2:
                            pe.wait_ge(eq_sb, c * NG + (g - 1))
                        nc.tensor.matmul(PS[2 + b][:, :], ones_bf[:, :], src_rows[u][:, g * GR * P:(g + 1) * GR * P],
                                         start=True, stop=True).then_inc(eq_ps, 1)

                    def layer2(c, u, g, b, least):
                        pe.wait_ge(h1_sb, c * NG + (g + 1))
                        if least >= 2:
                            pe.wait_ge(z2_sb, c * NG + (g - 1))
                        for j in range(GR):
                            ins = nc.tensor.matmul(PS[4 + b][:, j * H:(j + 1) * H], h1[b][:, j * P:(j + 1) * P], ew2_s[:, :],
                                                   start=True, stop=True)
                        ins.then_inc(z2_ps, 1)

                    def combine(c, u, g, b, least):
                        pe.wait_ge(m_sb, c * NG + (g + 1))
                        pe.wait_ge(eq_sb, c * NG + (g + 1))
                        if least >= 2:
                            pe.wait_ge(s_sb, c * NG + (g - 1))
                        for j in range(GR):
                            ins = nc.tensor.matmul(PS[6 + b][:, j * H:(j + 1) * H], equal[b][:, j * P:(j + 1) * P],
                                                   msg[b][:, j * H:(j + 1) * H], start=True, stop=True)
                        ins.then_inc(s_ps, 1)
                    slots(pe, head, (0, layer1), (1, layer2), (1, sources), (3, combine))

                @block.scalar
                def _(act):
                    def silu1(c, u, g, b, least):
                        act.wait_ge(z1_ps, c * NG + (g + 1))
                        if least >= 2:
                            act.wait_ge(z2_ps, c * NG + (g - 1))
                        nc.scalar.activation(h1[b], PS[b][:, :], ACT.Silu, bias=hid_s[:, 0:1]).then_inc(h1_sb, 1)

                    def silu2(c, u, g, b, least):
                        act.wait_ge(z2_sb, c * NG + (g + 1))
                        if least >= 2:
                            act.wait_ge(s_ps, c * NG + (g - 1))
                        nc.scalar.activation(msg[b], z2b[b], ACT.Silu).then_inc(m_sb, 1)

                    def take(c, u, g, b, least):
                        act.wait_ge(s_ps, c * NG + (g + 1))
                        if least >= 3:
                            for j in range(GR):
                                act.wait_ge(put[j], c * (16 * NG) + 16 * (g - 2))
                        nc.scalar.copy(total[g % 4], PS[6 + b][:, :]).then_inc(s_sb, 1)
                    slots(act, lambda i, u, c: None, (0, silu1), (2, silu2), (3, take))

        def finish():
            summed, a_ps, a_sb, h_ps, z_sb, h_sb, u_ps, u_sb, own_in, normed, written = (
                sem(f"f_{n}") for n in ("summed", "a_ps", "a_sb", "h_ps", "z_sb", "h_sb", "u_ps", "u_sb", "own_in",
                                        "normed", "written"))
            NPC = 4
            each = len(TILE_GROUPS) // NPC
            pieces = [list(range(k * each, (k + 1) * each if k < NPC - 1 else len(TILE_GROUPS))) for k in range(NPC)]
            table_in = [sem(f"f_table_in{k}") for k in range(NPC)]

            def cols(k):
                return pieces[k][0] * GR * H, min((pieces[k][-1] + 1) * GR * H, NP)

            def part(j, k):
                low, high = cols(k)
                if j < 3:
                    return (cross, node, xt)[j][:, low:high]
                low2 = low - cols(k // 2 * 2)[0]
                return rbuf[k // 2][:, low2:low2 + high - low]

            aT, zT, hT = ([node[:, NP + 1024 * a + 512 * b:NP + 1024 * a + 512 * (b + 1)] for b in range(2)] for a in range(3))
            NGR = len(TILE_GROUPS)
            block = nc.Block()
            with block:
                @block.sync
                def _(sp):
                    for k in range(NPC):
                        low, high = cols(k)
                        for j in range(GR):
                            sp.dma_start(part(j, k).rearrange("p (t h) -> p t h", h=H),
                                         agg_table[j][low:high, :].rearrange("(t p) h -> p t h", p=P)).then_inc(table_in[k], 16)
                    sp.wait_ge(normed, 1)
                    whole = N // P
                    sp.dma_start(out[0:whole * P, :].rearrange("(t p) f -> p t f", p=P), X[:, 0:whole, :]).then_inc(written, 16)
                    sp.dma_start(out[whole * P:N, :], X[0:N - whole * P, whole, :]).then_inc(written, 16)
                    sp.wait_ge(written, 32)

                @block.tensor
                def _(pe):
                    for s in range(NGR + 3):
                        if s < NGR:
                            for k in range(NPC):
                                if s == pieces[k][0]:
                                    pe.wait_ge(summed, (GR - 1) * (k + 1))
                            if s >= 2:
                                pe.wait_ge(a_sb, s - 1)
                            for j, t in enumerate(TILE_GROUPS[s]):
                                ins = nc.tensor.transpose(PS[s % 2][:, j * P:(j + 1) * P], cross[:, t * P:(t + 1) * P], ident[:, :])
                            ins.then_inc(a_ps, 1)
                        if 0 <= s - 1 < NGR:
                            g = s - 1
                            n = len(TILE_GROUPS[g]) * P
                            pe.wait_ge(a_sb, g + 1)
                            if g >= 2:
                                pe.wait_ge(z_sb, g - 1)
                            nc.tensor.matmul(PS[2 + g % 2][:, 0:n], nw1a_s[:, :], aT[g % 2][:, 0:n], start=True, stop=True)\
                                .then_inc(h_ps, 1)
                        if 0 <= s - 3 < NGR:
                            g = s - 3
                            pe.wait_ge(h_sb, g + 1)
                            if g >= 2:
                                pe.wait_ge(u_sb, g - 1)
                            for j in range(len(TILE_GROUPS[g])):
                                ins = nc.tensor.matmul(PS[4 + g % 2][:, j * F:(j + 1) * F], hT[g % 2][:, j * P:(j + 1) * P],
                                                       nw2_s[:, :], start=True, stop=True)
                            ins.then_inc(u_ps, 1)

                @block.scalar
                def _(act):
                    for half in OWN_HALVES:
                        low, high = half[0] * GR * P, min((half[-1] + 1) * GR * P, NP)
                        act.dma_start(gbuf[half[0] > 0][:, 0:high - low], x_hidden[:, low:high]).then_inc(own_in, 16)
                    for s in range(NGR + 2):
                        if s < NGR:
                            n = len(TILE_GROUPS[s]) * P
                            act.wait_ge(a_ps, s + 1)
                            if s >= 2:
                                act.wait_ge(h_ps, s - 1)
                            nc.scalar.copy(aT[s % 2][:, 0:n], PS[s % 2][:, 0:n]).then_inc(a_sb, 1)
                        if 0 <= s - 2 < NGR:
                            g = s - 2
                            n = len(TILE_GROUPS[g]) * P
                            act.wait_ge(z_sb, g + 1)
                            if g >= 2:
                                act.wait_ge(u_ps, g - 1)
                            nc.scalar.activation(hT[g % 2][:, 0:n], zT[g % 2][:, 0:n], ACT.Silu, bias=hid_s[:, 1:2]).then_inc(h_sb, 1)
                    act.wait_ge(var_made, 4)
                    nc.scalar.activation(var[:, :], var[:, :], ACT.Sqrt).then_inc(root_made, 1)

                @block.vector
                def _(dve):
                    dve.wait_ge(own_in, 32)
                    for s in range(NGR + 4):
                        for k in range(NPC):
                            if s == pieces[k][0]:
                                dve.wait_ge(table_in[k], 16 * GR)
                                for j in range(1, GR):
                                    nc.vector.tensor_tensor(part(0, k), part(0, k), part(j, k), ALU.add).then_inc(summed, 1)
                                    dve.wait_ge(summed, k * (GR - 1) + j)
                        if 0 <= s - 2 < NGR:
                            g = s - 2
                            n = len(TILE_GROUPS[g]) * P
                            dve.wait_ge(h_ps, g + 1)
                            if g >= 2:
                                dve.wait_ge(h_sb, g - 1)
                            nc.vector.tensor_tensor(zT[g % 2][:, 0:n], PS[2 + g % 2][:, 0:n], own(g), ALU.add).then_inc(z_sb, 1)
                        if 0 <= s - 4 < NGR:
                            g = s - 4
                            tiles = TILE_GROUPS[g]
                            rows3 = X[:, tiles[0]:tiles[-1] + 1, :]
                            dve.wait_ge(u_ps, g + 1)
                            nc.vector.tensor_tensor(rows3, PS[4 + g % 2][:, 0:len(tiles) * F].rearrange("p (t f) -> p t f", f=F),
                                                    rows3, ALU.add).then_inc(u_sb, 1)
                            for piece in pieces:
                                if g == piece[-1]:
                                    dve.wait_ge(u_sb, g + 1)
                                    first, last = piece[0] * GR, tiles[-1] + 1
                                    centre(X[:, first:last, :], S1[:, first:last, :], first, last)
                    scale(dve, X[:, :, :], 4, X[:, :, :])
                    nc.vector.tensor_copy(tot[:, 0:1], mean[:, 0:1]).then_inc(normed, 1)

        check_order()
        order_edges()
        edge_lists()
        gather_pass(0, rel_table, row_idx)
        degrees()
        collect(0)
        node_stage(0)
        for l in (1, 2, 3):
            gather_pass(l, node_table[l - 1], src_i, irregular)
            collect(l, irregular)
            product(l, X[:, :, :] if l == 1 else S2)
            node_stage(l)
        edge_tables()
        edge_mlp()
        finish()


def kernel(**inputs):
    import numpy as np
    import concourse.bacc as bacc
    from concourse.bass_utils import run_bass_kernel_spmd

    a = {k: np.asarray(v) for k, v in inputs.items()}

    def edges(v, fill):
        full = np.full((EP,) + v.shape[1:], fill, v.dtype)
        full[:E] = v
        return full.reshape((P, KT) + v.shape[1:])

    src, dst = edges(a["src"], NP - 1), edges(a["dst"], N)
    dst.reshape(-1)[E:] = N + np.arange(EP - E) * (NP - N) // (EP - E)
    ew1 = a["L3_gnn_ew1"]
    bias_rows = np.stack([a["L2_gnn_b1"], a["L2_gnn_b2"], a["L3_gnn_nb2"]])
    weighted = np.concatenate([a["edge_weight"][:, None], a["edge_attr_16"]], 1)
    arrays = {
        "x": np.concatenate([a["x"], np.zeros((NP - N, F), a["x"].dtype)]),
        "src": src,
        "dst": dst,
        "etype": edges(a["edge_type_16"], 0),
        "src_t": src.T.reshape(P, KT),
        "dst_t": dst.T.reshape(1, EP),
        "attr_t": edges(weighted, 0).transpose(2, 1, 0).reshape(1 + A, EP),
        "attr_rows": edges(weighted, 0),
        "rel_w": a["L0_gnn_W"].transpose(2, 0, 1).reshape(F, RELS * F),
        "gcn_w": np.stack([a["L2_gnn_W1"], a["L2_gnn_W2"]], 1),
        "bias_rows": np.broadcast_to(bias_rows, (P, 3, F)),
        "ew1": np.concatenate([ew1[:F], ew1[F:2 * F]], 1),
        "we": np.concatenate([ew1[2 * F + A:], ew1[2 * F:2 * F + A]]),
        "ew2": a["L3_gnn_ew2"],
        "hid_b": np.stack([a["L3_gnn_eb1"], a["L3_gnn_nb1"]], 1),
        "eb2_rows": np.broadcast_to(a["L3_gnn_eb2"], (P, H)),
        "nw1x": a["L3_gnn_nw1"][:F],
        "nw1a": a["L3_gnn_nw1"][F:],
        "nw2": a["L3_gnn_nw2"],
    }
    arrays = {k: np.ascontiguousarray(v) for k, v in arrays.items()}
    nc = bacc.Bacc("TRN2", target_bir_lowering=False, num_devices=1)
    args = {k: nc.dram_tensor(f"in_{k}", v.shape, mybir.dt.from_np(v.dtype), kind="ExternalInput").ap() for k, v in arrays.items()}
    out = nc.dram_tensor("out", (N, F), mybir.dt.float32, kind="ExternalOutput").ap()
    gnn_kernel(nc, out=out, **args)
    r = run_bass_kernel_spmd(nc, [{f"in_{k}": v for k, v in arrays.items()}], core_ids=[0])
    return r.results[0]["out"]
```
